# Optimizing a Trainium2 kernel written in Bass

```python
import numpy as np
import jax
import jax.numpy as jnp

def _softmax(x, axis=-1):
    return jax.nn.softmax(x, axis=axis)

def _gelu(x):
    return jax.nn.gelu(x, approximate=True)

def _silu(x):
    return jax.nn.silu(x)

def _sigmoid(x):
    return jax.nn.sigmoid(x)

def _layernorm(x, axis=-1, eps=1e-05):
    m = jnp.mean(x, axis=axis, keepdims=True)
    v = jnp.var(x, axis=axis, keepdims=True)
    return (x - m) / jnp.sqrt(v + eps)

def _scatter_add(tgt, idx, src, axis=0):
    return tgt.at[idx].add(src)

def _segment_sum(src, seg, n):
    return jax.ops.segment_sum(src, seg, n)
kernel_name = 'mk_recurrent_d2_jaxref_r8_35014e'

def setup_inputs(seed: int=0):
    np.random.seed(seed)
    _w = jnp.asarray

    def _L0_attn_setup():
        import jax, jax.numpy as jnp
        import numpy as np
        THETA = 10000.0
        EPS = 1e-06
        N_HEADS = 16

        def apply_rope(x):
            b, h, l, d = x.shape
            inv_freq = 1.0 / THETA ** (jnp.arange(0, d, 2, dtype=jnp.float32) / d)
            t = jnp.arange(l, dtype=jnp.float32)
            freqs = t[:, None] * inv_freq[None, :]
            cos = jnp.cos(freqs)[None, None]
            sin = jnp.sin(freqs)[None, None]
            x1 = x[..., 0::2]
            x2 = x[..., 1::2]
            out = jnp.stack([x1 * cos - x2 * sin, x1 * sin + x2 * cos], axis=-1)
            return out.reshape(b, h, l, d)
        key = jax.random.key(seed)
        ks = jax.random.split(key, 5)
        dim = 128
        b, l = (1, 256)
        scale = 1.0 / np.sqrt(dim)
        return {'x': jax.random.normal(ks[0], (b, l, dim), dtype=jnp.float32), 'wq': jax.random.normal(ks[1], (dim, dim), dtype=jnp.float32) * scale, 'wk': jax.random.normal(ks[2], (dim, dim), dtype=jnp.float32) * scale, 'wv': jax.random.normal(ks[3], (dim, dim), dtype=jnp.float32) * scale, 'wo': jax.random.normal(ks[4], (dim, dim), dtype=jnp.float32) * scale}
    _L0_attn_in = _L0_attn_setup()

    def _L0_ffn_setup():
        import jax, jax.numpy as jnp
        import numpy as np
        E = 8
        TOPK = 2

        def _moe_forward(x, Wg, W1, W2, W3):
            B, S, D = x.shape
            xt = x.reshape(-1, D)
            T = xt.shape[0]
            logits = xt @ Wg.T
            scores = jax.nn.softmax(logits, axis=-1)
            w, idx = jax.lax.top_k(scores, TOPK)
            w = w / (w.sum(axis=-1, keepdims=True) + 1e-20)
            cw = jnp.zeros((T, E), xt.dtype).at[jnp.arange(T)[:, None], idx].add(w)
            h = jax.nn.silu(jnp.einsum('td,ehd->teh', xt, W1)) * jnp.einsum('td,ehd->teh', xt, W3)
            out = jnp.einsum('teh,edh->ted', h, W2)
            y = jnp.einsum('te,ted->td', cw, out)
            return y.reshape(B, S, D)
        key = jax.random.key(seed)
        k0, k1, k2, k3, k4 = jax.random.split(key, 5)
        B, S, D, H = (1, 256, 128, 352)
        scale = 0.02
        x = jax.random.normal(k0, (B, S, D), jnp.float32)
        Wg = jax.random.normal(k1, (E, D), jnp.float32) * scale
        W1 = jax.random.normal(k2, (E, H, D), jnp.float32) * scale
        W2 = jax.random.normal(k3, (E, D, H), jnp.float32) * scale
        W3 = jax.random.normal(k4, (E, H, D), jnp.float32) * scale
        return {'x': x, 'Wg': Wg, 'W1': W1, 'W2': W2, 'W3': W3}
    _L0_ffn_in = _L0_ffn_setup()

    def _L1_attn_setup():
        import jax, jax.numpy as jnp
        import numpy as np
        EPS = float(np.finfo(np.float32).eps)
        B, S, F_, E, H = (8, 512, 128, 128, 16)
        HD = E // H
        LAYER = 1
        LAMBDA_INIT = 0.8 - 0.6 * float(np.exp(-0.3 * (LAYER - 1)))
        SCALE = 1.0 / float(np.sqrt(E // 2))

        def _rms(x, g):
            return x * jax.lax.rsqrt(jnp.mean(x * x, axis=-1, keepdims=True) + EPS) * g
        key = jax.random.key(seed)
        ks = jax.random.split(key, 7)
        x = jax.random.normal(ks[0], (B, S, F_), jnp.float32)
        s = 0.02
        Wq = jax.random.normal(ks[1], (E, F_), jnp.float32) * s
        Wk = jax.random.normal(ks[2], (E, F_), jnp.float32) * s
        Wv = jax.random.normal(ks[3], (E, F_), jnp.float32) * s
        W1 = jax.random.normal(ks[4], (E, E), jnp.float32) * s
        W2 = jax.random.normal(ks[5], (E, E), jnp.float32) * s
        lambda_params = jnp.full((4,), 0.8, jnp.float32)
        g1 = jnp.ones((F_,), jnp.float32)
        g2 = jnp.ones((HD,), jnp.float32)
        g3 = jnp.ones((E,), jnp.float32)
        return dict(x=x, Wq=Wq, Wk=Wk, Wv=Wv, lambda_params=lambda_params, g1=g1, g2=g2, g3=g3, W1=W1, W2=W2)
    _L1_attn_in = _L1_attn_setup()

    def _L1_ffn_setup():
        import jax, jax.numpy as jnp
        import numpy as np
        NUM_EXPERTS = 160
        TOP_K = 8
        ROUTED_SCALE = 2.5
        HIDDEN = 128
        INTER = 64
        key = jax.random.key(seed)
        ks = jax.random.split(key, 7)
        B, S = (1, 256)
        return {'hidden_states': jax.random.normal(ks[0], (B, S, HIDDEN), dtype=jnp.float32), 'router_w': jax.random.normal(ks[1], (NUM_EXPERTS, HIDDEN), dtype=jnp.float32) * 0.02, 'expert_bias': jnp.zeros((NUM_EXPERTS,), dtype=jnp.float32), 'w_gate': jax.random.normal(ks[2], (NUM_EXPERTS, INTER, HIDDEN), dtype=jnp.float32) * 0.02, 'w_down': jax.random.normal(ks[3], (NUM_EXPERTS, HIDDEN, INTER), dtype=jnp.float32) * 0.02, 'w_gate_shared': jax.random.normal(ks[4], (INTER, HIDDEN), dtype=jnp.float32) * 0.02, 'w_down_shared': jax.random.normal(ks[5], (HIDDEN, INTER), dtype=jnp.float32) * 0.02}
    _L1_ffn_in = _L1_ffn_setup()
    _d = {'L0_attn_x': _L0_attn_in['x'], 'L0_attn_wq': _L0_attn_in['wq'], 'L0_attn_wk': _L0_attn_in['wk'], 'L0_attn_wv': _L0_attn_in['wv'], 'L0_attn_wo': _L0_attn_in['wo'], 'L0_ffn_Wg': _L0_ffn_in['Wg'], 'L0_ffn_W1': _L0_ffn_in['W1'], 'L0_ffn_W2': _L0_ffn_in['W2'], 'L0_ffn_W3': _L0_ffn_in['W3'], 'L1_attn_Wq': _L1_attn_in['Wq'], 'L1_attn_Wk': _L1_attn_in['Wk'], 'L1_attn_Wv': _L1_attn_in['Wv'], 'L1_attn_lambda_params': _L1_attn_in['lambda_params'], 'L1_attn_g1': _L1_attn_in['g1'], 'L1_attn_g2': _L1_attn_in['g2'], 'L1_attn_g3': _L1_attn_in['g3'], 'L1_attn_W1': _L1_attn_in['W1'], 'L1_attn_W2': _L1_attn_in['W2'], 'L1_ffn_router_w': _L1_ffn_in['router_w'], 'L1_ffn_expert_bias': _L1_ffn_in['expert_bias'], 'L1_ffn_w_gate': _L1_ffn_in['w_gate'], 'L1_ffn_w_down': _L1_ffn_in['w_down'], 'L1_ffn_w_gate_shared': _L1_ffn_in['w_gate_shared'], 'L1_ffn_w_down_shared': _L1_ffn_in['w_down_shared']}
    _x0 = _d['L0_attn_x']
    _d['L0_attn_x'] = jax.random.normal(jax.random.fold_in(jax.random.key(seed), 1), (8, 512, 128), dtype=_x0.dtype)
    del _x0
    return _d

def reference(L0_attn_x, L0_attn_wq, L0_attn_wk, L0_attn_wv, L0_attn_wo, L0_ffn_Wg, L0_ffn_W1, L0_ffn_W2, L0_ffn_W3, L1_attn_Wq, L1_attn_Wk, L1_attn_Wv, L1_attn_lambda_params, L1_attn_g1, L1_attn_g2, L1_attn_g3, L1_attn_W1, L1_attn_W2, L1_ffn_router_w, L1_ffn_expert_bias, L1_ffn_w_gate, L1_ffn_w_down, L1_ffn_w_gate_shared, L1_ffn_w_down_shared):

    def _L0_attn_ref(x, wq, wk, wv, wo):
        import jax, jax.numpy as jnp
        import numpy as np
        THETA = 10000.0
        EPS = 1e-06
        N_HEADS = 16

        def apply_rope(x):
            b, h, l, d = x.shape
            inv_freq = 1.0 / THETA ** (jnp.arange(0, d, 2, dtype=jnp.float32) / d)
            t = jnp.arange(l, dtype=jnp.float32)
            freqs = t[:, None] * inv_freq[None, :]
            cos = jnp.cos(freqs)[None, None]
            sin = jnp.sin(freqs)[None, None]
            x1 = x[..., 0::2]
            x2 = x[..., 1::2]
            out = jnp.stack([x1 * cos - x2 * sin, x1 * sin + x2 * cos], axis=-1)
            return out.reshape(b, h, l, d)
        b, l, dim = x.shape
        h = N_HEADS
        d = dim // h
        q = (x @ wq).reshape(b, l, h, d)
        k = (x @ wk).reshape(b, l, h, d)
        v = (x @ wv).reshape(b, l, h, d)
        q = apply_rope(q.transpose(0, 2, 1, 3)).transpose(0, 2, 1, 3)
        k = apply_rope(k.transpose(0, 2, 1, 3)).transpose(0, 2, 1, 3)
        Q = jax.nn.relu(q)
        K = jax.nn.relu(k)
        kv_state = jnp.einsum('blhd,blhm->blhdm', K, v)
        kv_cumsum = jnp.cumsum(kv_state, axis=1)
        k_cumsum = jnp.cumsum(K, axis=1)
        numerator = jnp.einsum('blhd,blhdm->blhm', Q, kv_cumsum)
        denominator = jnp.einsum('blhd,blhd->blh', Q, k_cumsum)[..., None]
        out = numerator / (denominator + EPS)
        out = out.reshape(b, l, dim)
        return out @ wo

    def _L0_ffn_ref(x, Wg, W1, W2, W3):
        import jax, jax.numpy as jnp
        import numpy as np
        E = 8
        TOPK = 2

        def _moe_forward(x, Wg, W1, W2, W3):
            B, S, D = x.shape
            xt = x.reshape(-1, D)
            T = xt.shape[0]
            logits = xt @ Wg.T
            scores = jax.nn.softmax(logits, axis=-1)
            w, idx = jax.lax.top_k(scores, TOPK)
            w = w / (w.sum(axis=-1, keepdims=True) + 1e-20)
            cw = jnp.zeros((T, E), xt.dtype).at[jnp.arange(T)[:, None], idx].add(w)
            h = jax.nn.silu(jnp.einsum('td,ehd->teh', xt, W1)) * jnp.einsum('td,ehd->teh', xt, W3)
            out = jnp.einsum('teh,edh->ted', h, W2)
            y = jnp.einsum('te,ted->td', cw, out)
            return y.reshape(B, S, D)
        return _moe_forward(x, Wg, W1, W2, W3)

    def _L1_attn_ref(x, Wq, Wk, Wv, lambda_params, g1, g2, g3, W1, W2):
        import jax, jax.numpy as jnp
        import numpy as np
        EPS = float(np.finfo(np.float32).eps)
        B, S, F_, E, H = (8, 512, 128, 128, 16)
        HD = E // H
        LAYER = 1
        LAMBDA_INIT = 0.8 - 0.6 * float(np.exp(-0.3 * (LAYER - 1)))
        SCALE = 1.0 / float(np.sqrt(E // 2))

        def _rms(x, g):
            return x * jax.lax.rsqrt(jnp.mean(x * x, axis=-1, keepdims=True) + EPS) * g
        b, s_len, _ = x.shape
        xn = _rms(x, g1)
        Q = jnp.einsum('bsf,ef->bse', xn, Wq).reshape(b, s_len, H, HD)
        K = jnp.einsum('bsf,ef->bse', xn, Wk).reshape(b, s_len, H, HD)
        V = jnp.einsum('bsf,ef->bse', xn, Wv).reshape(b, s_len, H, HD)
        pQ = jax.nn.elu(Q)
        pK = jax.nn.elu(K)
        Q1, Q2 = jnp.split(pQ, 2, axis=-1)
        K1, K2 = jnp.split(pK, 2, axis=-1)
        kv1 = jnp.einsum('bshe,bshd->bsed', K1, V) * SCALE
        kv2 = jnp.einsum('bshe,bshd->bsed', K2, V) * SCALE
        w1 = jnp.einsum('bshe,bsed->bshd', Q1, kv1)
        w2 = jnp.einsum('bshe,bsed->bshd', Q2, kv2)
        lmb = jnp.exp(lambda_params[0] * lambda_params[1]) - jnp.exp(lambda_params[2] * lambda_params[3]) + LAMBDA_INIT
        attn = w1 - lmb * w2
        attn = (1.0 - LAMBDA_INIT) * _rms(attn, g2)
        attn = attn.reshape(b, s_len, E)
        attn = _rms(attn, g3) + attn
        h = jax.nn.gelu(jnp.einsum('bse,fe->bsf', attn, W1), approximate=False)
        out = jnp.einsum('bsf,ef->bse', h, W2) + attn
        return out

    def _L1_ffn_ref(hidden_states, router_w, expert_bias, w_gate, w_down, w_gate_shared, w_down_shared):
        import jax, jax.numpy as jnp
        import numpy as np
        NUM_EXPERTS = 160
        TOP_K = 8
        ROUTED_SCALE = 2.5
        HIDDEN = 128
        INTER = 64
        B, S, H = hidden_states.shape
        x = hidden_states.reshape(-1, H)
        T = x.shape[0]
        logits = x @ router_w.T + expert_bias[None, :]
        probs = jax.nn.sigmoid(logits)
        top_w, top_idx = jax.lax.top_k(probs, TOP_K)
        top_w = top_w / (jnp.sum(top_w, axis=-1, keepdims=True) + 1e-09)
        top_w = top_w * ROUTED_SCALE
        combine = jnp.zeros((T, NUM_EXPERTS), dtype=x.dtype)
        combine = combine.at[jnp.arange(T)[:, None], top_idx].set(top_w)
        h1 = jax.nn.silu(jnp.einsum('th,eih->eti', x, w_gate))
        h1w = h1 * combine.T[:, :, None]
        routed = jnp.einsum('eti,ehi->th', h1w, w_down)
        shared = jax.nn.silu(x @ w_gate_shared.T) @ w_down_shared.T
        return (routed + shared).reshape(B, S, H)
    x = L0_attn_x
    xn = _layernorm(x, axis=-1)
    s = _L0_attn_ref(xn, L0_attn_wq, L0_attn_wk, L0_attn_wv, L0_attn_wo)
    g = _silu(_L0_ffn_ref(xn, L0_ffn_Wg, L0_ffn_W1, L0_ffn_W2, L0_ffn_W3))
    x = x + s * g
    xn = _layernorm(x, axis=-1)
    s = _L1_attn_ref(xn, L1_attn_Wq, L1_attn_Wk, L1_attn_Wv, L1_attn_lambda_params, L1_attn_g1, L1_attn_g2, L1_attn_g3, L1_attn_W1, L1_attn_W2)
    g = _silu(_L1_ffn_ref(xn, L1_ffn_router_w, L1_ffn_expert_bias, L1_ffn_w_gate, L1_ffn_w_down, L1_ffn_w_gate_shared, L1_ffn_w_down_shared))
    x = x + s * g
    return x

_drawn_inputs = setup_inputs


def setup_inputs(seed=0):
    import zlib

    import numpy as np

    out = dict(_drawn_inputs(seed))
    spreads = {'L1_attn_lambda_params': (0.800000011920929, 0.6),
     'L1_attn_g1': (1.0, 0.6),
     'L1_attn_g2': (1.0, 0.6),
     'L1_attn_g3': (1.0, 0.6),
     'L1_ffn_expert_bias': (0.0, 0.593)}
    factors = {'L0_attn_wq': 8.0,
     'L0_attn_wk': 8.0,
     'L0_attn_wv': 8.0,
     'L0_attn_wo': 8.0,
     'L0_ffn_Wg': 8.0,
     'L0_ffn_W1': 8.0,
     'L0_ffn_W2': 8.0,
     'L0_ffn_W3': 8.0,
     'L1_attn_W1': 8.0,
     'L1_attn_W2': 8.0,
     'L1_ffn_router_w': 3.799,
     'L1_ffn_w_gate': 3.599,
     'L1_ffn_w_down': 3.576,
     'L1_ffn_w_gate_shared': 3.187,
     'L1_ffn_w_down_shared': 3.137}
    for name, (base, spread) in spreads.items():
        noise = np.random.default_rng([zlib.crc32(name.encode()), seed]).standard_normal(out[name].shape)
        drawn = base * np.exp(spread * noise) if base else spread * noise
        out[name] = jnp.asarray(drawn.astype(out[name].dtype))
    for name, factor in factors.items():
        out[name] = (out[name] * factor).astype(out[name].dtype)
    return out
```

```python
import concourse.bass as bass
from concourse import mybir
from contextlib import ExitStack
import numpy as np

F32 = mybir.dt.float32
BF16 = mybir.dt.bfloat16
ALU = mybir.AluOpType
ACT = mybir.ActivationFunctionType
AX = mybir.AxisListType

P = 128
D = 128
NB = 8
L = 512
T = L // P
H = 16
HD = D // H
HA = HD + 1
E0, HID0 = 8, 352
U0 = E0 * HID0 // P
E1, INTER = 160, 64
U1 = E1 * INTER // P
EB = 40
NBLK = E1 // EB
UPB = EB * INTER // P
TOPK1 = 8
LAG = 2
RH = 3
LN_EPS = 1e-5
ATT_EPS = 1e-6
RMS_EPS = float(np.finfo(np.float32).eps)
LAMBDA_INIT = 0.8 - 0.6 * float(np.exp(-0.3 * 0))
SCALE1 = 1.0 / float(np.sqrt(D // 2))

PER_BATCH = dict(
    xn0_ready=1, xn0T_ps=1, xn0T_ready=1, lg0_ps=1, e0_in=1, e0_ready=1, cw0_ready=1, cw0T_ps=1, cw0T_ready=1,
    qkv0_ps=T, rope_ready=T, v0_ready=T, qk0_ready=T, qkT0_ps=T, qkT0_ready=T, qm_ready=T, sc_ps=4 * T, at_ready=4 * T,
    av_ps=T, o0_ready=T, state_read=T - 1, state_ready=T - 1, oT_ps=T, oT_ready=T, sT0_ps=1, sT0_ready=1,
    gT0_ready=1, pT0_ready=1, p0_ps=1, x1_ready=1, xn1_ready=1, xn1T_ps=1, xn1T_ready=1, xgT_ready=1, lg1_ps=1,
    lg1a_ready=1, lg1b_ready=1, probs_ready=1, cw1_ready=1, cw1T_ps=1, cw1T_ready=1, rot_ready=1, cwrot_ready=1,
    qkv1_ps=T, mn1_ready=T, mx1_ready=T, ex1_ready=T, v1_ready=T, k1_ready=T, prod1_ready=T, a1_ready=T, a1T_ps=T,
    a1T_ready=1, h1_ps=1, gl_ready=1, o1_ps=1, sT1_ready=1,
    gT1_ready=1, pT1_ready=1, p1_ps=1, out_ready=1,
    g_ps=U0 + U1 + 1, up_ps=U0, b_ps=U0 + U1, silu_ready=U0 + U1 + 1, hu_ready=U0, hw_ready=U0 + U1,
    down_done=U0 + U1 - 1, acc_done=2,
    rsq_in=3 + 2 * T, rsq_ready=3 + 2 * T,
    x_loaded=16, out_stored=16, dve_link=0, act_link=0, pool_link=0,
)
DVE_LINKS, ACT_LINKS = 117, 0


class Seen:

    def __init__(self, sems):
        self.sems, self.count, self.reg, self.first = sems, {n: 0 for n in sems}, None, 0
        self.readers = {}

    def value(self, name, count):
        if self.reg is None:
            return count
        return (self.reg - self.first) * self.sems[name][1] + count

    def next(self, name, by=1):
        self.count[name] += by
        for names in self.readers.values():
            if name in names:
                names.remove(name)
        return self.sems[name][0], self.value(name, self.count[name])

    def lag(self, name, by):
        c = self.count[name] + 1 - by
        return None if c <= 0 and self.reg is None else (self.sems[name][0], self.value(name, c))

    def bank(self, bank):
        return [self.next(n) for n in list(self.readers.pop(bank, []))]

    def loop(self, reg, first):
        self.reg, self.first, self.entry = reg, first, dict(self.count)

    def loop_end(self, trips):
        for n, (_, per) in self.sems.items():
            got = self.count[n] - self.entry[n]
            assert got in (0, per), f"{n}: {got} events in the loop's body, {per} declared"
            self.count[n] += got * (trips - 1)
        self.reg = None


BESIDE0 = {0: ["out_silu"], 1: ["out_gate"], 2: ["out_T"], 3: ["out_add"], 4: ["rotate"], 21: ["a1T_copy"]}
for t in range(T):
    for at, name in ((5, "qkv1"), (5, "elu1"), (6, "mix1"), (9, "a1_T")):
        BESIDE0.setdefault(at + 4 * t, []).append((name, t))
BESIDE1 = {0: ["res_silu"], 1: ["res_gate", "ffh1"], 2: ["res_T", "gelu1"], 3: ["res_norm", "ffo1"], 4: ["s1"],
           6: ["xn1_T"], 7: ["xn1T_copy"], 8: ["router1"], 9: ["probs1"], 10: ["topk1"], 16: ["cw1_T"],
           17: ["cw1T_copy"], 18: ["norm0"], 21: ["xn0_T"], 22: ["xn0T_copy"], 23: ["router0"], 24: ["exp0"],
           25: ["topk0"], 29: ["cw0_T"], 30: ["cw0T_copy"], 79: ["wo"], 80: ["s0"]}
for t in range(T):
    for at, name in ((0, "qkv0"), (1, "rope"), (3, "qk_T"), (4, "qkT_copy"), (5, "scores_a"), (6, "mask_a"),
                     (7, "scores_b"), (8, "mask_b"), (9, "av"), (10, "o_norm"), (11, "o_T"), (11, "oT_copy")):
        BESIDE1.setdefault(31 + 12 * t + at, []).append((name, t))
ENTER = {"out_silu", "out_gate", "out_T", "out_add"}
MID = {"rotate", "qkv1", "elu1", "mix1", "a1_T", "a1T_copy", "ffh1", "gelu1", "ffo1", "s1"}
RES = {"res_silu", "res_gate", "res_T", "res_norm", "xn1_T", "xn1T_copy", "router1", "probs1", "topk1", "cw1_T",
       "cw1T_copy"}


def beside(table, u, want):
    for s in table.get(u, []):
        name, t = s if isinstance(s, tuple) else (s, 0)
        kind = "enter" if name in ENTER else "mid" if name in MID else "res" if name in RES else "pre"
        if kind in want:
            yield name, t


def build(nc, a, out):
    ctx = ExitStack()
    with ctx:
        def sb(name, shape, dt=F32):
            return ctx.enter_context(nc.sbuf_tensor(name, shape, dt))

        def load_all():
            pass

        w1_0, w3_0 = sb("w1_0", [P, U0 * P]), sb("w3_0", [P, U0 * P])
        w2_0 = sb("w2_0", [P, U0, D])
        wg_1, wd_1 = sb("wg_1", [P, U1 * P]), sb("wd_1", [P, U1, D])
        wgs, wds = sb("wgs", [P, INTER]), sb("wds", [INTER, D])
        wqkv0, wo0, wr0 = sb("wqkv0", [P, 3 * D]), sb("wo0", [P, D]), sb("wr0", [P, E0])
        wqkv1, wf1, wf2, wr1 = sb("wqkv1", [P, 3 * D]), sb("wf1", [P, D]), sb("wf2", [P, D]), sb("wr1", [P, E1])
        bias1, g1c, g2r, g3r, lam = sb("bias1", [P, E1]), sb("g1c", [P, 1]), sb("g2r", [P, HD]), sb("g3r", [P, D]), sb("lam", [P, 4])
        ident, identb = sb("ident", [P, P]), sb("identb", [P, P], BF16)
        cosr, sinr = sb("cosr", [P, T, HD]), sb("sinr", [P, T, HD])
        causal, headm, blockd = sb("causal", [P, P]), sb("headm", [P, 4]), sb("blockd", [P, H * HA])
        sel0, sel1 = sb("sel0", [3 * E0, U0 * P], BF16), sb("sel1", [3 * EB, UPB * P], BF16)
        xs, xn0, xn0T = sb("xs", [P, T, D]), sb("xn0", [P, T, D]), sb("xn0T", [P, L])
        st, mv, rs = sb("st", [P, T, 6]), sb("mv", [P, T, 2]), sb("rs", [P, T])
        mx0, l0, e0, sm0 = sb("mx0", [P, T]), sb("l0", [P, T, E0]), sb("e0", [P, T, E0]), sb("sm0", [P, T])
        sc0, m80, sr0 = sb("sc0", [P, T, 14]), sb("m80", [P, T, 8]), sb("sr0", [P, T, 14])
        cwf0, cwr0, cwp0 = sb("cwf0", [P, T, E0]), sb("cwr0", [P, T, E0]), sb("cwp0", [P, T, 3, E0], BF16)
        cw0T = sb("cw0T", [3 * E0, L], BF16)
        rA, rB, rr, qk, vaug = sb("rA", [P, 2 * D]), sb("rB", [P, 2 * D]), sb("rr", [P, 2 * D]), sb("qk", [P, 2 * D]), sb("vaug", [P, H, HA])
        qkT, qm, att = sb("qkT", [P, 2 * P]), sb("qm", [P, 4, P]), sb("att", [P, 4, 4 * P])
        attf = att[:].rearrange("p g c -> p (g c)")
        dn, rc, o0, oT = sb("dn", [P, H]), sb("rc", [P, H]), sb("o0", [P, H, HD]), sb("oT", [P, L])
        state, stmp = sb("state", [P, H * HA]), sb("stmp", [P, H * HA])
        sT0, gT, pT = sb("sT0", [P, L]), sb("gT", [P, L]), sb("pT", [P, L])
        x1n, x1, xn1, xn1Tn, xn1T, xgT = sb("x1n", [P, T, D]), sb("x1", [P, T, D]), xn0, sb("xn1Tn", [P, L]), sb("xn1T", [P, L]), sb("xgT", [P, L])
        ms1, r1 = sb("ms1", [P, T]), sb("r1", [P, T])
        lg, pr = sb("lg", [P, T, E1]), sb("pr", [P, T, E1])
        pr2 = attf[:, 0:T * E1].rearrange("p (t e) -> p t e", t=T)
        cwp1 = attf[:, T * E1:T * E1 + T * E1 * 3 // 2].bitcast(BF16).rearrange("p (t k a e) -> p t k a e", t=T, k=NBLK, a=3)
        prodA = attf[:, 0:HD * D].rearrange("p (e d h) -> p e d h", e=HD, d=HD)
        prodB = attf[:, HD * D:2 * HD * D].rearrange("p (h d e) -> p h d e", h=H, d=HD)
        m8, s8 = sb("m8", [P, T, 8]), sb("s8", [P, T])
        cw1Tn, cw1T = sb("cw1Tn", [3 * EB, NBLK, L], BF16), sb("cw1T", [3 * EB, NBLK, L], BF16)
        coef, lw = sb("coef", [P, HD]), sb("lw", [P, 4])
        mn1, mxq1, ex1, qk1, v1, qc1 = rA, rB, rr, qk, sb("v1", [P, D]), sb("qc1", [P, D])
        kv1 = sb("kv1", [P, HD, HD])
        at1, sq1, ss1, rd1, a1, a1b = sb("at1", [P, H, HD]), sb("sq1", [P, H, HD]), sb("ss1", [P, H]), sb("rd1", [P, 1]), sb("a1", [P, H, HD]), sb("a1b", [P, D])
        a1T, gl, sT1, gT1, outs = oT, qm, sb("sT1", [P, L]), gT, sb("outs", [P, T, D])
        hs, hw = sb("hs", [P, 2, L]), sb("hw", [P, RH, L])

        ps = {n: ctx.enter_context(nc.psum_tensor(n, [P, 512], F32)) for n in ("G0", "G1", "B0", "B1", "ACC", "U", "X0", "X1")}
        G, B = [ps["G0"], ps["G1"]], [ps["B0"], ps["B1"]]
        ACC, U, X0, X1 = ps["ACC"], ps["U"], ps["X0"], ps["X1"]

        sems = {n: (ctx.enter_context(nc.semaphore(n)), per) for n, per in PER_BATCH.items()}
        sems["dve_link"] = (sems["dve_link"][0], DVE_LINKS)
        sems["act_link"] = (sems["act_link"][0], ACT_LINKS)
        sem = {n: s for n, (s, _) in sems.items()}
        LOADS = ["small", "f0", "wg_a", "wg_b", "wd_a", "wd_b", "shared"]
        loaded = {n: ctx.enter_context(nc.semaphore(f"{n}_loaded")) for n in LOADS}
        const_ready = ctx.enter_context(nc.semaphore("const_ready"))
        coef_in = ctx.enter_context(nc.semaphore("coef_in"))
        coef_exp = ctx.enter_context(nc.semaphore("coef_exp"))

        small = [(wqkv0, "wqkv0"), (wr0, "wr0"), (ident, "ident"), (identb, "identb"), (cosr, "cosr"), (sinr, "sinr"),
                 (causal, "causal"), (headm, "headm"), (blockd, "blockd"), (wo0, "wo0"), (sel0, "sel0"), (sel1, "sel1"),
                 (wqkv1, "wqkv1"), (wf1, "wf1"), (wf2, "wf2"), (wr1, "wr1"), (bias1, "bias1"), (g1c, "g1c"),
                 (g2r, "g2r"), (g3r, "g3r"), (lam, "lam")]
        half = U1 // 2
        x_v = a["x"].rearrange("(b t p) d -> b p t d", b=NB, p=P)
        out_v = out.rearrange("(b t p) d -> b p t d", b=NB, p=P)

        neg_half, pause = sb("neg_half", [P, H]), sb("pause", [P, 1])

        block = ctx.enter_context(nc.Block())

        def pipeline(seen, fori, f0, f1):
            f1(False, {"pre"})
            f0(True, set())
            f1(False, {"res", "pre"})
            f0(True, {"mid"})
            f1(True, {"mid", "res", "pre"})
            f0(True, {"enter", "mid"})
            f1(True, {"mid", "res", "pre"})
            with fori(2, NB - 2) as g:
                seen.loop(g, 2)
                f0(True, {"enter", "mid"})
                f1(True, {"mid", "res", "pre"})
                seen.loop_end(NB - 4)
            f0(True, {"enter", "mid"})
            f1(True, {"mid", "res"})
            f0(False, {"enter", "mid"})
            f1(True, {"mid"})
            f0(False, {"enter"})

        @block.sync
        def _(sp):
            seen = Seen(sems)

            def load_x(b):
                sp.dma_start(xs[:], x_v[b]).then_inc(sem["x_loaded"], 16)

            def flush(b):
                sp.wait_ge(*seen.next("out_ready"))
                sp.dma_start(out_v[b], outs[:]).then_inc(sem["out_stored"], 16)

            load_x(0)
            for t, n in small:
                sp.dma_start(t[:], a[n]).then_inc(loaded["small"], 16)
            for t, n in ((w1_0, "w1_0"), (w3_0, "w3_0"), (w2_0, "w2_0")):
                sp.dma_start(t[:], a[n]).then_inc(loaded["f0"], 16)
            sp.dma_start(wg_1[:, 0:half * P], a["wg_1"][:, 0:half * P]).then_inc(loaded["wg_a"], 16)
            sp.dma_start(wd_1[:, 0:half, :], a["wd_1"][:, 0:half, :]).then_inc(loaded["wd_a"], 16)
            sp.dma_start(wg_1[:, half * P:], a["wg_1"][:, half * P:]).then_inc(loaded["wg_b"], 16)
            sp.dma_start(wd_1[:, half:, :], a["wd_1"][:, half:, :]).then_inc(loaded["wd_b"], 16)
            sp.dma_start(wgs[:], a["wgs"]).then_inc(loaded["shared"], 16)
            sp.dma_start(wds[:], a["wds"]).then_inc(loaded["shared"], 16)
            sp.wait_ge(*seen.next("x1_ready"))
            load_x(1)
            sp.wait_ge(*seen.next("x1_ready"))
            load_x(2)
            flush(0)
            sp.wait_ge(*seen.next("x1_ready"))
            load_x(3)
            with sp.Fori(2, NB - 2) as g:
                seen.loop(g, 2)
                flush(g - 1)
                sp.wait_ge(*seen.next("x1_ready"))
                load_x(g + 2)
                seen.loop_end(NB - 4)
            for b in range(NB - 3, NB):
                flush(b)
            sp.wait_ge(sem["out_stored"], 16 * NB)

        @block.tensor
        def _(pe):
            seen = Seen(sems)

            def reuse(bank):
                for s, v in seen.bank(bank):
                    pe.wait_ge(s, v)

            def transposes(bank, src, name):
                for t in range(T):
                    last = nc.tensor.transpose(ps[bank][:, t * P:(t + 1) * P], src(t), ident[:])
                last.then_inc(sem[name], 1)

            def s_xn0_T(t):
                pe.wait_ge(*seen.next("xn0_ready"))
                reuse("X0")
                transposes("X0", lambda t: xn0[:, t, :], "xn0T_ps")
                seen.readers["X0"] = ["xn0T_ready"]

            def s_router0(t):
                pe.wait_ge(*seen.next("xn0T_ready"))
                reuse("X1")
                for t in range(T):
                    last = nc.tensor.matmul(X1[:, t * E0:(t + 1) * E0], xn0T[:, t * P:(t + 1) * P], wr0[:], start=True, stop=True)
                last.then_inc(sem["lg0_ps"], 1)
                seen.readers["X1"] = ["e0_in"]

            def s_cw0_T(t):
                pe.wait_ge(*seen.next("cw0_ready"))
                reuse("X1")
                xb = X1[:, :].bitcast(BF16)
                for t in range(T):
                    last = nc.tensor.transpose(xb[0:3 * E0, t * P:(t + 1) * P],
                                               cwp0[:, t, :, :].rearrange("p a e -> p (a e)"), identb[:])
                last.then_inc(sem["cw0T_ps"], 1)
                seen.readers["X1"] = ["cw0T_ready"]

            def s_qkv0(t):
                reuse("X0")
                nc.tensor.matmul(X0[:, 0:3 * D], xn0T[:, t * P:(t + 1) * P], wqkv0[:], start=True, stop=True)\
                    .then_inc(sem["qkv0_ps"], 1)
                seen.readers["X0"] = ["rope_ready", "v0_ready"]

            def s_qk_T(t):
                pe.wait_ge(*seen.next("qk0_ready"))
                reuse("X1")
                nc.tensor.transpose(X1[:, 0:P], qk[:, 0:D], ident[:])
                nc.tensor.transpose(X1[:, P:2 * P], qk[:, D:2 * D], ident[:]).then_inc(sem["qkT0_ps"], 1)
                seen.readers["X1"] = ["qkT0_ready", "qm_ready"]

            def score(g, bank):
                reuse(bank)
                nc.tensor.matmul(ps[bank][:, :], qkT[32 * g:32 * g + 32, P:2 * P], qm[32 * g:32 * g + 32, :, :],
                                 start=True, stop=True).then_inc(sem["sc_ps"], 1)
                seen.readers[bank] = ["at_ready"]

            def s_scores_a(t):
                pe.wait_ge(*seen.next("qkT0_ready"))
                pe.wait_ge(*seen.next("qm_ready"))
                if t:
                    pe.wait_ge(*seen.next("state_ready"))
                    reuse("U")
                    nc.tensor.matmul(U[:, 0:H * HA], qkT[:, 0:P], state[:], start=True, stop=False, skip_group_check=True)
                score(0, "X0")
                score(1, "X1")

            def s_scores_b(t):
                pe.wait_ge(*seen.next("at_ready"))
                score_now(2, "X0")
                pe.wait_ge(*seen.next("at_ready"))
                score_now(3, "X1")

            def score_now(g, bank):
                nc.tensor.matmul(ps[bank][:, :], qkT[32 * g:32 * g + 32, P:2 * P], qm[32 * g:32 * g + 32, :, :],
                                 start=True, stop=True).then_inc(sem["sc_ps"], 1)
                seen.readers[bank] = []

            def s_av(t):
                pe.wait_ge(*seen.next("at_ready", 2))
                reuse("U")
                if t < T - 1:
                    nc.tensor.matmul(X0[:, 0:H * HA], qk[:, D:2 * D], vaug[:].rearrange("p h m -> p (h m)"), start=True, stop=True)
                    seen.readers["X0"] = ["state_read"]
                for h in range(H):
                    last = nc.tensor.matmul(U[:, h * HA:(h + 1) * HA], att[:, h // 4, (h % 4) * P:(h % 4 + 1) * P], vaug[:, h, :],
                                            start=(t == 0 and h == 0), stop=(h == H - 1), skip_group_check=True)
                last.then_inc(sem["av_ps"], 1)
                seen.readers["U"] = ["o0_ready"]

            def s_o_T(t):
                pe.wait_ge(*seen.next("o0_ready"))
                reuse("X1")
                nc.tensor.transpose(X1[:, 0:P], o0[:].rearrange("p h m -> p (h m)"), ident[:]).then_inc(sem["oT_ps"], 1)
                seen.readers["X1"] = ["oT_ready"]

            def s_wo(t):
                pe.wait_ge(*seen.next("oT_ready"))
                reuse("X0")
                nc.tensor.matmul(X0[:, :], wo0[:], oT[:], start=True, stop=True).then_inc(sem["sT0_ps"], 1)
                seen.readers["X0"] = ["sT0_ready"]

            def s_res_T(t):
                pe.wait_ge(*seen.next("pT0_ready"))
                reuse("X0")
                transposes("X0", lambda t: pT[:, t * P:(t + 1) * P], "p0_ps")
                seen.readers["X0"] = ["x1_ready"]

            def s_xn1_T(t):
                pe.wait_ge(*seen.next("xn1_ready"))
                reuse("X1")
                transposes("X1", lambda t: xn1[:, t, :], "xn1T_ps")
                seen.readers["X1"] = ["xn1T_ready", "xgT_ready"]

            def s_router1(t):
                pe.wait_ge(*seen.next("xn1T_ready"))
                reuse("X0")
                reuse("U")
                for t in range(T):
                    bank = (X0, U)[t // 2]
                    last = nc.tensor.matmul(bank[:, (t % 2) * E1:(t % 2 + 1) * E1], xn1Tn[:, t * P:(t + 1) * P], wr1[:],
                                            start=True, stop=True)
                last.then_inc(sem["lg1_ps"], 1)
                seen.readers["X0"], seen.readers["U"] = ["lg1a_ready"], ["lg1b_ready"]

            def s_cw1_T(t):
                pe.wait_ge(*seen.next("cw1_ready"))
                for bank in ("X0", "X1"):
                    reuse(bank)
                for k in range(NBLK):
                    xb = (X0, X1)[k // 2][:, :].bitcast(BF16)
                    for t in range(T):
                        c = (k % 2) * L + t * P
                        last = nc.tensor.transpose(xb[0:3 * EB, c:c + P], cwp1[:, t, k, :, :].rearrange("p a e -> p (a e)"), identb[:])
                last.then_inc(sem["cw1T_ps"], 1)
                seen.readers["X0"] = ["cw1T_ready"]
                seen.readers["X1"] = ["cw1T_ready"]

            def s_qkv1(t):
                reuse("X0")
                nc.tensor.matmul(X0[:, 0:3 * D], xgT[:, t * P:(t + 1) * P], wqkv1[:], start=True, stop=True)\
                    .then_inc(sem["qkv1_ps"], 1)
                seen.readers["X0"] = ["mn1_ready", "mx1_ready", "v1_ready"]

            def s_a1_T(t):
                pe.wait_ge(*seen.next("a1_ready"))
                if t == 0:
                    reuse("X1")
                nc.tensor.transpose(X1[:, t * P:(t + 1) * P], a1b[:], ident[:]).then_inc(sem["a1T_ps"], 1)
                seen.readers["X1"] = ["a1T_ready"] if t == T - 1 else []

            def s_ffh1(t):
                pe.wait_ge(*seen.next("a1T_ready"))
                reuse("U")
                nc.tensor.matmul(U[:, :], wf1[:], a1T[:], start=True, stop=True).then_inc(sem["h1_ps"], 1)
                seen.readers["U"] = ["gl_ready"]

            def s_ffo1(t):
                pe.wait_ge(*seen.next("gl_ready"))
                nc.tensor.matmul(U[:, :], wf2[:], gl[:].rearrange("p a b -> p (a b)"), start=True, stop=True).then_inc(sem["o1_ps"], 1)
                seen.readers["U"] = ["sT1_ready"]

            def s_out_T(t):
                pe.wait_ge(*seen.next("pT1_ready"))
                reuse("X0")
                transposes("X0", lambda t: pT[:, t * P:(t + 1) * P], "p1_ps")
                seen.readers["X0"] = ["out_ready"]

            steps = {n[2:]: f for n, f in locals().items() if n.startswith("s_")}

            def others(table, u, want):
                for name, t in beside(table, u, want):
                    if name in steps:
                        steps[name](t)

            def gate(u, bank_free_lag, w, x):
                w_free = seen.lag("g_ps", bank_free_lag)
                if w_free:
                    pe.wait_ge(sem["silu_ready"], w_free[1])
                m = w.shape[1]
                nc.tensor.matmul(G[u % 2][0:m, :], w, x, start=True, stop=True).then_inc(sem["g_ps"], 1)
                seen.next("g_ps")

            def weights(u, sel, cw):
                b_free = seen.lag("b_ps", 2)
                if b_free:
                    pe.wait_ge(sem["hw_ready"], b_free[1])
                nc.tensor.matmul(B[u % 2][:, :], sel, cw, start=True, stop=True).then_inc(sem["b_ps"], 1)
                seen.next("b_ps")

            def acc_start():
                reuse("ACC")

            def f0(units, want):
                n = U0
                if units:
                    reuse("U")
                for u in range(n + LAG):
                    if u < n and units:
                        gate(u, 1 if u == 0 else 2, w1_0[:, u * P:(u + 1) * P], xn0T[:])
                        weights(u, sel0[:, u * P:(u + 1) * P], cw0T[:])
                        reuse("U")
                        nc.tensor.matmul(U[:, :], w3_0[:, u * P:(u + 1) * P], xn0T[:], start=True, stop=True).then_inc(sem["up_ps"], 1)
                        seen.readers["U"] = ["hu_ready"]
                    if u >= LAG and units:
                        v = u - LAG
                        if v == 0:
                            acc_start()
                        pe.wait_ge(*seen.next("hw_ready"))
                        nc.tensor.matmul(ACC[:, :], w2_0[:, v, :], hw[:, v % RH, :], start=(v == 0), stop=(v == n - 1))\
                            .then_inc(sem["acc_done" if v == n - 1 else "down_done"], 1)
                    others(BESIDE0, u, want)
                if units:
                    seen.readers["ACC"] = ["gT0_ready"]

            first = [True]

            def f1(units, want):
                n = U1 + 1
                if units:
                    pe.wait_ge(*seen.next("rot_ready"))
                    pe.wait_ge(*seen.next("cwrot_ready"))
                for u in range(n + LAG):
                    if units and first[0]:
                        if u in (0, half):
                            pe.wait_ge(loaded["wg_a" if u == 0 else "wg_b"], 16)
                        if u in (LAG, half + LAG):
                            pe.wait_ge(loaded["wd_a" if u == LAG else "wd_b"], 16)
                        if u == U1:
                            pe.wait_ge(loaded["shared"], 32)
                            first[0] = False
                    if u < U1 and units:
                        gate(u, 2, wg_1[:, u * P:(u + 1) * P], xn1T[:])
                        k = u % UPB
                        weights(u, sel1[:, k * P:(k + 1) * P], cw1T[:, u // UPB, :])
                    if u == U1 and units:
                        gate(u, 2, wgs[:], xn1T[:])
                    if u >= LAG and units:
                        v = u - LAG
                        if v == 0:
                            acc_start()
                        if v < U1:
                            pe.wait_ge(*seen.next("hw_ready"))
                            nc.tensor.matmul(ACC[:, :], wd_1[:, v, :], hw[:, v % RH, :], start=(v == 0), stop=False)\
                                .then_inc(sem["down_done"], 1)
                        else:
                            s, c = seen.sems["silu_ready"][0], seen.value("g_ps", seen.count["g_ps"])
                            pe.wait_ge(s, c)
                            nc.tensor.matmul(ACC[:, :], wds[:], hs[0:INTER, v % 2, :], start=False, stop=True)\
                                .then_inc(sem["acc_done"], 1)
                    others(BESIDE1, u, want)
                if units:
                    seen.readers["ACC"] = ["gT1_ready"]

            pe.wait_ge(loaded["small"], 16 * len(small))
            pe.wait_ge(const_ready, 1)
            pe.wait_ge(loaded["f0"], 48)
            pipeline(seen, pe.Fori, f0, f1)

        @block.scalar
        def _(act):
            seen = Seen(sems)

            def copy(dst, src, after, name):
                if after:
                    act.wait_ge(*seen.next(after))
                nc.scalar.activation(dst, src, ACT.Copy).then_inc(sem[name], 1)

            def s_xn0T_copy(t):
                copy(xn0T[:], X0[:, :], "xn0T_ps", "xn0T_ready")

            def s_exp0(t):
                act.wait_ge(*seen.next("e0_in"))
                nc.scalar.activation(e0[:], l0[:], ACT.Exp).then_inc(sem["e0_ready"], 1)

            def s_cw0T_copy(t):
                copy(cw0T[:], X1[:, :].bitcast(BF16)[0:3 * E0, 0:L], "cw0T_ps", "cw0T_ready")

            def s_rope(t):
                act.wait_ge(*seen.next("rope_ready"))
                nc.scalar.activation(qk[:], rr[:], ACT.Relu).then_inc(sem["qk0_ready"], 1)
                copy(vaug[:, :, 0:HD], X0[:, 2 * D:3 * D].rearrange("p (h m) -> p h m", h=H), None, "v0_ready")

            def s_qkT_copy(t):
                copy(qkT[:], X1[:, 0:2 * P], "qkT0_ps", "qkT0_ready")

            def s_oT_copy(t):
                copy(oT[:, t * P:(t + 1) * P], X1[:, 0:P], "oT_ps", "oT_ready")

            def s_s0(t):
                copy(sT0[:], X0[:, :], "sT0_ps", "sT0_ready")

            def s_res_silu(t):
                act.wait_ge(*seen.next("acc_done"))
                nc.scalar.activation(gT[:], ACC[:, :], ACT.Silu).then_inc(sem["gT0_ready"], 1)

            def s_xn1T_copy(t):
                copy(xn1Tn[:], X1[:, :], "xn1T_ps", "xn1T_ready")

            def s_probs1(t):
                act.wait_ge(*seen.next("lg1a_ready"))
                act.wait_ge(*seen.next("lg1b_ready"))
                nc.scalar.activation(pr[:], lg[:], ACT.Sigmoid).then_inc(sem["probs_ready"], 1)

            def s_cw1T_copy(t):
                act.wait_ge(*seen.next("cw1T_ps"))
                for i, bank in enumerate((X0, X1)):
                    last = nc.scalar.activation(cw1Tn[:, 2 * i:2 * i + 2, :],
                                                bank[:, :].bitcast(BF16)[0:3 * EB, :].rearrange("p (k l) -> p k l", k=2), ACT.Copy)
                last.then_inc(sem["cw1T_ready"], 1)
                seen.next("cw1T_ready")

            def s_rotate(t):
                act.wait_ge(sem["cw1T_ready"], seen.value("cw1T_ready", seen.count["cw1T_ready"]))
                nc.scalar.activation(cw1T[:], cw1Tn[:], ACT.Copy).then_inc(sem["cwrot_ready"], 1)

            def s_elu1(t):
                copy_r = r1[:, t:t + 1]
                act.wait_ge(*seen.next("mx1_ready"))
                nc.scalar.activation(v1[:], X0[:, 2 * D:3 * D], ACT.Copy, scale=copy_r).then_inc(sem["v1_ready"], 1)
                act.wait_ge(*seen.next("mn1_ready"))
                nc.scalar.activation(ex1[:], mn1[:], ACT.Exp).then_inc(sem["ex1_ready"], 1)

            def s_a1T_copy(t):
                act.wait_ge(*seen.next("a1T_ps", T))
                nc.scalar.activation(a1T[:], X1[:, :], ACT.Copy).then_inc(sem["a1T_ready"], 1)

            def s_gelu1(t):
                act.wait_ge(*seen.next("h1_ps"))
                nc.scalar.activation(gl[:].rearrange("p a b -> p (a b)"), U[:, :], ACT.Gelu).then_inc(sem["gl_ready"], 1)

            def s_out_silu(t):
                act.wait_ge(*seen.next("acc_done"))
                nc.scalar.activation(gT1[:], ACC[:, :], ACT.Silu).then_inc(sem["gT1_ready"], 1)

            steps = {n[2:]: f for n, f in locals().items() if n.startswith("s_")}

            def others(table, u, want):
                for name, t in beside(table, u, want):
                    if name in steps:
                        steps[name](t)

            def units_of(n, table, units, want):
                for u in range(n):
                    if u == 0:
                        others(table, u, want)
                    if units:
                        act.wait_ge(*seen.next("g_ps"))
                        if u >= 2:
                            act.wait_ge(*seen.next("hw_ready"))
                        m = INTER if n == U1 + 1 and u == U1 else P
                        nc.scalar.activation(hs[0:m, u % 2, :], G[u % 2][0:m, :], ACT.Silu).then_inc(sem["silu_ready"], 1)
                    if u > 0:
                        others(table, u, want)
                if units:
                    seen.next("hw_ready", 2 if n == U0 else 1)

            act.wait_ge(coef_in, 2)
            nc.scalar.activation(lw[:, 2:4], lw[:, 0:2], ACT.Exp).then_inc(coef_exp, 1)
            pipeline(seen, act.Fori, lambda un, w: units_of(U0, BESIDE0, un, w), lambda un, w: units_of(U1 + 1, BESIDE1, un, w))

        @block.gpsimd
        def _(pool):
            seen = Seen(sems)

            def s_mix1(t):
                pool.wait_ge(*seen.next("k1_ready"))
                pool.wait_ge(*seen.next("v1_ready"))
                k = qk1[:, D:2 * D].rearrange("p (h e) -> p e h", h=H).unsqueeze(2).broadcast_to([P, HD, HD, H])
                v = v1[:].rearrange("p (h d) -> p d h", h=H).unsqueeze(1).broadcast_to([P, HD, HD, H])
                nc.gpsimd.tensor_tensor(prodA, k, v, ALU.mult).then_inc(sem["prod1_ready"], 1)

                rsqrt(ss1[:])
                rsqrt(rd1[:])

            def rsqrt(v):
                pool.wait_ge(*seen.next("rsq_in"))
                nc.gpsimd.tensor_tensor(v, v, neg_half[:, 0:v.shape[1]], ALU.pow).then_inc(sem["rsq_ready"], 1)

            def s_norm0(t):
                rsqrt(rs[:])

            def s_res_norm(t):
                rsqrt(rs[:])
                rsqrt(r1[:])

            steps = {n[2:]: f for n, f in locals().items() if n.startswith("s_")}

            def others(n, table, want):
                for u in range(n):
                    for name, t in beside(table, u, want):
                        if name in steps:
                            steps[name](t)

            nc.gpsimd.memset(neg_half[:], -0.5).then_inc(sem["pool_link"], 1)
            pool.wait_ge(sem["pool_link"], 1)
            pipeline(seen, pool.Fori, lambda un, w: others(U0, BESIDE0, w), lambda un, w: others(U1 + 1, BESIDE1, w))

        @block.vector
        def _(dve):
            seen = Seen(sems)

            def link(ins):
                seen.next("dve_link")
                ins.then_inc(sem["dve_link"], 1)
                return ins

            def join():
                dve.wait_ge(sem["dve_link"], seen.value("dve_link", seen.count["dve_link"]))

            def join_alone():
                join()
                nc.vector.memset(pause[:], 0.0)

            def rsqrt(ins):
                ins.then_inc(sem["rsq_in"], 1)
                dve.wait_ge(*seen.next("rsq_ready"))

            def norm(src, dst, name):
                for t in range(T):
                    link(nc.vector.bn_stats(st[:, t, :], src[:, t, :]))
                join_alone()
                for t in range(T):
                    link(nc.vector.bn_aggr(mv[:, t, :], st[:, t, :]))
                join()
                rsqrt(nc.vector.tensor_scalar(rs[:], mv[:, :, 1], LN_EPS, None, ALU.add))
                for t in range(T):
                    last = nc.vector.tensor_scalar(dst[:, t, :], src[:, t, :], mv[:, t, 0:1], rs[:, t:t + 1], ALU.subtract, ALU.mult)
                last.then_inc(sem[name], 1)

            def parts(cw, rest, out_p, name):
                link(nc.vector.tensor_copy(out_p(0), cw))
                join()
                link(nc.vector.tensor_tensor(rest, cw, out_p(0), ALU.subtract))
                join()
                link(nc.vector.tensor_copy(out_p(1), rest))
                join()
                nc.vector.tensor_tensor(out_p(2), rest, out_p(1), ALU.subtract).then_inc(sem[name], 1)

            def s_norm0(t):
                dve.wait_ge(*seen.next("x_loaded", 16))
                norm(xs, xn0, "xn0_ready")

            def s_exp0(t):
                dve.wait_ge(*seen.next("lg0_ps"))
                lgt = X1[:, 0:T * E0].rearrange("p (t e) -> p t e", t=T)
                link(nc.vector.tensor_reduce(mx0[:], lgt, AX.X, ALU.max))
                join()
                nc.vector.tensor_tensor(l0[:], lgt, mx0[:].unsqueeze(2).broadcast_to([P, T, E0]), ALU.subtract).then_inc(sem["e0_in"], 1)

            def s_topk0(t):
                dve.wait_ge(*seen.next("e0_ready"))
                link(nc.vector.tensor_reduce(sm0[:], e0[:], AX.X, ALU.add))
                join()
                link(nc.vector.reciprocal(sm0[:], sm0[:]))
                join()
                link(nc.vector.tensor_tensor(sc0[:, :, 0:E0], e0[:], sm0[:].unsqueeze(2).broadcast_to([P, T, E0]), ALU.mult))
                join_alone()
                for t in range(T):
                    link(nc.vector.max(m80[:, t, :], sc0[:, t, 0:E0]))
                join()
                link(nc.vector.memset(m80[:, :, 2:8], -1.0))
                link(nc.vector.tensor_tensor(sm0[:], m80[:, :, 0], m80[:, :, 1], ALU.add))
                join_alone()
                for t in range(T):
                    link(nc.vector.match_replace(sr0[:, t, :], m80[:, t, :], sc0[:, t, :], 0.0))
                link(nc.vector.tensor_scalar(sm0[:], sm0[:], 1e-20, None, ALU.add))
                join()
                link(nc.vector.reciprocal(sm0[:], sm0[:]))
                link(nc.vector.tensor_tensor(cwf0[:], sc0[:, :, 0:E0], sr0[:, :, 0:E0], ALU.subtract))
                join()
                link(nc.vector.tensor_tensor(cwf0[:], cwf0[:], sm0[:].unsqueeze(2).broadcast_to([P, T, E0]), ALU.mult))
                join()
                parts(cwf0[:], cwr0[:], lambda i: cwp0[:, :, i, :], "cw0_ready")

            def s_rope(t):
                dve.wait_ge(*seen.next("qkv0_ps"))
                x = X0[:, 0:2 * D].rearrange("p (h m) -> p h m", m=HD)
                c = cosr[:, t, :].unsqueeze(1).broadcast_to([P, 2 * H, HD])
                link(nc.vector.tensor_tensor(rA[:].rearrange("p (h m) -> p h m", m=HD), x, c, ALU.mult))
                xp = X0[:, 0:2 * D].rearrange("p (h i two) -> p h i two", i=HD // 2, two=2)
                op = rB[:].rearrange("p (h i two) -> p h i two", i=HD // 2, two=2)
                s = sinr[:, t, :].rearrange("p (i two) -> p i two", two=2)
                for j in range(2):
                    link(nc.vector.tensor_tensor(op[:, :, :, j], xp[:, :, :, 1 - j],
                                                 s[:, :, j].unsqueeze(1).broadcast_to([P, 2 * H, HD // 2]), ALU.mult))
                join()
                nc.vector.tensor_tensor(rr[:], rA[:], rB[:], ALU.add).then_inc(sem["rope_ready"], 1)

            def s_qkT_copy(t):
                dve.wait_ge(*seen.next("qkT0_ready"))
                nc.vector.tensor_tensor(qm[:], qkT[:, 0:P].unsqueeze(1).broadcast_to([P, 4, P]),
                                        headm[:].unsqueeze(2).broadcast_to([P, 4, P]), ALU.mult).then_inc(sem["qm_ready"], 1)

            def mask(g):
                dve.wait_ge(*seen.next("sc_ps"))
                nc.vector.tensor_tensor(att[:, g, :].rearrange("p (r i) -> p r i", r=4),
                                        (X0, X1)[g % 2][:, :].rearrange("p (r i) -> p r i", r=4),
                                        causal[:].unsqueeze(1).broadcast_to([P, 4, P]), ALU.mult).then_inc(sem["at_ready"], 1)

            def s_mask_a(t):
                mask(0)
                mask(1)

            def s_mask_b(t):
                mask(2)
                mask(3)

            def s_o_norm(t):
                dve.wait_ge(*seen.next("av_ps"))
                u = U[:, 0:H * HA].rearrange("p (h m) -> p h m", m=HA)
                link(nc.vector.tensor_scalar(dn[:], u[:, :, HD], ATT_EPS, None, ALU.add))
                if t == 0:
                    link(nc.vector.memset(state[:], 0.0))
                if t < T - 1:
                    nc.vector.tensor_tensor(stmp[:], X0[:, 0:H * HA], blockd[:], ALU.mult).then_inc(sem["state_read"], 1)
                join()
                link(nc.vector.reciprocal(rc[:], dn[:]))
                if t < T - 1:
                    dve.wait_ge(*seen.next("state_read"))
                    nc.vector.tensor_tensor(state[:], state[:], stmp[:], ALU.add).then_inc(sem["state_ready"], 1)
                join()
                nc.vector.tensor_tensor(o0[:], u[:, :, 0:HD], rc[:].unsqueeze(2).broadcast_to([P, H, HD]), ALU.mult)\
                    .then_inc(sem["o0_ready"], 1)

            def s_res_gate(t):
                dve.wait_ge(*seen.next("gT0_ready"))
                dve.wait_ge(*seen.next("sT0_ready"))
                nc.vector.tensor_tensor(pT[:], sT0[:], gT[:], ALU.mult).then_inc(sem["pT0_ready"], 1)

            def s_res_norm(t):
                dve.wait_ge(*seen.next("p0_ps"))
                nc.vector.tensor_tensor(x1n[:], xs[:], X0[:, :].rearrange("p (t d) -> p t d", t=T), ALU.add).then_inc(sem["x1_ready"], 1)
                dve.wait_ge(*seen.next("x1_ready"))
                norm(x1n, xn1, "xn1_ready")
                link(nc.vector.tensor_tensor(ms1[:], rs[:], rs[:], ALU.mult))
                join()
                link(nc.vector.tensor_tensor(ms1[:], ms1[:], mv[:, :, 1], ALU.mult))
                join()
                rsqrt(nc.vector.tensor_scalar(r1[:], ms1[:], RMS_EPS, None, ALU.add))

            def s_xn1T_copy(t):
                dve.wait_ge(*seen.next("xn1T_ready"))
                nc.vector.tensor_scalar(xgT[:], xn1Tn[:], g1c[:, 0:1], None, ALU.mult).then_inc(sem["xgT_ready"], 1)

            def s_probs1(t):
                dve.wait_ge(*seen.next("lg1_ps"))
                for i, (bank, done) in enumerate(((X0, "lg1a_ready"), (U, "lg1b_ready"))):
                    nc.vector.tensor_tensor(lg[:, 2 * i:2 * i + 2, :], bank[:, 0:2 * E1].rearrange("p (t e) -> p t e", t=2),
                                            bias1[:].unsqueeze(1).broadcast_to([P, 2, E1]), ALU.add).then_inc(sem[done], 1)

            def s_topk1(t):
                dve.wait_ge(*seen.next("probs_ready"))
                nc.vector.memset(pause[:], 0.0)
                for t in range(T):
                    link(nc.vector.max(m8[:, t, :], pr[:, t, :]))
                join_alone()
                for t in range(T):
                    link(nc.vector.match_replace(pr2[:, t, :], m8[:, t, :], pr[:, t, :], 0.0))
                link(nc.vector.tensor_reduce(s8[:], m8[:], AX.X, ALU.add))
                join()
                link(nc.vector.tensor_scalar(s8[:], s8[:], 1e-9, None, ALU.add))
                link(nc.vector.tensor_tensor(lg[:], pr[:], pr2[:], ALU.subtract))
                join()
                link(nc.vector.reciprocal(s8[:], s8[:]))
                join()
                link(nc.vector.tensor_tensor(pr[:], lg[:], s8[:].unsqueeze(2).broadcast_to([P, T, E1]), ALU.mult))
                join()
                link(nc.vector.tensor_scalar(lg[:], pr[:], 2.5, None, ALU.mult))
                join()

                def split(v):
                    return v.rearrange("p t (k e) -> p t k e", k=NBLK)
                cw, rest = split(lg[:]), split(pr[:])
                parts(cw, rest, lambda i: cwp1[:, :, :, i, :], "cw1_ready")

            def s_rotate(t):
                if seen.count["out_ready"]:
                    dve.wait_ge(sem["out_ready"], seen.value("out_ready", seen.count["out_ready"]))
                nc.vector.tensor_copy(x1[:], x1n[:])
                nc.vector.tensor_copy(xn1T[:], xn1Tn[:]).then_inc(sem["rot_ready"], 1)

            def s_elu1(t):
                dve.wait_ge(*seen.next("qkv1_ps"))
                nc.vector.tensor_scalar(mn1[:], X0[:, 0:2 * D], r1[:, t:t + 1], 0.0, ALU.mult, ALU.min).then_inc(sem["mn1_ready"], 1)
                nc.vector.tensor_scalar(mxq1[:], X0[:, 0:2 * D], r1[:, t:t + 1], 0.0, ALU.mult, ALU.max).then_inc(sem["mx1_ready"], 1)
                dve.wait_ge(*seen.next("mx1_ready"))
                dve.wait_ge(*seen.next("ex1_ready"))
                nc.vector.scalar_tensor_tensor(qk1[:], ex1[:], -1.0, mxq1[:], ALU.add, ALU.add).then_inc(sem["k1_ready"], 1)
                dve.wait_ge(*seen.next("k1_ready"))
                link(nc.vector.tensor_tensor(qc1[:].rearrange("p (h e) -> p h e", h=H), qk1[:, 0:D].rearrange("p (h e) -> p h e", h=H),
                                             coef[:].unsqueeze(1).broadcast_to([P, H, HD]), ALU.mult))

            def s_mix1(t):
                dve.wait_ge(*seen.next("prod1_ready"))
                link(nc.vector.tensor_reduce(kv1[:], prodA, AX.X, ALU.add))
                join()
                q = qc1[:].rearrange("p (h e) -> p h e", h=H).unsqueeze(2).broadcast_to([P, H, HD, HD])
                kv = kv1[:].rearrange("p e d -> p d e").unsqueeze(1).broadcast_to([P, H, HD, HD])
                link(nc.vector.tensor_tensor(prodB, q, kv, ALU.mult))
                join()
                link(nc.vector.tensor_reduce(at1[:], prodB, AX.X, ALU.add))
                join()
                link(nc.vector.tensor_tensor(sq1[:], at1[:], at1[:], ALU.mult))
                join()
                link(nc.vector.tensor_reduce(ss1[:], sq1[:], AX.X, ALU.add))
                join()
                rsqrt(nc.vector.tensor_scalar(ss1[:], ss1[:], 1.0 / HD, RMS_EPS, ALU.mult, ALU.add))
                link(nc.vector.tensor_tensor(sq1[:], at1[:], ss1[:].unsqueeze(2).broadcast_to([P, H, HD]), ALU.mult))
                join()
                link(nc.vector.tensor_tensor(a1[:], sq1[:], g2r[:].unsqueeze(1).broadcast_to([P, H, HD]), ALU.mult))
                join()
                link(nc.vector.scalar_tensor_tensor(sq1[:], a1[:], 1.0, a1[:], ALU.mult, ALU.mult, accum_out=rd1[:]))
                join()
                rsqrt(nc.vector.tensor_scalar(rd1[:], rd1[:], 1.0 / D, RMS_EPS, ALU.mult, ALU.add))
                sqf = sq1[:].rearrange("p h d -> p (h d)")
                link(nc.vector.tensor_scalar(sqf, g3r[:], rd1[:, 0:1], 1.0, ALU.mult, ALU.add))
                join()
                nc.vector.tensor_tensor(a1b[:], a1[:].rearrange("p h d -> p (h d)"), sqf, ALU.mult).then_inc(sem["a1_ready"], 1)

            def s_s1(t):
                dve.wait_ge(*seen.next("o1_ps"))
                nc.vector.tensor_tensor(sT1[:], a1T[:], U[:, :], ALU.add).then_inc(sem["sT1_ready"], 1)

            def s_out_gate(t):
                dve.wait_ge(*seen.next("gT1_ready"))
                dve.wait_ge(*seen.next("sT1_ready"))
                nc.vector.tensor_tensor(pT[:], sT1[:], gT1[:], ALU.mult).then_inc(sem["pT1_ready"], 1)

            def s_out_add(t):
                dve.wait_ge(*seen.next("p1_ps"))
                if seen.count["out_stored"]:
                    dve.wait_ge(sem["out_stored"], seen.value("out_stored", seen.count["out_stored"]))
                seen.next("out_stored", 16)
                seen.next("out_ready")
                nc.vector.tensor_tensor(outs[:], x1[:], X0[:, :].rearrange("p (t d) -> p t d", t=T), ALU.add).then_inc(sem["out_ready"], 1)

            steps = {n[2:]: f for n, f in locals().items() if n.startswith("s_")}

            def others(table, u, want):
                for name, t in beside(table, u, want):
                    if name in steps:
                        steps[name](t)

            def hw_free(u):
                if u < RH:
                    if seen.count["acc_done"]:
                        dve.wait_ge(sem["acc_done"], seen.value("acc_done", seen.count["acc_done"]))
                else:
                    dve.wait_ge(*seen.next("down_done"))

            def f0(units, want):
                for u in range(U0):
                    if units:
                        dve.wait_ge(*seen.next("silu_ready"))
                        dve.wait_ge(*seen.next("up_ps"))
                        nc.vector.tensor_tensor(hs[:, u % 2, :], hs[:, u % 2, :], U[:, :], ALU.mult).then_inc(sem["hu_ready"], 1)
                        dve.wait_ge(*seen.next("hu_ready"))
                        dve.wait_ge(*seen.next("b_ps"))
                        hw_free(u)
                        nc.vector.tensor_tensor(hw[:, u % RH, :], hs[:, u % 2, :], B[u % 2][:, :], ALU.mult).then_inc(sem["hw_ready"], 1)
                    others(BESIDE0, u, want)
                if units:
                    seen.next("down_done", RH - 1)
                    seen.next("acc_done")

            def f1(units, want):
                for u in range(U1 + 1):
                    if units:
                        dve.wait_ge(*seen.next("silu_ready"))
                        if u < U1:
                            dve.wait_ge(*seen.next("b_ps"))
                            hw_free(u)
                            nc.vector.tensor_tensor(hw[:, u % RH, :], hs[:, u % 2, :], B[u % 2][:, :], ALU.mult).then_inc(sem["hw_ready"], 1)
                    others(BESIDE1, u, want)
                if units:
                    seen.next("down_done", RH)
                    seen.next("acc_done")

            dve.wait_ge(loaded["small"], 16 * len(small))
            nc.vector.memset(sc0[:], -1.0)
            nc.vector.memset(vaug[:], 1.0).then_inc(const_ready, 1)
            lm = lam[:].rearrange("p (a b) -> p a b", b=2)
            nc.vector.tensor_tensor(lw[:, 0:2], lm[:, :, 0], lm[:, :, 1], ALU.mult).then_inc(coef_in, 1)
            link(nc.vector.memset(coef[:], SCALE1))
            nc.vector.tensor_scalar(g2r[:], g2r[:], 1.0 - LAMBDA_INIT, None, ALU.mult).then_inc(coef_in, 1)
            dve.wait_ge(coef_exp, 1)
            link(nc.vector.tensor_tensor(lw[:, 0:1], lw[:, 2:3], lw[:, 3:4], ALU.subtract))
            join()
            link(nc.vector.tensor_scalar(lw[:, 1:2], lw[:, 0:1], LAMBDA_INIT, -1.0, ALU.add, ALU.mult))
            join()
            link(nc.vector.tensor_scalar(coef[:, HD // 2:HD], coef[:, HD // 2:HD], lw[:, 1:2], None, ALU.mult))
            join()
            pipeline(seen, dve.Fori, f0, f1)


def kernel(**inputs):
    import numpy as _np
    import concourse.bacc as _bacc
    from concourse import mybir as _mybir
    from concourse.bass_utils import run_bass_kernel_spmd as _run

    i = {k: _np.asarray(v) for k, v in inputs.items()}
    f4 = _np.float32
    bf = _mybir.dt.np(BF16) if hasattr(_mybir.dt, "np") else None
    import ml_dtypes
    bf = ml_dtypes.bfloat16

    def tiles(w, n):
        return w.reshape(n, P, D).transpose(1, 0, 2)

    def rows(v):
        return _np.broadcast_to(v.reshape(1, -1), (P, v.size))

    inv_freq = (f4(1.0) / _np.power(f4(10000.0), _np.arange(0, HD, 2, dtype=f4) / f4(HD), dtype=f4)).astype(f4)
    freqs = (_np.arange(L, dtype=f4)[:, None] * inv_freq[None, :]).astype(f4)
    cos, sin = _np.cos(freqs.astype(_np.float64)), _np.sin(freqs.astype(_np.float64))
    cosr = _np.repeat(cos, 2, axis=1)
    sinr = _np.stack([-sin, sin], axis=-1).reshape(L, HD)
    pos = _np.arange(P)
    sel0 = _np.tile((_np.arange(U0 * P)[None, :] // HID0 == _np.arange(E0)[:, None]), (3, 1))
    sel1 = _np.tile((_np.arange(UPB * P)[None, :] // INTER == _np.arange(EB)[:, None]), (3, 1))
    given = {
        "x": i["L0_attn_x"].reshape(NB * L, D),
        "wqkv0": _np.concatenate([i["L0_attn_wq"], i["L0_attn_wk"], i["L0_attn_wv"]], axis=1),
        "wo0": i["L0_attn_wo"],
        "wr0": i["L0_ffn_Wg"].T,
        "w1_0": i["L0_ffn_W1"].reshape(-1, D).T,
        "w3_0": i["L0_ffn_W3"].reshape(-1, D).T,
        "w2_0": tiles(i["L0_ffn_W2"].transpose(0, 2, 1).reshape(-1, D), U0),
        "wqkv1": _np.concatenate([i["L1_attn_Wq"], i["L1_attn_Wk"], i["L1_attn_Wv"]], axis=0).T,
        "wf1": i["L1_attn_W1"].T,
        "wf2": i["L1_attn_W2"].T,
        "wr1": i["L1_ffn_router_w"].T,
        "bias1": rows(i["L1_ffn_expert_bias"]),
        "g1c": i["L1_attn_g1"].reshape(P, 1),
        "g2r": rows(i["L1_attn_g2"]),
        "g3r": rows(i["L1_attn_g3"]),
        "lam": rows(i["L1_attn_lambda_params"]),
        "wg_1": i["L1_ffn_w_gate"].reshape(-1, D).T,
        "wd_1": tiles(i["L1_ffn_w_down"].transpose(0, 2, 1).reshape(-1, D), U1),
        "wgs": i["L1_ffn_w_gate_shared"].T,
        "wds": i["L1_ffn_w_down_shared"].T,
        "ident": _np.eye(P, dtype=f4),
        "identb": _np.eye(P, dtype=bf),
        "cosr": cosr.astype(f4).reshape(T, P, HD).transpose(1, 0, 2),
        "sinr": sinr.astype(f4).reshape(T, P, HD).transpose(1, 0, 2),
        "causal": (pos[:, None] <= pos[None, :]).astype(f4),
        "headm": ((pos[:, None] // HD) % 4 == _np.arange(4)[None, :]).astype(f4),
        "blockd": (pos[:, None] // HD == _np.arange(H * HA)[None, :] // HA).astype(f4),
        "sel0": sel0.astype(bf),
        "sel1": sel1.astype(bf),
    }
    nc = _bacc.Bacc("TRN2", target_bir_lowering=False, num_devices=1)
    arrays, aps = {}, {}
    for name, v in given.items():
        v = _np.ascontiguousarray(v)
        arrays[f"in_{name}"] = v
        aps[name] = nc.dram_tensor(f"in_{name}", v.shape, _mybir.dt.from_np(v.dtype), kind="ExternalInput").ap()
    out = nc.dram_tensor("out_dram", (NB * L, D), F32, kind="ExternalOutput").ap()
    build(nc, aps, out)
    r = _run(nc, [arrays], core_ids=[0])
    return r.results[0]["out_dram"].reshape(NB, L, D)
```

```python
import concourse.bass as bass
from concourse import mybir
from contextlib import ExitStack
import numpy as np

F32 = mybir.dt.float32
BF16 = mybir.dt.bfloat16
I32, U32 = mybir.dt.int32, mybir.dt.uint32
ALU = mybir.AluOpType
ACT = mybir.ActivationFunctionType
AX = mybir.AxisListType

P = 128
D = 128
NB = 8
L = 512
T = L // P
H = 16
HD = D // H
HA = HD + 1
E0, HID0 = 8, 352
U0 = E0 * HID0 // P
E1, INTER = 160, 64
TOPK1 = 8
LAG = 2
RH = 3

TILES = E1 + NB * L * TOPK1 // P
Q = 4
GROUPS = 2 * -(-TILES // (2 * Q * NB))
NG = GROUPS * NB
NJ = NG * Q
JB = -(-NJ // P)
LN_EPS = 1e-5
ATT_EPS = 1e-6
RMS_EPS = float(np.finfo(np.float32).eps)
LAMBDA_INIT = 0.8 - 0.6 * float(np.exp(-0.3 * 0))
SCALE1 = 1.0 / float(np.sqrt(D // 2))

PER_BATCH = dict(
    xn0_ready=1, xn0T_ps=1, xn0T_ready=1, lg0_ps=1, e0_in=1, e0_ready=1, cw0_ready=1, cw0T_ps=1, cw0T_ready=1,
    rot_ready=1, s_rot_ready=1,
    qkv0_ps=T, rope_ready=T, v0_ready=T, qk0_ready=T, qkT0_ps=T, qkT0_ready=T, qm_ready=T, sc_ps=4 * T, at_ready=4 * T,
    av_ps=T, o0_ready=T, state_read=T - 1, state_ready=T - 1, oT_ps=T, oT_ready=T, sT0_ps=1, sT0_ready=1,
    gT0_ready=1, pT0_ready=1, p0_ps=1, x1_ready=1, xn1_ready=1, xn1T_ps=1, xn1T_ready=1, lg1_ps=1,
    lg1a_ready=1, lg1b_ready=1, probs_ready=1, chosen_ready=1, rank_ps=1, ranka_read=1, rankb_read=1, run_ready=1,
    places_ready=1, idx_ready=1,
    g_ps=U0, up_ps=U0, b_ps=U0, silu_ready=U0, hu_ready=U0, hw_ready=U0, down_done=U0 - 1, acc_done=1,
    xg_ready=1, qkv1_ps=T, mn1_ready=T, mx1_ready=T, ex1_ready=T, v1_ready=T, k1_ready=T, prod1_ready=T, a1_ready=T,
    a1T_ps=T, a1T_ready=1, h1_ps=1, gl_ready=1, o1_ps=1, s1_ready=1, sg_ps=1, sg_ready=1, sh_ps=1, sh_ready=1,
    xt_ps=GROUPS, xt_ready=GROUPS, gt_ps=GROUPS, gt_ready=GROUPS, ht_ps=GROUPS, ht_ready=GROUPS, y_ps=GROUPS, y_ready=GROUPS,
    idxc_ready=1, w8_ready=1, sum_ready=1, g1_ready=1, out_ready=1, gathered_used=T,
    rsq_in=3 + 0, rsq_ready=3 + 0, rsq1_in=2 * T, rsq1_ready=2 * T,
    x_loaded=16, xr_loaded=16, x1_stored=16, xn1T_stored=16, pp_stored=16, scattered=16 * T * TOPK1,
    xin_loaded=16, s1_stored=16, sh_stored=16, rows0_loaded=16 * GROUPS // 2,
    rows1_loaded=16 * GROUPS // 2, y_stored=16 * GROUPS,
    ppf_loaded=16, x1f_loaded=16, s1f_loaded=16, shf_loaded=16, gath0=16 * TOPK1 * T // 2, gath1=16 * TOPK1 * T // 2,
    out_stored=16,
    dve_link=0, dve_link2=0, dve_link3=0, pool_link=1, pool_link3=T,
)
LINKS = dict(dve_link=105, dve_link2=41, dve_link3=42)


class Seen:

    def __init__(self, sems):
        self.sems, self.count, self.reg, self.first = sems, {n: 0 for n in sems}, None, 0
        self.readers = {}

    def value(self, name, count):
        if self.reg is None:
            return count
        return (self.reg - self.first) * self.sems[name][1] + count

    def next(self, name, by=1):
        self.count[name] += by
        for names in self.readers.values():
            if name in names:
                names.remove(name)
        return self.sems[name][0], self.value(name, self.count[name])

    def lag(self, name, by):
        c = self.count[name] + 1 - by
        return None if c <= 0 and self.reg is None else (self.sems[name][0], self.value(name, c))

    def bank(self, bank):
        return [self.next(n) for n in list(self.readers.pop(bank, []))]

    def loop(self, reg, first):
        self.reg, self.first, self.entry = reg, first, dict(self.count)

    def loop_end(self, trips):
        for n, (_, per) in self.sems.items():
            got = self.count[n] - self.entry[n]
            assert got in (0, per), f"{n}: {got} events in the loop's body, {per} declared"
            self.count[n] += got * (trips - 1)
        self.reg = None


STEPS = {0: ["res_silu"], 1: ["res_gate"], 3: ["res_T"], 4: ["res_add"], 6: ["res_norm"], 9: ["xn1_T", "res_r1"],
         10: ["xn1T_copy"], 11: ["norm0a"], 12: ["router1"], 13: ["probs1"], 14: ["norm0b"], 15: ["topk1a"],
         16: ["xn0_T"], 17: ["xn0T_copy"], 18: ["topk1b", "router0"], 19: ["exp0"], 21: ["rank"], 22: ["topk0a"],
         23: ["place_a"], 24: ["topk0b"], 26: ["place_b"], 28: ["place_c"], 29: ["cw0_T", "scatter"],
         30: ["cw0T_copy"], 86: ["wo"], 87: ["s0"]}
for t in range(T):
    for at, name in ((0, "qkv0"), (1, "rope"), (3, "qk_T"), (4, "qkT_copy"), (6, "scores_a"), (7, "mask_a"),
                     (9, "scores_b"), (10, "mask_b"), (11, "av"), (12, "o_norm"), (14, "o_T"), (14, "oT_copy")):
        STEPS.setdefault(31 + 13 * t + at, []).append((name, t))
RES = {"res_silu", "res_gate", "res_T", "res_add", "res_norm", "res_r1", "xn1_T", "xn1T_copy", "router1", "probs1",
       "topk1a", "topk1b", "rank", "place_a", "place_b", "place_c", "scatter"}
STEPS1 = {0: [("a1_T", T - 1), "a1T_copy"], 1: ["ffh1", "gelu1", "xg"], 2: ["ffo1", "s1"], 3: ["shared_up"],
          4: ["shared_down"]}
for t in range(T):
    if t:
        STEPS1.setdefault(3 * t + 1, []).append(("mix1c", t - 1))
        STEPS1.setdefault(3 * t + 2, []).append(("a1_T", t - 1))
    for at, name in ((1, "qkv1"), (1, "elu1"), (2, "mix1a"), (3, "mix1b")):
        STEPS1.setdefault(3 * t + at, []).append((name, t))
STEPS1[GROUPS - 1] = [("mix1c", T - 1)]
LATE = {("a1_T", T - 1), ("a1T_copy", 0), ("ffh1", 0), ("gelu1", 0), ("ffo1", 0), ("s1", 0)}


def beside(table, u, want):
    for s in table.get(u, []):
        name, t = s if isinstance(s, tuple) else (s, 0)
        if ("res" if name in RES else "late" if (name, t) in LATE else "pre") in want:
            yield name, t


def build(nc, a, out):
    ctx = ExitStack()
    with ctx:
        def sb(name, shape, dt=F32):
            return ctx.enter_context(nc.sbuf_tensor(name, shape, dt))

        def dram(name, shape, dt=F32):
            return nc.dram_tensor(name, shape, dt, kind="Internal").ap()

        w1_0, w3_0 = sb("w1_0", [P, U0 * P]), sb("w3_0", [P, U0 * P])
        w2_0 = sb("w2_0", [P, U0, D])
        wg_1 = sb("wg_1", [P, E1 * INTER])
        wd_1 = sb("wd_1", [P, E1 // 2 * D])
        wgs, wds = sb("wgs", [P, INTER]), sb("wds", [INTER, D])
        wqkv0, wo0, wr0 = sb("wqkv0", [P, 3 * D]), sb("wo0", [P, D]), sb("wr0", [P, E0])
        wqkv1, wf1, wf2, wr1 = sb("wqkv1", [P, 3 * D]), sb("wf1", [P, D]), sb("wf2", [P, D]), sb("wr1", [P, E1])
        bias1, g1c, g2r, g3r, lam = sb("bias1", [P, E1]), sb("g1c", [P, 1]), sb("g2r", [P, HD]), sb("g3r", [P, D]), sb("lam", [P, 4])
        ident, identb = sb("ident", [P, P]), sb("identb", [P, P], BF16)
        before, onesb = sb("before", [P, P], BF16), sb("onesb", [P, P], BF16)
        cosr, sinr = sb("cosr", [P, T, HD]), sb("sinr", [P, T, HD])
        causal, headm, blockd = sb("causal", [P, P]), sb("headm", [P, 4]), sb("blockd", [P, H * HA])
        sel0 = sb("sel0", [3 * E0, U0 * P], BF16)
        jcol, hid = sb("jcol", [P, JB]), sb("hid", [P, 1])
        neg_half, pause, ppause = sb("neg_half", [P, H]), sb("pause", [P, 1]), sb("ppause", [P, 1])
        xs, xn0, xn0Tn, xn0T = sb("xs", [P, T, D]), sb("xn0", [P, T, D]), sb("xn0Tn", [P, L]), sb("xn0T", [P, L])
        st, mv, rs = sb("st", [P, T, 6]), sb("mv", [P, T, 2]), sb("rs", [P, T])
        mx0, l0, e0, sm0 = sb("mx0", [P, T]), sb("l0", [P, T, E0]), sb("e0", [P, T, E0]), sb("sm0", [P, T])
        sc0, m80, sr0 = sb("sc0", [P, T, 14]), sb("m80", [P, T, 8]), sb("sr0", [P, T, 14])
        cwf0, cwr0, cwp0 = sb("cwf0", [P, T, E0]), sb("cwr0", [P, T, E0]), sb("cwp0", [P, T, 3, E0], BF16)
        cw0Tn, cw0T = sb("cw0Tn", [3 * E0, L], BF16), sb("cw0T", [3 * E0, L], BF16)
        rA, rB, rr, qk, vaug = sb("rA", [P, 2 * D]), sb("rB", [P, 2 * D]), sb("rr", [P, 2 * D]), sb("qk", [P, 2 * D]), sb("vaug", [P, H, HA])
        qkT, qm, att = sb("qkT", [P, 2 * P]), sb("qm", [P, 4, P]), sb("att", [P, 4, 4 * P])
        attf = att[:].rearrange("p g c -> p (g c)")
        dn, rc, o0, oT = sb("dn", [P, H]), sb("rc", [P, H]), sb("o0", [P, H, HD]), sb("oT", [P, L])
        state, stmp = sb("state", [P, H * HA]), sb("stmp", [P, H * HA])
        sT0n, sT0, gT, pT = sb("sT0n", [P, L]), sb("sT0", [P, L]), sb("gT", [P, L]), sb("pT", [P, L])
        hs, hw = sb("hs", [P, 2, L]), sb("hw", [P, RH, L])
        xr, x1n, xn1, xn1Tn = sb("xr", [P, T, D]), sb("x1n", [P, T, D]), sb("xn1", [P, T, D]), sb("xn1Tn", [P, L])
        ms1, r1, r1all, s8, s8all = sb("ms1", [P, T]), sb("r1", [P, T]), sb("r1all", [P, NB, T]), sb("s8", [P, T]), sb("s8all", [P, NB, T])
        pp = sb("pp", [P, 2, T, E1])
        place, pr = pp[:, 0, :, :], pp[:, 1, :, :]
        m8, p8 = sb("m8", [P, T, 8]), sb("p8", [P, T, 8])
        idxy = sb("idxy", [P, NB + 1, T * 8], U32)
        idx = sb("idx", [P, T * 8], U32)
        pr2 = attf[:, 0:T * E1].rearrange("p (t e) -> p t e", t=T)
        chosen = attf[:, T * E1:T * E1 * 3 // 2].bitcast(BF16).rearrange("p (t e) -> p t e", t=T)
        run, runn = sb("run", [P, E1]), sb("runn", [P, E1])
        pages, pagesn, new = sb("pages", [P, E1]), sb("pagesn", [P, E1]), sb("new", [P, E1])
        pagesi, ones1 = sb("pagesi", [P, E1], I32), sb("ones1", [P, E1])
        given = sb("given", [P, E1])
        shift, shiftn, dshift = sb("shift", [P, E1]), sb("shiftn", [P, E1]), sb("dshift", [P, E1])
        limit, base, scr = sb("limit", [P, E1]), sb("base", [P, E1]), sb("scr", [P, E1])
        cj, ej, hj, parj = sb("cj", [P, JB]), sb("ej", [P, JB]), sb("hj", [P, JB]), sb("parj", [P, JB])
        hji, tabi = sb("hji", [P, JB], I32), sb("tabi", [P, 2, JB], I32)
        half_of = qm[:].rearrange("p a b -> p (a b)")
        tabs = hw[0:1, 0:2, :].bitcast(I32)
        xin, xgT, r1c = sb("xin", [P, L]), xn0, sb("r1c", [P, T])
        xgT = xn0[:].rearrange("p t d -> p (t d)")
        coef, lw = sb("coef", [P, HD]), sb("lw", [P, 4])
        mn1, mxq1, ex1, qk1, v1, qc1 = rA, rB, rr, qk, sb("v1", [P, D]), sb("qc1", [P, D])
        prodA = attf[:, 0:HD * D].rearrange("p (e d h) -> p e d h", e=HD, d=HD)
        prodB = attf[:, HD * D:2 * HD * D].rearrange("p (h d e) -> p h d e", h=H, d=HD)
        kv1, at1, sq1, ss1, rd1, a1 = sb("kv1", [P, HD, HD]), sb("at1", [P, H, HD]), sb("sq1", [P, H, HD]), sb("ss1", [P, H]), sb("rd1", [P, 1]), sb("a1", [P, H, HD])
        a1b, a1T, gl, s1b, sg, shb = xn1, oT, sT0, x1n, pT, xr
        idxc = idx
        xg = w1_0[:, 0:2 * Q * D].rearrange("p (r q d) -> p r q d", r=2, q=Q)
        h1d = w1_0[:, 2 * Q * D:3 * Q * D].rearrange("p (q s i) -> p q s i", q=Q, s=2)
        xgTt, hT, ys = xn0T, xn0Tn, hs
        y8 = att[:].rearrange("p g c -> p (g c)").rearrange("p (r k d) -> p r k d", r=2, k=8)
        w8, acc, g1, outs = sb("w8", [P, T, 8]), xs, gT, xn1
        terms = wg_1[:, 0:T * TOPK1 * E1].rearrange("p (k e) -> p k e", e=E1)
        x1f, s1f, shf = w3_0[:, 0:T * D].rearrange("p (t d) -> p t d", t=T), x1n, xr

        rows = dram("rows", (NJ * P, D))
        y_d = dram("y_rows", (NG * Q * P, D))
        tab_d = dram("tile_table", (2, JB * P), I32)
        x1_d, s1_d, sh_d = dram("x1_d", (NB, P, T, D)), dram("s1_d", (NB, P, T, D)), dram("sh_d", (NB, P, T, D))
        xn1T_d, pp_d = dram("xn1T_d", (NB, P, L)), dram("pp_d", (NB, P, 2, T, E1))

        ps = {n: ctx.enter_context(nc.psum_tensor(n, [P, 512], F32)) for n in ("G0", "G1", "B", "V", "ACC", "U", "X0", "X1")}
        G, B, V = [ps["G0"], ps["G1"]], ps["B"], ps["V"]
        ACC, U, X0, X1 = ps["ACC"], ps["U"], ps["X0"], ps["X1"]

        sems = {n: (ctx.enter_context(nc.semaphore(n)), LINKS.get(n, per)) for n, per in PER_BATCH.items()}
        sem = {n: s for n, (s, _) in sems.items()}
        loaded = {n: ctx.enter_context(nc.semaphore(f"{n}_loaded")) for n in ("small", "f0", "w1", "zeros", "tab")}
        once = {n: ctx.enter_context(nc.semaphore(n)) for n in ("const_ready", "zero_ready", "coef_in", "coef_exp", "half_in", "half_ps",
                                                                "tab_ready", "tab_out", "half_ready", "phase2", "yst0", "yst1", "neg_ready")}

        small = [(wqkv0, "wqkv0"), (wr0, "wr0"), (ident, "ident"), (identb, "identb"), (cosr, "cosr"), (sinr, "sinr"),
                 (causal, "causal"), (headm, "headm"), (blockd, "blockd"), (wo0, "wo0"), (sel0, "sel0"),
                 (wqkv1, "wqkv1"), (wf1, "wf1"), (wf2, "wf2"), (wr1, "wr1"), (bias1, "bias1"), (g1c, "g1c"),
                 (g2r, "g2r"), (g3r, "g3r"), (lam, "lam"), (before, "before"), (onesb, "onesb"), (jcol, "jcol"), (hid, "hid")]
        x_v = a["x"].rearrange("(b t p) d -> b p t d", b=NB, p=P)
        out_v = out.rearrange("(b t p) d -> b p t d", b=NB, p=P)

        block = ctx.enter_context(nc.Block())

        def layer0(seen, fori, f0):
            f0(-1, False, {"pre"})
            f0(0, True, {"pre"})
            f0(1, True, {"res", "pre"})
            f0(2, True, {"res", "pre"})
            with fori(3, NB - 1) as g:
                seen.loop(g, 3)
                f0(g, True, {"res", "pre"})
                seen.loop_end(NB - 4)
            f0(NB - 1, True, {"res"})
            f0(NB, False, {"res"})

        def per_batch(seen, fori, f, first=0):
            f(0)
            with fori(1, NB) as b:
                seen.loop(b, 1)
                f(b)
                seen.loop_end(NB - 1)

        def now(b):
            return {"pre"} if isinstance(b, int) and b == 0 else {"late", "pre"}

        def done(eng, name, n):
            if not (isinstance(n, int) and n < 0):
                eng.wait_ge(sem[name], n + 1)

        def settled(eng, seen, name, by=1):
            if seen.count[name]:
                eng.wait_ge(sem[name], seen.value(name, seen.count[name]))
            seen.next(name, by)

        @block.sync
        def _(sp):
            seen = Seen(sems)

            def load(dst, src, name):
                sp.dma_start(dst, src).then_inc(sem[name], 16)

            load(xs[:], x_v[0], "x_loaded")
            load(xr[:], x_v[0], "xr_loaded")
            for t, n in small:
                sp.dma_start(t[:], a[n]).then_inc(loaded["small"], 16)
            for t, n in ((w1_0, "w1_0"), (w3_0, "w3_0"), (w2_0, "w2_0")):
                sp.dma_start(t[:], a[n]).then_inc(loaded["f0"], 16)
            sp.wait_ge(once["zero_ready"], 1)
            sp.dma_start(rows.rearrange("(p j r) d -> p j (r d)", p=P, r=T), x1n[:].rearrange("p t d -> p (t d)").unsqueeze(1).broadcast_to([P, NJ // T, L]))\
                .then_inc(loaded["zeros"], 16)
            for t, n in ((wg_1, "wg_1"), (wd_1, "wd_1"), (wgs, "wgs"), (wds, "wds")):
                sp.dma_start(t[:], a[n]).then_inc(loaded["w1"], 16)

            def f0(b, units, want, more_x=True):
                if "res" in want:
                    sp.wait_ge(*seen.next("x1_ready"))
                    load(x1_d[b - 1], x1n[:], "x1_stored")
                    if not (isinstance(b, int) and b >= NB):
                        load(xr[:], x_v[b], "xr_loaded")
                if "pre" in want:
                    sp.wait_ge(*seen.next("xn0_ready"))
                    if more_x:
                        load(xs[:], x_v[b + 2], "x_loaded")
                if "res" in want:
                    sp.wait_ge(*seen.next("xn1T_ready"))
                    load(xn1T_d[b - 1], xn1Tn[:], "xn1T_stored")
                    sp.wait_ge(*seen.next("places_ready"))
                    load(pp_d[b - 1], pp[:], "pp_stored")

            f0(-1, False, {"pre"})
            f0(0, True, {"pre"})
            f0(1, True, {"res", "pre"})
            f0(2, True, {"res", "pre"})
            with sp.Fori(3, NB - 2) as g:
                seen.loop(g, 3)
                f0(g, True, {"res", "pre"})
                seen.loop_end(NB - 5)
            f0(NB - 2, True, {"res", "pre"}, more_x=False)
            f0(NB - 1, True, {"res"})
            f0(NB, False, {"res"})

            sp.wait_ge(once["tab_ready"], 1)
            sp.dma_start(tab_d.rearrange("f (k p) -> p f k", p=P), tabi[:], allow_slow_non_contiguous=True).then_inc(once["tab_out"], 16)
            sp.wait_ge(once["tab_out"], 16)
            sp.dma_start(tabs, tab_d.rearrange("f (o j) -> o f j", o=1)).then_inc(loaded["tab"], 16)
            sp.wait_ge(loaded["tab"], 16)
            sp.wait_ge(sem["scattered"], 16 * T * TOPK1 * NB)
            sp.wait_ge(loaded["zeros"], 16)
            sp.wait_ge(sem["x1_stored"], 16 * NB)
            sp.wait_ge(sem["xn1T_stored"], 16 * NB)
            sp.wait_ge(sem["pp_stored"], 16 * NB)

            rows_v = rows.rearrange("(g q p) d -> g p q d", q=Q, p=P)

            def load_rows(n, par):
                done(sp, "xt_ps", n - 2)
                load(xg[:, par, :, :], rows_v[n], f"rows{par}_loaded")

            y_v = y_d.rearrange("(g q p) d -> g p q d", q=Q, p=P)

            def store_y(n, par):
                done(sp, "y_ready", n)
                sp.dma_start(y_v[n], ys[:, par, :].rearrange("p (q d) -> p q d", q=Q)).then_inc(once[f"yst{par}"], 16)

            LAGY = 5

            def layer1(b):
                for u in range(GROUPS):
                    n = b * GROUPS + u
                    if u == 0:
                        settled(sp, seen, "xg_ready")
                        settled(sp, seen, "sg_ps")
                        load(xin[:], xn1T_d[b], "xin_loaded")
                    load_rows(n, u % 2)
                    if not (isinstance(b, int) and n < LAGY):
                        store_y(n - LAGY, (u - LAGY) % 2)
                    if u == 6:
                        sp.wait_ge(*seen.next("sh_ready"))
                        load(sh_d[b], shb[:], "sh_stored")
                    if u == 4 and "late" in now(b):
                        sp.wait_ge(*seen.next("s1_ready"))
                        load(s1_d[b - 1], s1b[:], "s1_stored")

            per_batch(seen, sp.Fori, layer1)
            for n in range(NG - LAGY, NG):
                store_y(n, n % 2)
            sp.wait_ge(*seen.next("s1_ready"))
            load(s1_d[NB - 1], s1b[:], "s1_stored")
            sp.wait_ge(sem["s1_stored"], 16 * NB)
            sp.wait_ge(sem["sh_stored"], 16 * NB)

            def end(b):
                load(pp[:], pp_d[b], "ppf_loaded")
                load(x1f[:], x1_d[b], "x1f_loaded")
                load(s1f[:], s1_d[b], "s1f_loaded")
                load(shf[:], sh_d[b], "shf_loaded")
                sp.wait_ge(*seen.next("out_ready"))
                load(out_v[b], outs[:], "out_stored")

            per_batch(seen, sp.Fori, end)
            sp.wait_ge(sem["out_stored"], 16 * NB)

        @block.tensor
        def _(pe):
            seen = Seen(sems)

            def reuse(bank):
                for s, v in seen.bank(bank):
                    pe.wait_ge(s, v)

            def transposes(bank, src, name):
                for t in range(T):
                    last = nc.tensor.transpose(ps[bank][:, t * P:(t + 1) * P], src(t), ident[:])
                last.then_inc(sem[name], 1)

            def s_xn0_T(t):
                pe.wait_ge(*seen.next("xn0_ready"))
                reuse("X0")
                transposes("X0", lambda t: xn0[:, t, :], "xn0T_ps")
                seen.readers["X0"] = ["xn0T_ready"]

            def s_router0(t):
                pe.wait_ge(*seen.next("xn0T_ready"))
                reuse("X1")
                for t in range(T):
                    last = nc.tensor.matmul(X1[:, t * E0:(t + 1) * E0], xn0Tn[:, t * P:(t + 1) * P], wr0[:], start=True, stop=True)
                last.then_inc(sem["lg0_ps"], 1)
                seen.readers["X1"] = ["e0_in"]

            def s_cw0_T(t):
                pe.wait_ge(*seen.next("cw0_ready"))
                reuse("X1")
                xb = X1[:, :].bitcast(BF16)
                for t in range(T):
                    last = nc.tensor.transpose(xb[0:3 * E0, t * P:(t + 1) * P],
                                               cwp0[:, t, :, :].rearrange("p a e -> p (a e)"), identb[:])
                last.then_inc(sem["cw0T_ps"], 1)
                seen.readers["X1"] = ["cw0T_ready"]

            def s_qkv0(t):
                reuse("X0")
                nc.tensor.matmul(X0[:, 0:3 * D], xn0Tn[:, t * P:(t + 1) * P], wqkv0[:], start=True, stop=True)\
                    .then_inc(sem["qkv0_ps"], 1)
                seen.readers["X0"] = ["rope_ready", "v0_ready"]

            def s_qk_T(t):
                pe.wait_ge(*seen.next("qk0_ready"))
                reuse("X1")
                nc.tensor.transpose(X1[:, 0:P], qk[:, 0:D], ident[:])
                nc.tensor.transpose(X1[:, P:2 * P], qk[:, D:2 * D], ident[:]).then_inc(sem["qkT0_ps"], 1)
                seen.readers["X1"] = ["qkT0_ready", "qm_ready"]

            def score(g, bank):
                reuse(bank)
                nc.tensor.matmul(ps[bank][:, :], qkT[32 * g:32 * g + 32, P:2 * P], qm[32 * g:32 * g + 32, :, :],
                                 start=True, stop=True).then_inc(sem["sc_ps"], 1)
                seen.readers[bank] = ["at_ready"]

            def s_scores_a(t):
                pe.wait_ge(*seen.next("qkT0_ready"))
                pe.wait_ge(*seen.next("qm_ready"))
                if t:
                    pe.wait_ge(*seen.next("state_ready"))
                    reuse("V")
                    nc.tensor.matmul(V[:, 0:H * HA], qkT[:, 0:P], state[:], start=True, stop=False, skip_group_check=True)
                score(0, "X0")
                score(1, "X1")

            def s_scores_b(t):
                pe.wait_ge(*seen.next("at_ready"))
                score_now(2, "X0")
                pe.wait_ge(*seen.next("at_ready"))
                score_now(3, "X1")

            def score_now(g, bank):
                nc.tensor.matmul(ps[bank][:, :], qkT[32 * g:32 * g + 32, P:2 * P], qm[32 * g:32 * g + 32, :, :],
                                 start=True, stop=True).then_inc(sem["sc_ps"], 1)
                seen.readers[bank] = []

            def s_av(t):
                pe.wait_ge(*seen.next("at_ready", 2))
                reuse("V")
                if t < T - 1:
                    nc.tensor.matmul(X0[:, 0:H * HA], qk[:, D:2 * D], vaug[:].rearrange("p h m -> p (h m)"), start=True, stop=True)
                    seen.readers["X0"] = ["state_read"]
                for h in range(H):
                    last = nc.tensor.matmul(V[:, h * HA:(h + 1) * HA], att[:, h // 4, (h % 4) * P:(h % 4 + 1) * P], vaug[:, h, :],
                                            start=(t == 0 and h == 0), stop=(h == H - 1), skip_group_check=True)
                last.then_inc(sem["av_ps"], 1)
                seen.readers["V"] = ["o0_ready"]

            def s_o_T(t):
                pe.wait_ge(*seen.next("o0_ready"))
                reuse("X1")
                nc.tensor.transpose(X1[:, 0:P], o0[:].rearrange("p h m -> p (h m)"), ident[:]).then_inc(sem["oT_ps"], 1)
                seen.readers["X1"] = ["oT_ready"]

            def s_wo(t):
                pe.wait_ge(*seen.next("oT_ready"))
                reuse("X0")
                nc.tensor.matmul(X0[:, :], wo0[:], oT[:], start=True, stop=True).then_inc(sem["sT0_ps"], 1)
                seen.readers["X0"] = ["sT0_ready"]

            def s_res_T(t):
                pe.wait_ge(*seen.next("pT0_ready"))
                reuse("X0")
                transposes("X0", lambda t: pT[:, t * P:(t + 1) * P], "p0_ps")
                seen.readers["X0"] = ["x1_ready"]

            def s_xn1_T(t):
                pe.wait_ge(*seen.next("xn1_ready"))
                reuse("X1")
                transposes("X1", lambda t: xn1[:, t, :], "xn1T_ps")
                seen.readers["X1"] = ["xn1T_ready"]

            def s_router1(t):
                pe.wait_ge(*seen.next("xn1T_ready"))
                reuse("X0")
                reuse("V")
                for t in range(T):
                    bank = (X0, V)[t // 2]
                    last = nc.tensor.matmul(bank[:, (t % 2) * E1:(t % 2 + 1) * E1], xn1Tn[:, t * P:(t + 1) * P], wr1[:],
                                            start=True, stop=True)
                last.then_inc(sem["lg1_ps"], 1)
                seen.readers["X0"], seen.readers["V"] = ["lg1a_ready"], ["lg1b_ready"]

            def s_rank(t):
                pe.wait_ge(*seen.next("chosen_ready"))
                for bank in ("X0", "X1", "V"):
                    reuse(bank)
                for t in range(T):
                    o = (X0, X1)[t // 2][:, (t % 2) * E1:(t % 2 + 1) * E1]
                    nc.tensor.matmul(o, before[:], chosen[:, t, :], start=True, stop=(t == 0))
                    for s in range(t):
                        nc.tensor.matmul(o, onesb[:], chosen[:, s, :], start=False, stop=(s == t - 1))
                for t in range(T):
                    last = nc.tensor.matmul(V[:, 0:E1], onesb[:], chosen[:, t, :], start=(t == 0), stop=(t == T - 1))
                last.then_inc(sem["rank_ps"], 1)
                seen.readers["X0"], seen.readers["X1"], seen.readers["V"] = ["ranka_read"], ["rankb_read"], ["run_ready"]

            def s_qkv1(t):
                reuse("X0")
                nc.tensor.matmul(X0[:, 0:3 * D], xgT[:, t * P:(t + 1) * P], wqkv1[:], start=True, stop=True)\
                    .then_inc(sem["qkv1_ps"], 1)
                seen.readers["X0"] = ["mn1_ready", "mx1_ready", "v1_ready"]

            def s_a1_T(t):
                pe.wait_ge(*seen.next("a1_ready"))
                if t == 0:
                    reuse("X1")
                nc.tensor.transpose(X1[:, t * P:(t + 1) * P], a1b[:, t, :], ident[:]).then_inc(sem["a1T_ps"], 1)
                seen.readers["X1"] = ["a1T_ready"] if t == T - 1 else []

            def s_xg(t):
                pe.wait_ge(*seen.next("xg_ready"))

            def s_shared_up(t):
                reuse("U")
                nc.tensor.matmul(U[0:INTER, :], wgs[:], xin[:], start=True, stop=True).then_inc(sem["sg_ps"], 1)
                seen.readers["U"] = ["sg_ready"]

            def s_shared_down(t):
                pe.wait_ge(*seen.next("sg_ready"))
                reuse("X1")
                for t in range(T):
                    last = nc.tensor.matmul(X1[:, t * P:(t + 1) * P], sg[0:INTER, t * P:(t + 1) * P], wds[:], start=True, stop=True)
                last.then_inc(sem["sh_ps"], 1)
                seen.readers["X1"] = ["sh_ready"]

            def s_ffh1(t):
                pe.wait_ge(*seen.next("a1T_ready"))
                reuse("U")
                nc.tensor.matmul(U[:, :], wf1[:], a1T[:], start=True, stop=True).then_inc(sem["h1_ps"], 1)
                seen.readers["U"] = ["gl_ready"]

            def s_ffo1(t):
                pe.wait_ge(*seen.next("gl_ready"))
                reuse("X0")
                for t in range(T):
                    last = nc.tensor.matmul(X0[:, t * P:(t + 1) * P], gl[:, t * P:(t + 1) * P], wf2[:], start=True, stop=True)
                last.then_inc(sem["o1_ps"], 1)
                seen.readers["X0"] = ["s1_ready"]

            steps = {n[2:]: f for n, f in locals().items() if n.startswith("s_")}

            def others(table, u, want):
                for name, t in beside(table, u, want):
                    if name in steps:
                        steps[name](t)

            def f0(b, units, want):
                if isinstance(b, int) and b == 0:
                    pe.wait_ge(loaded["f0"], 48)
                if units:
                    pe.wait_ge(*seen.next("rot_ready"))
                for s in range(4 * (U0 + LAG)):
                    u, part = divmod(s, 4)
                    if units and u < U0 and part == 0:
                        free = seen.lag("g_ps", 2)
                        if free:
                            pe.wait_ge(sem["silu_ready"], free[1])
                        nc.tensor.matmul(G[u % 2][:, :], w1_0[:, u * P:(u + 1) * P], xn0T[:], start=True, stop=True).then_inc(sem["g_ps"], 1)
                        seen.next("g_ps")
                    if units and u < U0 and part == 1:
                        free = seen.lag("up_ps", 1)
                        if free:
                            pe.wait_ge(sem["hu_ready"], free[1])
                        nc.tensor.matmul(U[:, :], w3_0[:, u * P:(u + 1) * P], xn0T[:], start=True, stop=True).then_inc(sem["up_ps"], 1)
                        seen.next("up_ps")
                    if units and u < U0 and part == 2:
                        free = seen.lag("b_ps", 1)
                        if free:
                            pe.wait_ge(sem["hw_ready"], free[1])
                        nc.tensor.matmul(B[:, :], sel0[:, u * P:(u + 1) * P], cw0T[:], start=True, stop=True).then_inc(sem["b_ps"], 1)
                        seen.next("b_ps")
                    if units and u >= LAG and part == 3:
                        v = u - LAG
                        if v == 0:
                            reuse("ACC")
                        pe.wait_ge(*seen.next("hw_ready"))
                        nc.tensor.matmul(ACC[:, :], w2_0[:, v, :], hw[:, v % RH, :], start=(v == 0), stop=(v == U0 - 1))\
                            .then_inc(sem["acc_done" if v == U0 - 1 else "down_done"], 1)
                    others(STEPS, s, want)
                if units:
                    seen.readers["ACC"] = ["gT0_ready"]

            pe.wait_ge(loaded["small"], 16 * len(small))
            pe.wait_ge(once["const_ready"], 1)
            layer0(seen, pe.Fori, f0)

            pe.wait_ge(once["half_in"], 1)
            for bank in ("X0", "X1", "V"):
                reuse(bank)
            for k in range(JB):
                last = nc.tensor.matmul(X0[:, k * P:(k + 1) * P], parj[:, k:k + 1].broadcast_to([P, P]), ident[:], start=True, stop=True)
            last.then_inc(once["half_ps"], 1)
            pe.wait_ge(once["half_ready"], 1)
            pe.wait_ge(loaded["w1"], 64)
            pe.wait_ge(loaded["tab"], 16)
            pe.wait_ge(once["phase2"], 1)

            def columns(field, n, high):
                _, at = nc.values_load_multi_w_load_instructions(
                    tabs[0:1, field, bass.ds(n * Q, Q)], engines=[mybir.EngineType.PE], min_val=0, max_val=high,
                    skip_runtime_bounds_check_because="the table's experts are held below E1")
                return at

            def group(n, b, u, stages):
                def has(k):
                    return k in stages and not (isinstance(b, int) and b == 0 and u < k)
                if has(0):
                    pe.wait_ge(sem[f"rows{u % 2}_loaded"], (b * (GROUPS // 2) + u // 2 + 1) * 16)
                    done(pe, "xt_ready", n - 1)
                    for q in range(Q):
                        last = nc.tensor.transpose(G[0][:, q * P:(q + 1) * P], xg[:, u % 2, q, :], ident[:])
                    last.then_inc(sem["xt_ps"], 1)
                if has(1):
                    done(pe, "xt_ready", n - 1)
                    done(pe, "gt_ready", n - 2)
                    at = columns(0, n - 1, (E1 - 1) * INTER)
                    for q in range(Q):
                        last = nc.tensor.matmul(B[:, q * INTER:(q + 1) * INTER], xgTt[:, q * P:(q + 1) * P],
                                                wg_1[:, bass.ds(at[q], INTER)], start=True, stop=True)
                    last.then_inc(sem["gt_ps"], 1)
                if has(2):
                    done(pe, "gt_ready", n - 2)
                    done(pe, "ht_ready", n - 3)
                    for q in range(Q):
                        last = nc.tensor.transpose(V[:, q * P:(q + 1) * P], h1d[:, q, :, :].rearrange("p a i -> p (a i)"), ident[:])
                    last.then_inc(sem["ht_ps"], 1)
                if has(3):
                    done(pe, "ht_ready", n - 3)
                    done(pe, "y_ready", n - 4)
                    at = columns(1, n - 3, (E1 // 2 - 1) * D)
                    for q in range(Q):
                        last = nc.tensor.matmul(ACC[:, q * P:(q + 1) * P], hT[:, q * P:(q + 1) * P],
                                                wd_1[:, bass.ds(at[q], D)], start=True, stop=True)
                    last.then_inc(sem["y_ps"], 1)

            def layer1(b):
                for u in range(GROUPS):
                    group(b * GROUPS + u, b, u, {0, 1, 2, 3})
                    others(STEPS1, u, now(b))

            per_batch(seen, pe.Fori, layer1)
            for k in range(1, 4):
                group(NG - 1 + k, NB, 10 ** 6, set(range(k, 4)))
            for u in range(GROUPS):
                others(STEPS1, u, {"late"})

        @block.scalar
        def _(act):
            seen = Seen(sems)

            def copy(dst, src, after, name):
                if after:
                    act.wait_ge(*seen.next(after))
                nc.scalar.activation(dst, src, ACT.Copy).then_inc(sem[name], 1)

            def s_xn0T_copy(t):
                settled(act, seen, "rot_ready")
                copy(xn0Tn[:], X0[:, :], "xn0T_ps", "xn0T_ready")

            def s_exp0(t):
                act.wait_ge(*seen.next("e0_in"))
                nc.scalar.activation(e0[:], l0[:], ACT.Exp).then_inc(sem["e0_ready"], 1)

            def s_cw0T_copy(t):
                copy(cw0Tn[:], X1[:, :].bitcast(BF16)[0:3 * E0, 0:L], "cw0T_ps", "cw0T_ready")

            def s_rope(t):
                act.wait_ge(*seen.next("rope_ready"))
                nc.scalar.activation(qk[:], rr[:], ACT.Relu).then_inc(sem["qk0_ready"], 1)
                copy(vaug[:, :, 0:HD], X0[:, 2 * D:3 * D].rearrange("p (h m) -> p h m", h=H), None, "v0_ready")

            def s_qkT_copy(t):
                copy(qkT[:], X1[:, 0:2 * P], "qkT0_ps", "qkT0_ready")

            def s_oT_copy(t):
                copy(oT[:, t * P:(t + 1) * P], X1[:, 0:P], "oT_ps", "oT_ready")

            def s_s0(t):
                settled(act, seen, "s_rot_ready")
                copy(sT0n[:], X0[:, :], "sT0_ps", "sT0_ready")

            def s_res_silu(t):
                act.wait_ge(*seen.next("acc_done"))
                nc.scalar.activation(gT[:], ACC[:, :], ACT.Silu).then_inc(sem["gT0_ready"], 1)

            def s_xn1T_copy(t):
                settled(act, seen, "xn1T_stored", 16)
                copy(xn1Tn[:], X1[:, :], "xn1T_ps", "xn1T_ready")

            def s_probs1(t):
                act.wait_ge(*seen.next("lg1a_ready"))
                act.wait_ge(*seen.next("lg1b_ready"))
                nc.scalar.activation(pr, place, ACT.Sigmoid).then_inc(sem["probs_ready"], 1)

            def s_elu1(t):
                act.wait_ge(*seen.next("mx1_ready"))
                nc.scalar.activation(v1[:], X0[:, 2 * D:3 * D], ACT.Copy, scale=r1c[:, t:t + 1]).then_inc(sem["v1_ready"], 1)
                act.wait_ge(*seen.next("mn1_ready"))
                nc.scalar.activation(ex1[:], mn1[:], ACT.Exp).then_inc(sem["ex1_ready"], 1)

            def s_shared_up(t):
                act.wait_ge(*seen.next("sg_ps"))
                nc.scalar.activation(sg[0:INTER, :], U[0:INTER, :], ACT.Silu).then_inc(sem["sg_ready"], 1)

            def s_shared_down(t):
                act.wait_ge(*seen.next("sh_ps"))
                settled(act, seen, "sh_stored", 16)
                nc.scalar.activation(shb[:], X1[:, :].rearrange("p (t d) -> p t d", t=T), ACT.Copy).then_inc(sem["sh_ready"], 1)

            def s_a1T_copy(t):
                act.wait_ge(*seen.next("a1T_ps", T))
                nc.scalar.activation(a1T[:], X1[:, :], ACT.Copy).then_inc(sem["a1T_ready"], 1)

            def s_gelu1(t):
                act.wait_ge(*seen.next("h1_ps"))
                nc.scalar.activation(gl[:], U[:, :], ACT.Gelu).then_inc(sem["gl_ready"], 1)

            steps = {n[2:]: f for n, f in locals().items() if n.startswith("s_")}

            def others(table, u, want):
                for name, t in beside(table, u, want):
                    if name in steps:
                        steps[name](t)

            def f0(b, units, want):
                for s in range(4 * U0):
                    u, part = divmod(s, 4)
                    if units and part == (1 if s > 4 else 1):
                        act.wait_ge(*seen.next("g_ps"))
                        if u >= 2:
                            act.wait_ge(*seen.next("hw_ready"))
                        nc.scalar.activation(hs[:, u % 2, :], G[u % 2][:, :], ACT.Silu).then_inc(sem["silu_ready"], 1)
                    others(STEPS, s, want)
                if units:
                    seen.next("hw_ready", 2)

            act.wait_ge(once["coef_in"], 2)
            nc.scalar.activation(lw[:, 2:4], lw[:, 0:2], ACT.Exp).then_inc(once["coef_exp"], 1)
            layer0(seen, act.Fori, f0)

            def group(n, b, u, stages):
                def has(k):
                    return k in stages and not (isinstance(b, int) and b == 0 and u < k)
                if has(0):
                    done(act, "xt_ps", n)
                    done(act, "gt_ps", n - 1)
                    nc.scalar.activation(xgTt[:], G[0][:, :], ACT.Copy).then_inc(sem["xt_ready"], 1)
                if has(1):
                    done(act, "gt_ps", n - 1)
                    done(act, "ht_ps", n - 2)
                    nc.scalar.activation(h1d[:], B[:, 0:Q * INTER].rearrange("p (q i) -> p q i", q=Q).unsqueeze(2)
                                         .broadcast_to([P, Q, 2, INTER]), ACT.Silu).then_inc(sem["gt_ready"], 1)
                if has(3):
                    done(act, "y_ps", n - 3)
                    par = (u - 3) % 2 if u < 10 ** 6 else (n - 3) % 2
                    if not (isinstance(b, int) and b == 0 and u < 5):
                        k = (b * (GROUPS // 2) + (u - 3) // 2) if u < 10 ** 6 else (n - 3) // 2
                        act.wait_ge(once[f"yst{par}"], k * 16)
                    nc.scalar.activation(ys[:, par, :], ACC[:, :], ACT.Copy).then_inc(sem["y_ready"], 1)

            def layer1(b):
                for u in range(GROUPS):
                    group(b * GROUPS + u, b, u, {0, 1, 3})
                    others(STEPS1, u, now(b))

            act.wait_ge(once["phase2"], 1)
            per_batch(seen, act.Fori, layer1)
            for k in range(1, 4):
                group(NG - 1 + k, NB, 10 ** 6, {1, 3} if k == 1 else {3})
            for u in range(GROUPS):
                others(STEPS1, u, {"late"})

            def end(b):
                act.wait_ge(*seen.next("sum_ready"))
                nc.scalar.activation(g1[:], acc[:].rearrange("p t d -> p (t d)"), ACT.Silu).then_inc(sem["g1_ready"], 1)

            per_batch(seen, act.Fori, end)

        @block.gpsimd
        def _(pool):
            seen = Seen(sems)

            def rsqrt(v, name="rsq"):
                pool.wait_ge(*seen.next(name + "_in"))
                nc.gpsimd.tensor_tensor(v, v, neg_half[:, 0:v.shape[1]], ALU.pow).then_inc(sem[name + "_ready"], 1)

            def waited(name):
                if seen.count[name]:
                    pool.wait_ge(sem[name], seen.value(name, seen.count[name]))
                seen.next(name)
                nc.gpsimd.tensor_tensor(ppause[:], neg_half[:, 0:1], neg_half[:, 0:1], ALU.mult).then_inc(sem[name], 1)

            def s_norm0a(t):
                rsqrt(rs[:])

            def s_res_add(t):
                rsqrt(rs[:])

            def s_res_norm(t):
                rsqrt(r1[:])

            def s_scatter(t):
                pool.wait_ge(*seen.next("idx_ready"))
                waited("pool_link")
                for t in range(T):
                    for k in range(TOPK1):
                        pool.indirect_dma_start(rows, bass.IndirectOffsetOnAxis(ap=idx[:, t * 8 + k:t * 8 + k + 1], axis=0), xn1[:, t, :], None)\
                            .then_inc(sem["scattered"], 16)

            def s_mix1a(t):
                rsqrt(ss1[:], "rsq1")

            def s_mix1b(t):
                rsqrt(rd1[:], "rsq1")

            steps = {n[2:]: f for n, f in locals().items() if n.startswith("s_")}

            def others(n, table, want):
                for u in range(n):
                    for name, t in beside(table, u, want):
                        if name in steps:
                            steps[name](t)

            nc.gpsimd.memset(x1n[:], 0.0).then_inc(once["zero_ready"], 1)
            nc.gpsimd.memset(neg_half[:], -0.5).then_inc(once["neg_ready"], 1)
            pool.wait_ge(once["neg_ready"], 1)

            def f0(b, units, want):
                if isinstance(b, int) and b == 1:
                    pool.wait_ge(loaded["zeros"], 16)
                others(4 * U0, STEPS, want)

            layer0(seen, pool.Fori, f0)
            pool.wait_ge(once["phase2"], 1)
            per_batch(seen, pool.Fori, lambda b: others(GROUPS, STEPS1, now(b)))
            for par in range(2):
                pool.wait_ge(once[f"yst{par}"], 16 * NG // 2)

            def end(b):
                for t in range(T):
                    if t == 0:
                        pool.wait_ge(*seen.next("idxc_ready"))
                    c = seen.count["gathered_used"] - 1
                    if c > 0 or seen.reg is not None:
                        pool.wait_ge(sem["gathered_used"], seen.value("gathered_used", c))
                    seen.next("gathered_used")
                    waited("pool_link3")
                    for k in range(TOPK1):
                        pool.indirect_dma_start(y8[:, t % 2, k, :], None, y_d, bass.IndirectOffsetOnAxis(ap=idxc[:, t * 8 + k:t * 8 + k + 1], axis=0))\
                            .then_inc(sem[f"gath{t % 2}"], 16)

            per_batch(seen, pool.Fori, end)

        @block.vector
        def _(dve):
            seen = Seen(sems)
            LK = ["dve_link"]

            def link(ins):
                seen.next(LK[0])
                ins.then_inc(sem[LK[0]], 1)
                return ins

            def join():
                dve.wait_ge(sem[LK[0]], seen.value(LK[0], seen.count[LK[0]]))

            def join_alone():
                join()
                nc.vector.memset(pause[:], 0.0)

            def ask(ins, name="rsq"):
                ins.then_inc(sem[name + "_in"], 1)
                seen.next(name + "_in")

            def take(name="rsq"):
                dve.wait_ge(*seen.next(name + "_ready"))

            def norm_ask(src):
                for t in range(T):
                    link(nc.vector.bn_stats(st[:, t, :], src[:, t, :]))
                join_alone()
                for t in range(T):
                    link(nc.vector.bn_aggr(mv[:, t, :], st[:, t, :]))
                join()
                ask(nc.vector.tensor_scalar(rs[:], mv[:, :, 1], LN_EPS, None, ALU.add))

            def norm_take(src, dst, name):
                take()
                for t in range(T):
                    last = nc.vector.tensor_scalar(dst[:, t, :], src[:, t, :], mv[:, t, 0:1], rs[:, t:t + 1], ALU.subtract, ALU.mult)
                last.then_inc(sem[name], 1)

            def parts(cw, rest, out_p, name):
                link(nc.vector.tensor_copy(out_p(0), cw))
                join()
                link(nc.vector.tensor_tensor(rest, cw, out_p(0), ALU.subtract))
                join()
                link(nc.vector.tensor_copy(out_p(1), rest))
                join()
                nc.vector.tensor_tensor(out_p(2), rest, out_p(1), ALU.subtract).then_inc(sem[name], 1)

            def s_norm0a(t):
                dve.wait_ge(*seen.next("x_loaded", 16))
                norm_ask(xs)

            def s_norm0b(t):
                norm_take(xs, xn0, "xn0_ready")

            def s_exp0(t):
                dve.wait_ge(*seen.next("lg0_ps"))
                lgt = X1[:, 0:T * E0].rearrange("p (t e) -> p t e", t=T)
                link(nc.vector.tensor_reduce(mx0[:], lgt, AX.X, ALU.max))
                join()
                nc.vector.tensor_tensor(l0[:], lgt, mx0[:].unsqueeze(2).broadcast_to([P, T, E0]), ALU.subtract).then_inc(sem["e0_in"], 1)

            def s_topk0a(t):
                dve.wait_ge(*seen.next("e0_ready"))
                link(nc.vector.tensor_reduce(sm0[:], e0[:], AX.X, ALU.add))
                join()
                link(nc.vector.reciprocal(sm0[:], sm0[:]))
                join()
                link(nc.vector.tensor_tensor(sc0[:, :, 0:E0], e0[:], sm0[:].unsqueeze(2).broadcast_to([P, T, E0]), ALU.mult))
                join_alone()
                for t in range(T):
                    link(nc.vector.max(m80[:, t, :], sc0[:, t, 0:E0]))

            def s_topk0b(t):
                join()
                link(nc.vector.memset(m80[:, :, 2:8], -1.0))
                link(nc.vector.tensor_tensor(sm0[:], m80[:, :, 0], m80[:, :, 1], ALU.add))
                join_alone()
                for t in range(T):
                    link(nc.vector.match_replace(sr0[:, t, :], m80[:, t, :], sc0[:, t, :], 0.0))
                link(nc.vector.tensor_scalar(sm0[:], sm0[:], 1e-20, None, ALU.add))
                join()
                link(nc.vector.reciprocal(sm0[:], sm0[:]))
                link(nc.vector.tensor_tensor(cwf0[:], sc0[:, :, 0:E0], sr0[:, :, 0:E0], ALU.subtract))
                join()
                link(nc.vector.tensor_tensor(cwf0[:], cwf0[:], sm0[:].unsqueeze(2).broadcast_to([P, T, E0]), ALU.mult))
                join()
                parts(cwf0[:], cwr0[:], lambda i: cwp0[:, :, i, :], "cw0_ready")

            def s_rope(t):
                dve.wait_ge(*seen.next("qkv0_ps"))
                x = X0[:, 0:2 * D].rearrange("p (h m) -> p h m", m=HD)
                c = cosr[:, t, :].unsqueeze(1).broadcast_to([P, 2 * H, HD])
                link(nc.vector.tensor_tensor(rA[:].rearrange("p (h m) -> p h m", m=HD), x, c, ALU.mult))
                xp = X0[:, 0:2 * D].rearrange("p (h i two) -> p h i two", i=HD // 2, two=2)
                op = rB[:].rearrange("p (h i two) -> p h i two", i=HD // 2, two=2)
                s = sinr[:, t, :].rearrange("p (i two) -> p i two", two=2)
                for j in range(2):
                    link(nc.vector.tensor_tensor(op[:, :, :, j], xp[:, :, :, 1 - j],
                                                 s[:, :, j].unsqueeze(1).broadcast_to([P, 2 * H, HD // 2]), ALU.mult))
                join()
                nc.vector.tensor_tensor(rr[:], rA[:], rB[:], ALU.add).then_inc(sem["rope_ready"], 1)

            def s_qkT_copy(t):
                dve.wait_ge(*seen.next("qkT0_ready"))
                nc.vector.tensor_tensor(qm[:], qkT[:, 0:P].unsqueeze(1).broadcast_to([P, 4, P]),
                                        headm[:].unsqueeze(2).broadcast_to([P, 4, P]), ALU.mult).then_inc(sem["qm_ready"], 1)

            def mask(g):
                dve.wait_ge(*seen.next("sc_ps"))
                nc.vector.tensor_tensor(att[:, g, :].rearrange("p (r i) -> p r i", r=4),
                                        (X0, X1)[g % 2][:, :].rearrange("p (r i) -> p r i", r=4),
                                        causal[:].unsqueeze(1).broadcast_to([P, 4, P]), ALU.mult).then_inc(sem["at_ready"], 1)

            def s_mask_a(t):
                mask(0)
                mask(1)

            def s_mask_b(t):
                mask(2)
                mask(3)

            def s_o_norm(t):
                dve.wait_ge(*seen.next("av_ps"))
                u = V[:, 0:H * HA].rearrange("p (h m) -> p h m", m=HA)
                link(nc.vector.tensor_scalar(dn[:], u[:, :, HD], ATT_EPS, None, ALU.add))
                if t == 0:
                    link(nc.vector.memset(state[:], 0.0))
                if t < T - 1:
                    nc.vector.tensor_tensor(stmp[:], X0[:, 0:H * HA], blockd[:], ALU.mult).then_inc(sem["state_read"], 1)
                join()
                link(nc.vector.reciprocal(rc[:], dn[:]))
                if t < T - 1:
                    dve.wait_ge(*seen.next("state_read"))
                    nc.vector.tensor_tensor(state[:], state[:], stmp[:], ALU.add).then_inc(sem["state_ready"], 1)
                join()
                nc.vector.tensor_tensor(o0[:], u[:, :, 0:HD], rc[:].unsqueeze(2).broadcast_to([P, H, HD]), ALU.mult)\
                    .then_inc(sem["o0_ready"], 1)

            bres = [0]

            def s_res_gate(t):
                dve.wait_ge(*seen.next("gT0_ready"))
                dve.wait_ge(*seen.next("s_rot_ready"))
                nc.vector.tensor_tensor(pT[:], sT0[:], gT[:], ALU.mult).then_inc(sem["pT0_ready"], 1)

            def s_res_add(t):
                dve.wait_ge(*seen.next("p0_ps"))
                dve.wait_ge(*seen.next("xr_loaded", 16))
                settled(dve, seen, "x1_stored", 16)
                nc.vector.tensor_tensor(x1n[:], xr[:], X0[:, :].rearrange("p (t d) -> p t d", t=T), ALU.add).then_inc(sem["x1_ready"], 1)
                dve.wait_ge(*seen.next("x1_ready"))
                norm_ask(x1n)

            def s_res_norm(t):
                settled(dve, seen, "scattered", 16 * T * TOPK1)
                norm_take(x1n, xn1, "xn1_ready")
                link(nc.vector.tensor_tensor(ms1[:], rs[:], rs[:], ALU.mult))
                join()
                link(nc.vector.tensor_tensor(ms1[:], ms1[:], mv[:, :, 1], ALU.mult))
                join()
                ask(nc.vector.tensor_scalar(r1[:], ms1[:], RMS_EPS, None, ALU.add))

            def s_res_r1(t):
                take()
                link(nc.vector.tensor_copy(r1all[:, bres[0], :], r1[:]))

            def s_probs1(t):
                dve.wait_ge(*seen.next("lg1_ps"))
                settled(dve, seen, "pp_stored", 16)
                for i, (bank, done_) in enumerate(((X0, "lg1a_ready"), (V, "lg1b_ready"))):
                    nc.vector.tensor_tensor(place[:, 2 * i:2 * i + 2, :], bank[:, 0:2 * E1].rearrange("p (t e) -> p t e", t=2),
                                            bias1[:].unsqueeze(1).broadcast_to([P, 2, E1]), ALU.add).then_inc(sem[done_], 1)

            def s_topk1a(t):
                dve.wait_ge(*seen.next("probs_ready"))
                nc.vector.memset(pause[:], 0.0)
                for t in range(T):
                    link(nc.vector.max(m8[:, t, :], pr[:, t, :]))

            def s_topk1b(t):
                join_alone()
                for t in range(T):
                    link(nc.vector.match_replace(pr2[:, t, :], m8[:, t, :], pr[:, t, :], -1.0))
                link(nc.vector.tensor_reduce(s8[:], m8[:], AX.X, ALU.add))
                join()
                nc.vector.tensor_tensor(chosen, pr2, pr, ALU.not_equal).then_inc(sem["chosen_ready"], 1)
                link(nc.vector.tensor_scalar(s8[:], s8[:], 1e-9, None, ALU.add))
                join()
                link(nc.vector.reciprocal(s8[:], s8[:]))
                join()
                link(nc.vector.tensor_scalar(s8all[:, bres[0], :], s8[:], 2.5, None, ALU.mult))

            def s_place_a(t):
                dve.wait_ge(*seen.next("rank_ps"))
                nc.vector.tensor_tensor(runn[:], run[:], V[:, 0:E1], ALU.add).then_inc(sem["run_ready"], 1)
                dve.wait_ge(*seen.next("run_ready"))
                link(nc.vector.tensor_scalar(pagesi[:], runn[:], float(P - 2), None, ALU.add))
                link(nc.vector.scalar_tensor_tensor(limit[:], pages[:], float(P), run[:], ALU.mult, ALU.subtract))
                join()
                link(nc.vector.tensor_scalar(pagesi[:], pagesi[:], 7, None, ALU.arith_shift_right))
                join()
                link(nc.vector.tensor_copy(pagesn[:], pagesi[:]))
                join()
                link(nc.vector.tensor_tensor(new[:], pagesn[:], pages[:], ALU.subtract))
                link(nc.vector.tensor_copy(hj[:, 0:1], given[:, E1 - 1:E1]))
                join()
                link(nc.vector.tensor_tensor_scan(given[:], ones1[:], new[:], 0.0, ALU.mult, ALU.add))
                join()
                link(nc.vector.tensor_scalar(given[:], given[:], hj[:, 0:1], None, ALU.add))
                join()
                link(nc.vector.tensor_tensor(shiftn[:], given[:], pagesn[:], ALU.subtract))
                join()
                link(nc.vector.tensor_tensor(dshift[:], shift[:], shiftn[:], ALU.subtract))
                link(nc.vector.scalar_tensor_tensor(base[:], shiftn[:], float(P), run[:], ALU.mult, ALU.add))
                join()

            def s_place_b(t):
                link(nc.vector.scalar_tensor_tensor(shift[:], new[:], 0.0, dshift[:], ALU.is_equal, ALU.mult))
                link(nc.vector.tensor_scalar(scr[:], dshift[:], float(P), None, ALU.mult))
                for i, bank in enumerate((X0, X1)):
                    link(nc.vector.tensor_tensor(pr2[:, 2 * i:2 * i + 2, :], bank[:, 0:2 * E1].rearrange("p (t e) -> p t e", t=2),
                                                 limit[:].unsqueeze(1).broadcast_to([P, 2, E1]), ALU.is_le))
                join()
                link(nc.vector.tensor_tensor(shift[:], shift[:], shiftn[:], ALU.add))
                link(nc.vector.tensor_tensor(pr2, pr2, scr[:].unsqueeze(1).broadcast_to([P, T, E1]), ALU.mult))
                for i, (bank, done_) in enumerate(((X0, "ranka_read"), (X1, "rankb_read"))):
                    nc.vector.tensor_tensor(place[:, 2 * i:2 * i + 2, :], bank[:, 0:2 * E1].rearrange("p (t e) -> p t e", t=2),
                                            base[:].unsqueeze(1).broadcast_to([P, 2, E1]), ALU.add).then_inc(sem[done_], 1)
                dve.wait_ge(*seen.next("ranka_read"))
                dve.wait_ge(*seen.next("rankb_read"))
                join()
                link(nc.vector.tensor_copy(run[:], runn[:]))
                link(nc.vector.tensor_copy(pages[:], pagesn[:]))
                link(nc.vector.tensor_tensor(place, place, pr2, ALU.add))
                join()
                dve.wait_ge(*seen.next("chosen_ready"))
                nc.vector.tensor_tensor(place, place, chosen, ALU.mult).then_inc(sem["places_ready"], 1)

            def s_place_c(t):
                dve.wait_ge(*seen.next("places_ready"))
                nc.vector.memset(pause[:], 0.0)
                for t in range(T):
                    link(nc.vector.max(p8[:, t, :], place[:, t, :]))
                join()
                p8f = p8[:].rearrange("p t k -> p (t k)")
                link(nc.vector.tensor_scalar(idxy[:, bres[0], :], p8f, -1.0, None, ALU.add))
                nc.vector.tensor_scalar(idx[:], p8f, -1.0, None, ALU.add).then_inc(sem["idx_ready"], 1)
                for k in range(JB):
                    link(nc.vector.tensor_scalar(scr[:], given[:], jcol[:, k:k + 1], 0.0, ALU.is_le, ALU.add, accum_out=cj[:, k:k + 1]))
                    join()
                link(nc.vector.scalar_tensor_tensor(cj[:], cj[:], E1 - 0.5, cj[:], ALU.is_lt, ALU.mult))
                join()
                link(nc.vector.tensor_tensor(ej[:], ej[:], cj[:], ALU.add))

            def s_xg(t):
                dve.wait_ge(*seen.next("xin_loaded", 16))
                link(nc.vector.tensor_copy(r1c[:], r1all[:, bres[0], :]))
                nc.vector.tensor_scalar(xgT, xin[:], g1c[:, 0:1], None, ALU.mult).then_inc(sem["xg_ready"], 1)
                join()

            def s_elu1(t):
                dve.wait_ge(*seen.next("qkv1_ps"))
                nc.vector.tensor_scalar(mn1[:], X0[:, 0:2 * D], r1c[:, t:t + 1], 0.0, ALU.mult, ALU.min).then_inc(sem["mn1_ready"], 1)
                nc.vector.tensor_scalar(mxq1[:], X0[:, 0:2 * D], r1c[:, t:t + 1], 0.0, ALU.mult, ALU.max).then_inc(sem["mx1_ready"], 1)

            def s_mix1a(t):
                dve.wait_ge(*seen.next("mx1_ready"))
                dve.wait_ge(*seen.next("ex1_ready"))
                nc.vector.scalar_tensor_tensor(qk1[:], ex1[:], -1.0, mxq1[:], ALU.add, ALU.add).then_inc(sem["k1_ready"], 1)
                dve.wait_ge(*seen.next("k1_ready"))
                link(nc.vector.tensor_tensor(qc1[:].rearrange("p (h e) -> p h e", h=H), qk1[:, 0:D].rearrange("p (h e) -> p h e", h=H),
                                             coef[:].unsqueeze(1).broadcast_to([P, H, HD]), ALU.mult))
                dve.wait_ge(*seen.next("v1_ready"))
                k = qk1[:, D:2 * D].rearrange("p (h e) -> p e h", h=H).unsqueeze(2).broadcast_to([P, HD, HD, H])
                v = v1[:].rearrange("p (h d) -> p d h", h=H).unsqueeze(1).broadcast_to([P, HD, HD, H])
                nc.vector.tensor_tensor(prodA, k, v, ALU.mult).then_inc(sem["prod1_ready"], 1)
                dve.wait_ge(*seen.next("prod1_ready"))
                link(nc.vector.tensor_reduce(kv1[:], prodA, AX.X, ALU.add))
                join()
                q = qc1[:].rearrange("p (h e) -> p h e", h=H).unsqueeze(2).broadcast_to([P, H, HD, HD])
                kv = kv1[:].rearrange("p e d -> p d e").unsqueeze(1).broadcast_to([P, H, HD, HD])
                link(nc.vector.tensor_tensor(prodB, q, kv, ALU.mult))
                join()
                link(nc.vector.tensor_reduce(at1[:], prodB, AX.X, ALU.add))
                join()
                link(nc.vector.tensor_tensor(sq1[:], at1[:], at1[:], ALU.mult))
                join()
                link(nc.vector.tensor_reduce(ss1[:], sq1[:], AX.X, ALU.add))
                join()
                ask(nc.vector.tensor_scalar(ss1[:], ss1[:], 1.0 / HD, RMS_EPS, ALU.mult, ALU.add), "rsq1")

            def s_mix1b(t):
                take("rsq1")
                link(nc.vector.tensor_tensor(sq1[:], at1[:], ss1[:].unsqueeze(2).broadcast_to([P, H, HD]), ALU.mult))
                join()
                link(nc.vector.tensor_tensor(a1[:], sq1[:], g2r[:].unsqueeze(1).broadcast_to([P, H, HD]), ALU.mult))
                join()
                link(nc.vector.scalar_tensor_tensor(sq1[:], a1[:], 1.0, a1[:], ALU.mult, ALU.mult, accum_out=rd1[:]))
                join()
                ask(nc.vector.tensor_scalar(rd1[:], rd1[:], 1.0 / D, RMS_EPS, ALU.mult, ALU.add), "rsq1")

            def s_mix1c(t):
                take("rsq1")
                sqf = sq1[:].rearrange("p h d -> p (h d)")
                link(nc.vector.tensor_scalar(sqf, g3r[:], rd1[:, 0:1], 1.0, ALU.mult, ALU.add))
                join()
                nc.vector.tensor_tensor(a1b[:, t, :], a1[:].rearrange("p h d -> p (h d)"), sqf, ALU.mult).then_inc(sem["a1_ready"], 1)

            def s_s1(t):
                dve.wait_ge(*seen.next("o1_ps"))
                settled(dve, seen, "s1_stored", 16)
                nc.vector.tensor_tensor(s1b[:], a1b[:], X0[:, :].rearrange("p (t d) -> p t d", t=T), ALU.add).then_inc(sem["s1_ready"], 1)

            steps = {n[2:]: f for n, f in locals().items() if n.startswith("s_")}

            def others(table, u, want):
                for name, t in beside(table, u, want):
                    if name in steps:
                        steps[name](t)

            def f0(b, units, want):
                if isinstance(b, int) and b == 1:
                    dve.wait_ge(loaded["zeros"], 16)
                bres[0] = b - 1
                if units:
                    dve.wait_ge(*seen.next("xn0T_ready"))
                    dve.wait_ge(*seen.next("cw0T_ready"))
                    settled(dve, seen, "acc_done")
                    link(nc.vector.tensor_copy(cw0T[:], cw0Tn[:]))
                    nc.vector.tensor_copy(xn0T[:], xn0Tn[:]).then_inc(sem["rot_ready"], 1)
                for s in range(4 * U0):
                    u, part = divmod(s, 4)
                    if units and part == 2:
                        dve.wait_ge(*seen.next("silu_ready"))
                        dve.wait_ge(*seen.next("up_ps"))
                        nc.vector.tensor_tensor(hs[:, u % 2, :], hs[:, u % 2, :], U[:, :], ALU.mult).then_inc(sem["hu_ready"], 1)
                        dve.wait_ge(*seen.next("hu_ready"))
                        dve.wait_ge(*seen.next("b_ps"))
                        if u >= RH:
                            dve.wait_ge(*seen.next("down_done"))
                        nc.vector.tensor_tensor(hw[:, u % RH, :], hs[:, u % 2, :], B[:, :], ALU.mult).then_inc(sem["hw_ready"], 1)
                    if units and s == 4:
                        dve.wait_ge(*seen.next("sT0_ready"))
                        if "res" in want:
                            dve.wait_ge(sem["pT0_ready"], seen.value("pT0_ready", seen.count["pT0_ready"] + 1))
                        nc.vector.tensor_copy(sT0[:], sT0n[:]).then_inc(sem["s_rot_ready"], 1)
                    others(STEPS, s, want)
                if "res" in want:
                    seen.next("pT0_ready")
                if units:
                    seen.next("down_done", RH - 1)

            dve.wait_ge(loaded["small"], 16 * len(small))
            nc.vector.memset(sc0[:], -1.0)
            nc.vector.memset(idxy[:], 0)
            for v, x in ((run, 1.0), (ones1, 1.0), (pages, 0.0), (given, 0.0), (shift, 0.0), (ej, 0.0)):
                link(nc.vector.memset(v[:], x))
            nc.vector.memset(vaug[:], 1.0).then_inc(once["const_ready"], 1)
            lm = lam[:].rearrange("p (a b) -> p a b", b=2)
            nc.vector.tensor_tensor(lw[:, 0:2], lm[:, :, 0], lm[:, :, 1], ALU.mult).then_inc(once["coef_in"], 1)
            link(nc.vector.memset(coef[:], SCALE1))
            nc.vector.tensor_scalar(g2r[:], g2r[:], 1.0 - LAMBDA_INIT, None, ALU.mult).then_inc(once["coef_in"], 1)
            dve.wait_ge(once["coef_exp"], 1)
            link(nc.vector.tensor_tensor(lw[:, 0:1], lw[:, 2:3], lw[:, 3:4], ALU.subtract))
            join()
            link(nc.vector.tensor_scalar(lw[:, 1:2], lw[:, 0:1], LAMBDA_INIT, -1.0, ALU.add, ALU.mult))
            join()
            link(nc.vector.tensor_scalar(coef[:, HD // 2:HD], coef[:, HD // 2:HD], lw[:, 1:2], None, ALU.mult))
            join()
            layer0(seen, dve.Fori, f0)

            join()
            link(nc.vector.tensor_copy(hji[:], ej[:]))
            link(nc.vector.tensor_scalar(tabi[:, 0, :], ej[:], float(INTER), None, ALU.mult))
            join()
            link(nc.vector.tensor_scalar(hji[:], hji[:], 1, None, ALU.arith_shift_right))
            join()
            link(nc.vector.tensor_copy(hj[:], hji[:]))
            join()
            nc.vector.tensor_scalar(tabi[:, 1, :], hj[:], float(D), None, ALU.mult).then_inc(once["tab_ready"], 1)
            nc.vector.scalar_tensor_tensor(parj[:], hj[:], -2.0, ej[:], ALU.mult, ALU.add).then_inc(once["half_in"], 1)
            dve.wait_ge(once["half_ps"], 1)
            nc.vector.tensor_scalar(half_of, X0[:, :], hid[:, 0:1], None, ALU.is_equal).then_inc(once["half_ready"], 1)
            dve.wait_ge(once["half_ready"], 1)
            dve.wait_ge(sem["scattered"], 16 * T * TOPK1 * NB)
            dve.wait_ge(sem["x1_stored"], 16 * NB)
            dve.wait_ge(sem["xn1T_stored"], 16 * NB)
            dve.wait_ge(sem["pp_stored"], 16 * NB)
            nc.vector.memset(pause[:], 0.0).then_inc(once["phase2"], 1)
            LK[0] = "dve_link2"

            def group(n, b, u):
                if isinstance(b, int) and b == 0 and u < 2:
                    return
                done(dve, "ht_ps", n - 2)
                done(dve, "y_ps", n - 3)
                nc.vector.tensor_tensor(hT[:].rearrange("p (q r) -> p q r", q=Q), V[:, :].rearrange("p (q r) -> p q r", q=Q),
                                        half_of[:, bass.ds((n - 2) * Q, Q)].unsqueeze(2).broadcast_to([P, Q, P]), ALU.mult)\
                    .then_inc(sem["ht_ready"], 1)

            def layer1(b):
                bres[0] = b
                for u in range(GROUPS):
                    group(b * GROUPS + u, b, u)
                    others(STEPS1, u, now(b))

            per_batch(seen, dve.Fori, layer1)
            for k in range(1, 3):
                group(NG - 1 + k, NB, 10 ** 6)
            for u in range(GROUPS):
                others(STEPS1, u, {"late"})
            LK[0] = "dve_link3"
            nc.vector.tensor_copy(idxc[:], idxy[:, 0, :]).then_inc(sem["idxc_ready"], 1)

            def end(b):
                dve.wait_ge(*seen.next("ppf_loaded", 16))
                nc.vector.memset(pause[:], 0.0)
                for t in range(T):
                    link(nc.vector.max(p8[:, t, :], place[:, t, :]))
                join()
                for t in range(T):
                    for k in range(TOPK1):
                        link(nc.vector.scalar_tensor_tensor(terms[:, t * TOPK1 + k, :], place[:, t, :], p8[:, t, k:k + 1], pr[:, t, :], ALU.is_equal, ALU.mult,
                                                            accum_out=w8[:, t, k:k + 1]))
                join()
                link(nc.vector.tensor_tensor(w8[:], w8[:], s8all[:, b, :].unsqueeze(2).broadcast_to([P, T, 8]), ALU.mult))
                join()
                for t in range(T):
                    dve.wait_ge(*seen.next(f"gath{t % 2}", 16 * TOPK1))
                    if t == T - 1:
                        dve.wait_ge(sem["gath0"], seen.value("gath0", seen.count["gath0"]))
                        nc.vector.tensor_copy(idxc[:], idxy[:, b + 1, :]).then_inc(sem["idxc_ready"], 1)
                    y = y8[:, t % 2, :, :]
                    link(nc.vector.tensor_tensor(y, y, w8[:, t, :].unsqueeze(2).broadcast_to([P, 8, D]), ALU.mult))
                    join()
                    nc.vector.tensor_reduce(acc[:, t, :], y.rearrange("p k d -> p d k"), AX.X, ALU.add).then_inc(sem["gathered_used"], 1)
                    dve.wait_ge(*seen.next("gathered_used"))
                dve.wait_ge(*seen.next("shf_loaded", 16))
                nc.vector.tensor_tensor(acc[:], acc[:], shf[:], ALU.add).then_inc(sem["sum_ready"], 1)
                dve.wait_ge(*seen.next("g1_ready"))
                dve.wait_ge(*seen.next("s1f_loaded", 16))
                link(nc.vector.tensor_tensor(s1f[:], s1f[:], g1[:].rearrange("p (t d) -> p t d", t=T), ALU.mult))
                join()
                dve.wait_ge(*seen.next("x1f_loaded", 16))
                settled(dve, seen, "out_stored", 16)
                nc.vector.tensor_tensor(outs[:], x1f[:], s1f[:], ALU.add).then_inc(sem["out_ready"], 1)

            per_batch(seen, dve.Fori, end)


def kernel(**inputs):
    import numpy as _np
    import concourse.bacc as _bacc
    from concourse import mybir as _mybir
    from concourse.bass_utils import run_bass_kernel_spmd as _run

    i = {k: _np.asarray(v) for k, v in inputs.items()}
    f4 = _np.float32
    bf = _mybir.dt.np(BF16) if hasattr(_mybir.dt, "np") else None
    import ml_dtypes
    bf = ml_dtypes.bfloat16

    def tiles(w, n):
        return w.reshape(n, P, D).transpose(1, 0, 2)

    def rows(v):
        return _np.broadcast_to(v.reshape(1, -1), (P, v.size))

    inv_freq = (f4(1.0) / _np.power(f4(10000.0), _np.arange(0, HD, 2, dtype=f4) / f4(HD), dtype=f4)).astype(f4)
    freqs = (_np.arange(L, dtype=f4)[:, None] * inv_freq[None, :]).astype(f4)
    cos, sin = _np.cos(freqs.astype(_np.float64)), _np.sin(freqs.astype(_np.float64))
    cosr = _np.repeat(cos, 2, axis=1)
    sinr = _np.stack([-sin, sin], axis=-1).reshape(L, HD)
    pos = _np.arange(P)
    sel0 = _np.tile((_np.arange(U0 * P)[None, :] // HID0 == _np.arange(E0)[:, None]), (3, 1))
    given = {
        "x": i["L0_attn_x"].reshape(NB * L, D),
        "wqkv0": _np.concatenate([i["L0_attn_wq"], i["L0_attn_wk"], i["L0_attn_wv"]], axis=1),
        "wo0": i["L0_attn_wo"],
        "wr0": i["L0_ffn_Wg"].T,
        "w1_0": i["L0_ffn_W1"].reshape(-1, D).T,
        "w3_0": i["L0_ffn_W3"].reshape(-1, D).T,
        "w2_0": tiles(i["L0_ffn_W2"].transpose(0, 2, 1).reshape(-1, D), U0),
        "wqkv1": _np.concatenate([i["L1_attn_Wq"], i["L1_attn_Wk"], i["L1_attn_Wv"]], axis=0).T,
        "wf1": i["L1_attn_W1"].T,
        "wf2": i["L1_attn_W2"].T,
        "wr1": i["L1_ffn_router_w"].T,
        "bias1": rows(i["L1_ffn_expert_bias"]),
        "g1c": i["L1_attn_g1"].reshape(P, 1),
        "g2r": rows(i["L1_attn_g2"]),
        "g3r": rows(i["L1_attn_g3"]),
        "lam": rows(i["L1_attn_lambda_params"]),
        "wg_1": i["L1_ffn_w_gate"].reshape(-1, D).T,
        "wd_1": tiles(i["L1_ffn_w_down"].transpose(0, 2, 1).reshape(-1, D), E1 // 2).reshape(P, -1),
        "wgs": i["L1_ffn_w_gate_shared"].T,
        "wds": i["L1_ffn_w_down_shared"].T,
        "ident": _np.eye(P, dtype=f4),
        "identb": _np.eye(P, dtype=bf),
        "cosr": cosr.astype(f4).reshape(T, P, HD).transpose(1, 0, 2),
        "sinr": sinr.astype(f4).reshape(T, P, HD).transpose(1, 0, 2),
        "causal": (pos[:, None] <= pos[None, :]).astype(f4),
        "headm": ((pos[:, None] // HD) % 4 == _np.arange(4)[None, :]).astype(f4),
        "blockd": (pos[:, None] // HD == _np.arange(H * HA)[None, :] // HA).astype(f4),
        "sel0": sel0.astype(bf),
        "before": (pos[:, None] < pos[None, :]).astype(bf),
        "onesb": _np.ones((P, P), dtype=bf),
        "jcol": (_np.arange(JB)[None, :] * P + pos[:, None]).astype(f4),
        "hid": (pos[:, None] // INTER).astype(f4),
    }
    nc = _bacc.Bacc("TRN2", target_bir_lowering=False, num_devices=1)
    arrays, aps = {}, {}
    for name, v in given.items():
        v = _np.ascontiguousarray(v)
        arrays[f"in_{name}"] = v
        aps[name] = nc.dram_tensor(f"in_{name}", v.shape, _mybir.dt.from_np(v.dtype), kind="ExternalInput").ap()
    out = nc.dram_tensor("out_dram", (NB * L, D), F32, kind="ExternalOutput").ap()
    build(nc, aps, out)
    r = _run(nc, [arrays], core_ids=[0])
    return r.results[0]["out_dram"].reshape(NB, L, D)
```

```python
import concourse.bass as bass
from concourse import mybir
from contextlib import ExitStack
import numpy as np

F32 = mybir.dt.float32
BF16 = mybir.dt.bfloat16
I32, U32 = mybir.dt.int32, mybir.dt.uint32
ALU = mybir.AluOpType
ACT = mybir.ActivationFunctionType
AX = mybir.AxisListType

P = 128
D = 128
NB = 8
L = 512
T = L // P
H = 16
HD = D // H
HA = HD + 1
E0, HID0 = 8, 352
U0 = E0 * HID0 // P
E1, INTER = 160, 64
TOPK1 = 8
LAG = 2
TERMS = 4
RH = 3

TILES = E1 + NB * L * TOPK1 // P
Q = 4
GROUPS = 2 * -(-TILES // (2 * Q * NB))
NG = GROUPS * NB
NJ = NG * Q
JB = -(-NJ // P)
MORE_PAGES = L * TOPK1 // P
FIRST_PAGES = E1 + MORE_PAGES
assert FIRST_PAGES + (NB - 1) * MORE_PAGES <= NJ and NJ % (NB - 1) == 0
LN_EPS = 1e-5
ATT_EPS = 1e-6
RMS_EPS = float(np.finfo(np.float32).eps)
LAMBDA_INIT = 0.8 - 0.6 * float(np.exp(-0.3 * 0))
SCALE1 = 1.0 / float(np.sqrt(D // 2))

PER_BATCH = dict(
    xn0_ready=1, xn0T_ps=1, xn0T_ready=1, lg0_ps=1, e0_in=1, e0_ready=1, cw0_ready=1, cw0T_ps=1, cw0T_ready=1,
    rot_ready=1, s_rot_ready=1,
    qkv0_ps=T, rope_ready=T, v0_ready=T, qk0_ready=T, qkT0_ps=T, qkT0_ready=T, qm_ready=T, sc_ps=4 * T, at_ready=4 * T,
    av_ps=T, o0_ready=T, state_read=T - 1, state_ready=T - 1, oT_ps=T, oT_ready=T, sT0_ps=1, sT0_ready=1,
    gT0_ready=1, pT0_ready=1, p0_ps=1, x1_ready=1, xn1_ready=1, xn1T_ps=1, xn1T_ready=1, lg1_ps=1,
    lg1a_ready=1, lg1b_ready=1, probs_ready=1, chosen_ready=1, rank_ps=1, ranka_read=1, rankb_read=1, run_ready=1,
    places_ready=1, idx_ready=1,
    g_ps=U0, up_ps=U0, b_ps=U0, silu_ready=U0, hu_ready=U0, hw_ready=U0, down_done=U0 - 1, acc_done=1,
    xg_ready=1, qkv1_ps=T, mn1_ready=T, mx1_ready=T, ex1_ready=T, v1_ready=T, k1_ready=T, prod1_ready=T, a1_ready=T,
    a1T_ps=T, a1T_ready=1, h1_ps=1, gl_ready=1, o1_ps=1, s1_ready=1, sg_ps=1, sg_ready=1, sh_ps=1, sh_ready=1,
    xt_ps=GROUPS, xt_ready=GROUPS, gt_ps=GROUPS, gt_ready=GROUPS, ht_ps=GROUPS, ht_ready=GROUPS, y_ps=GROUPS, y_ready=GROUPS,
    idxc_ready=1, sum_ready=2, g1_ready=2, out_ready=2, gathered_used=2 * T,
    rsq_in=3 + 0, rsq_ready=3 + 0, rsq1_in=2 * T, rsq1_ready=2 * T,
    x_loaded=16, xr_loaded=16, x1_stored=16, xn1T_stored=16, scattered=16 * T * TOPK1,
    xin_loaded=16, s1_stored=16, sh_stored=16, rows0_loaded=16 * GROUPS // 2,
    rows1_loaded=16 * GROUPS // 2, y_stored=16 * GROUPS,
    x1f_loaded=32, s1f_loaded=32, shf_loaded=32, gath0=16 * TOPK1 * T, gath1=16 * TOPK1 * T,
    out_stored=32,
    dve_link=0, dve_link2=0, dve_link3=0, pool_link=1, pool_link3=2 * T,
)
LINKS = dict(dve_link=138, dve_link2=41, dve_link3=52)


class Seen:

    def __init__(self, sems):
        self.sems, self.count, self.reg, self.first = sems, {n: 0 for n in sems}, None, 0
        self.readers = {}

    def value(self, name, count):
        if self.reg is None:
            return count
        return (self.reg - self.first) * self.sems[name][1] + count

    def next(self, name, by=1):
        self.count[name] += by
        for names in self.readers.values():
            if name in names:
                names.remove(name)
        return self.sems[name][0], self.value(name, self.count[name])

    def lag(self, name, by):
        c = self.count[name] + 1 - by
        return None if c <= 0 and self.reg is None else (self.sems[name][0], self.value(name, c))

    def bank(self, bank):
        return [self.next(n) for n in list(self.readers.pop(bank, []))]

    def loop(self, reg, first):
        self.reg, self.first, self.entry = reg, first, dict(self.count)

    def loop_end(self, trips):
        for n, (_, per) in self.sems.items():
            got = self.count[n] - self.entry[n]
            assert got in (0, per), f"{n}: {got} events in the loop's body, {per} declared"
            self.count[n] += got * (trips - 1)
        self.reg = None


STEPS = {0: ["res_silu"], 1: ["res_gate"], 3: ["res_T"], 4: ["res_add"], 6: ["res_norm"], 9: ["xn1_T", "res_r1"],
         10: ["xn1T_copy"], 11: ["norm0a"], 12: ["router1"], 13: ["probs1"], 14: ["norm0b"], 15: ["topk1a"],
         16: ["xn0_T"], 17: ["xn0T_copy"], 18: ["topk1b", "router0"], 19: ["exp0"], 21: ["rank"], 48: ["topk0a"], 61: ["topk0b"],
         23: ["place_a"], 25: ["place_b"], 28: ["place_c"], 29: ["scatter"], 72: ["cw0_T", "cw0T_copy"], 86: ["wo"], 87: ["s0"]}
for t in range(T):
    for at, name in ((0, "qkv0"), (1, "rope"), (3, "qk_T"), (4, "qkT_copy"), (6, "scores_a"), (7, "mask_a"),
                     (9, "scores_b"), (10, "mask_b"), (11, "av"), (12, "o_norm"), (14, "o_T"), (14, "oT_copy")):
        STEPS.setdefault(31 + 13 * t + at, []).append((name, t))
    STEPS[31 + 13 * t + 4].append(("weights", t))
RES = {"res_silu", "res_gate", "res_T", "res_add", "res_norm", "res_r1", "xn1_T", "xn1T_copy", "router1", "probs1",
       "topk1a", "topk1b", "rank", "place_a", "place_b", "place_c", "weights", "scatter"}
STEPS1 = {0: [("mix1c", T - 1)], 1: [("a1_T", T - 1), "a1T_copy", "xg"], 2: ["ffh1"], 3: ["gelu1"],
          4: ["ffo1", "s1", "shared_up"], 5: ["shared_down"]}
for t in range(T):
    if t:
        STEPS1.setdefault(3 * t + 2, []).append(("mix1c", t - 1))
        STEPS1.setdefault(3 * t + 3, []).append(("a1_T", t - 1))
    for at, name in ((1, "qkv1"), (1, "elu1"), (2, "exp1"), (3, "mix1a"), (4, "mix1b")):
        STEPS1.setdefault(3 * t + at, []).append((name, t))
LATE = {("mix1c", T - 1), ("a1_T", T - 1), ("a1T_copy", 0), ("ffh1", 0), ("gelu1", 0), ("ffo1", 0), ("s1", 0)}
FIRST_END = NB // 2
ENDS = {0: [("weigh", 7)], 1: [("load_s1", 1), ("end_sum", 1), "idxc"], 2: [("end_silu", 1)], 3: [("end_out", 1)],
        4: [("store_out", 1)], 5: [("load_rest", 0), ("load_s1", 0)], 9: [("end_silu", 0)], 10: [("end_out", 0)],
        11: [("store_out", 0)], 12: [("load_rest", 1)]}
for i, (at, used) in enumerate(((2, 4), (3, 5), (5, 7), (6, 8), (8, 10), (9, 11), (11, 13), (12, None))):
    ENDS.setdefault(at, []).append(("gather", i))
    if used:
        ENDS.setdefault(used, []).append(("weigh", i))
ENDS[8].append(("end_sum", 0))
LATE_END = {("weigh", 7), ("load_s1", 1), ("end_sum", 1), ("end_silu", 1), ("end_out", 1), ("store_out", 1)}
ENDING = {"load_rest", "load_s1", "gather", "weigh", "end_sum", "end_silu", "end_out", "store_out", "idxc"}
for at, names in ENDS.items():
    STEPS1.setdefault(at, []).extend(names)


def kind(name, t):
    if name in RES:
        return "res"
    if name in ENDING:
        return "late_end" if (name, t) in LATE_END else "end"
    return "late" if (name, t) in LATE else "pre"


def beside(table, u, want):
    for s in table.get(u, []):
        name, t = s if isinstance(s, tuple) else (s, 0)
        if kind(name, t) in want:
            yield name, t


def build(nc, a, out):
    ctx = ExitStack()
    with ctx:
        def sb(name, shape, dt=F32):
            return ctx.enter_context(nc.sbuf_tensor(name, shape, dt))

        def dram(name, shape, dt=F32):
            return nc.dram_tensor(name, shape, dt, kind="Internal").ap()

        w1_0, w3_0 = sb("w1_0", [P, U0 * P]), sb("w3_0", [P, U0 * P])
        w2_0 = sb("w2_0", [P, U0, D])
        wg_1 = sb("wg_1", [P, E1 * INTER])
        wd_1 = sb("wd_1", [P, E1 // 2 * D])
        wgs, wds = sb("wgs", [P, INTER]), sb("wds", [INTER, D])
        wqkv0, wo0, wr0 = sb("wqkv0", [P, 3 * D]), sb("wo0", [P, D]), sb("wr0", [P, E0])
        wqkv1, wf1, wf2, wr1 = sb("wqkv1", [P, 3 * D]), sb("wf1", [P, D]), sb("wf2", [P, D]), sb("wr1", [P, E1])
        bias1, g1c, g2r, g3r, lam = sb("bias1", [P, E1]), sb("g1c", [P, 1]), sb("g2r", [P, HD]), sb("g3r", [P, D]), sb("lam", [P, 4])
        ident, identb = sb("ident", [P, P]), sb("identb", [P, P], BF16)
        before, onesb = sb("before", [P, P], BF16), sb("onesb", [P, P], BF16)
        cosr, sinr = sb("cosr", [P, T, HD]), sb("sinr", [P, T, HD])
        causal, headm, blockd = sb("causal", [P, P]), sb("headm", [P, 4]), sb("blockd", [P, H * HA])
        sel0 = sb("sel0", [3 * E0, U0 * P], BF16)
        jcol, hid = sb("jcol", [P, JB]), sb("hid", [P, 1])
        zero = sb("zero", [P, D])
        neg_half, pause, ppause = sb("neg_half", [P, H]), sb("pause", [P, 1]), sb("ppause", [P, 1])
        xs, xn0, xn0Tn, xn0T = sb("xs", [P, T, D]), sb("xn0", [P, T, D]), sb("xn0Tn", [P, L]), sb("xn0T", [P, L])
        st, mv, rs = sb("st", [P, T, 6]), sb("mv", [P, T, 2]), sb("rs", [P, T])
        mx0, l0, e0, sm0 = sb("mx0", [P, T]), sb("l0", [P, T, E0]), sb("e0", [P, T, E0]), sb("sm0", [P, T])
        sc0, m80, sr0 = sb("sc0", [P, T, 14]), sb("m80", [P, T, 8]), sb("sr0", [P, T, 14])
        cwf0, cwr0, cwp0 = sb("cwf0", [P, T, E0]), sb("cwr0", [P, T, E0]), sb("cwp0", [P, T, 3, E0], BF16)
        cw0Tn, cw0T = sb("cw0Tn", [3 * E0, L], BF16), sb("cw0T", [3 * E0, L], BF16)
        rA, rB, rr, qk, vaug = sb("rA", [P, 2 * D]), sb("rB", [P, 2 * D]), sb("rr", [P, 2 * D]), sb("qk", [P, 2 * D]), sb("vaug", [P, H, HA])
        qkT, qm, att = sb("qkT", [P, 2 * P]), sb("qm", [P, 4, P]), sb("att", [P, 4, 4 * P])
        attf = att[:].rearrange("p g c -> p (g c)")
        dn, rc, o0, oT = sb("dn", [P, H]), sb("rc", [P, H]), sb("o0", [P, H, HD]), sb("oT", [P, L])
        state, stmp = sb("state", [P, H * HA]), sb("stmp", [P, H * HA])
        sT0n, sT0, gT, pT = sb("sT0n", [P, L]), sb("sT0", [P, L]), sb("gT", [P, L]), sb("pT", [P, L])
        hs, hw = sb("hs", [P, 2, L]), sb("hw", [P, RH, L])
        xr, x1n, xn1, xn1Tn = sb("xr", [P, T, D]), sb("x1n", [P, T, D]), sb("xn1", [P, T, D]), sb("xn1Tn", [P, L])
        ms1, r1, r1all, s8 = sb("ms1", [P, T]), sb("r1", [P, T]), sb("r1all", [P, NB, T]), sb("s8", [P, T])
        w8, w8all, terms = sb("w8", [P, T, TOPK1]), sb("w8all", [P, NB, T * TOPK1]), sb("terms", [P, TERMS, E1])
        pp = sb("pp", [P, 2, T, E1])
        place, pr = pp[:, 0, :, :], pp[:, 1, :, :]
        m8, p8 = sb("m8", [P, T, 8]), sb("p8", [P, T, 8])
        idxy = sb("idxy", [P, NB + 1, T * 8], U32)
        idx = sb("idx", [P, T * 8], U32)
        pr2 = attf[:, 0:T * E1].rearrange("p (t e) -> p t e", t=T)
        chosen = attf[:, T * E1:T * E1 * 3 // 2].bitcast(BF16).rearrange("p (t e) -> p t e", t=T)
        run, runn = sb("run", [P, E1]), sb("runn", [P, E1])
        pages, pagesn, new = sb("pages", [P, E1]), sb("pagesn", [P, E1]), sb("new", [P, E1])
        pagesi, ones1 = sb("pagesi", [P, E1], I32), sb("ones1", [P, E1])
        given = sb("given", [P, E1])
        shift, shiftn, dshift = sb("shift", [P, E1]), sb("shiftn", [P, E1]), sb("dshift", [P, E1])
        limit, base, scr = sb("limit", [P, E1]), sb("base", [P, E1]), sb("scr", [P, E1])
        cj, ej, hj, parj = sb("cj", [P, JB]), sb("ej", [P, JB]), sb("hj", [P, JB]), sb("parj", [P, JB])
        hji, tabi = sb("hji", [P, JB], I32), sb("tabi", [P, 2, JB], I32)
        w2f = w2_0[:].rearrange("p u d -> p (u d)")
        half_of = qm[:].rearrange("p a b -> p (a b)")
        tabs = [w2f[0:1, 2048:2560].bitcast(I32), w3_0[0:1, 2048:2560].bitcast(I32)]
        xin, xgT, r1c = sb("xin", [P, L]), xn0, sb("r1c", [P, T])
        xgT = xn0[:].rearrange("p t d -> p (t d)")
        coef, lw = sb("coef", [P, HD]), sb("lw", [P, 4])
        mn1, mxq1, ex1, qk1, v1, qc1 = rA, rB, rr, qk, xs[:, 0, :], xs[:, 1, :]
        prodA = attf[:, 0:HD * D].rearrange("p (e d h) -> p e d h", e=HD, d=HD)
        prodB = attf[:, HD * D:2 * HD * D].rearrange("p (h d e) -> p h d e", h=H, d=HD)
        kv1, sq1, ss1, rd1 = state[:, 0:HD * HD].rearrange("p (e d) -> p e d", e=HD), stmp[:, 0:D].rearrange("p (h d) -> p h d", h=H), sb("ss1", [P, H]), sb("rd1", [P, 1])
        at1, a1 = (xs[:, i, :].rearrange("p (h d) -> p h d", h=H) for i in (2, 3))
        a1b, a1T, gl, s1b, sg, shb = xn1, oT, sT0, x1n, pT, xr
        idxc, w8c = sb("idxc", [P, 2, T * 8], U32), sb("w8c", [P, 2, T * 8])
        xg = w1_0[:, 0:2 * Q * D].rearrange("p (r q d) -> p r q d", r=2, q=Q)
        h1d = w1_0[:, 2 * Q * D:3 * Q * D].rearrange("p (q s i) -> p q s i", q=Q, s=2)
        xgTt, hT, ys = xn0T, xn0Tn, hs
        y8 = w2f[:, 0:2048].rearrange("p (r k d) -> p r k d", r=2, k=8)
        g1 = w1_0[:, 2048:2560]
        acc = w1_0[:, 1536:2048].rearrange("p (t d) -> p t d", t=T)
        x1f, s1f, shf, outs = (w3_0[:, i * T * D:(i + 1) * T * D].rearrange("p (t d) -> p t d", t=T) for i in range(4))

        rows = dram("rows", (NJ * P, D))
        y_d = dram("y_rows", (NG * Q * P, D))
        tab_d = dram("tile_table", (2, JB * P), I32)
        x1_d, s1_d, sh_d = dram("x1_d", (NB, P, T, D)), dram("s1_d", (NB, P, T, D)), dram("sh_d", (NB, P, T, D))
        xn1T_d = dram("xn1T_d", (NB, P, L))

        ps = {n: ctx.enter_context(nc.psum_tensor(n, [P, 512], F32)) for n in ("G0", "G1", "B", "V", "ACC", "U", "X0", "X1")}
        G, B, V = [ps["G0"], ps["G1"]], ps["B"], ps["V"]
        ACC, U, X0, X1 = ps["ACC"], ps["U"], ps["X0"], ps["X1"]

        sems = {n: (ctx.enter_context(nc.semaphore(n)), LINKS.get(n, per)) for n, per in PER_BATCH.items()}
        sem = {n: s for n, (s, _) in sems.items()}
        loaded = {n: ctx.enter_context(nc.semaphore(f"{n}_loaded")) for n in ("small", "f0", "w1", "zeros", "rest_zeros", "tab")}
        once = {n: ctx.enter_context(nc.semaphore(n)) for n in ("const_ready", "zero_ready", "coef_in", "coef_exp", "half_in", "half_ps",
                                                                "tab_ready", "tab_out", "half_ready", "phase2", "yst0", "yst1", "neg_ready")}

        small = [(wqkv0, "wqkv0"), (wr0, "wr0"), (ident, "ident"), (identb, "identb"), (cosr, "cosr"), (sinr, "sinr"),
                 (causal, "causal"), (headm, "headm"), (blockd, "blockd"), (wo0, "wo0"), (sel0, "sel0"),
                 (wqkv1, "wqkv1"), (wf1, "wf1"), (wf2, "wf2"), (wr1, "wr1"), (bias1, "bias1"), (g1c, "g1c"),
                 (g2r, "g2r"), (g3r, "g3r"), (lam, "lam"), (before, "before"), (onesb, "onesb"), (jcol, "jcol"), (hid, "hid")]
        x_v = a["x"].rearrange("(b t p) d -> b p t d", b=NB, p=P)
        out_v = out.rearrange("(b t p) d -> b p t d", b=NB, p=P)

        block = ctx.enter_context(nc.Block())

        def layer0(seen, fori, f0):
            f0(-1, False, {"pre"})
            f0(0, True, {"pre"})
            f0(1, True, {"res", "pre"})
            f0(2, True, {"res", "pre"})
            with fori(3, NB - 1) as g:
                seen.loop(g, 3)
                f0(g, True, {"res", "pre"})
                seen.loop_end(NB - 4)
            f0(NB - 1, True, {"res"})
            f0(NB, False, {"res"})

        def layer1_passes(seen, fori, f):
            f(0, {"pre"})
            with fori(1, FIRST_END) as b:
                seen.loop(b, 1)
                f(b, {"pre", "late"})
                seen.loop_end(FIRST_END - 1)
            f(FIRST_END, {"pre", "late", "end"})
            with fori(FIRST_END + 1, NB) as b:
                seen.loop(b, FIRST_END + 1)
                f(b, {"pre", "late", "end", "late_end"})
                seen.loop_end(NB - FIRST_END - 1)

        def ended(b, half):
            return (b - FIRST_END) * 2 + half

        def done(eng, name, n):
            if not (isinstance(n, int) and n < 0):
                eng.wait_ge(sem[name], n + 1)

        def settled(eng, seen, name, by=1):
            if seen.count[name]:
                eng.wait_ge(sem[name], seen.value(name, seen.count[name]))
            seen.next(name, by)

        @block.sync
        def _(sp):
            seen = Seen(sems)

            def load(dst, src, name):
                sp.dma_start(dst, src).then_inc(sem[name], 16)

            load(xs[:], x_v[0], "x_loaded")
            load(xr[:], x_v[0], "xr_loaded")
            for t, n in small:
                sp.dma_start(t[:], a[n]).then_inc(loaded["small"], 16)
            for t, n in ((w1_0, "w1_0"), (w3_0, "w3_0"), (w2_0, "w2_0")):
                sp.dma_start(t[:], a[n]).then_inc(loaded["f0"], 16)
            sp.wait_ge(once["zero_ready"], 1)
            def clear(pages_d, first, n, name):
                sp.dma_start(pages_d.rearrange("(j p) d -> p j d", p=P)[:, bass.ds(first, n), :], zero[:].unsqueeze(1).broadcast_to([P, n, D]))\
                    .then_inc(loaded[name], 16)

            clear(rows, 0, FIRST_PAGES, "zeros")
            used = FIRST_PAGES + (NB - 1) * MORE_PAGES
            clear(rows, used, NJ - used, "rest_zeros")
            for t, n in ((wg_1, "wg_1"), (wd_1, "wd_1"), (wgs, "wgs"), (wds, "wds")):
                sp.dma_start(t[:], a[n]).then_inc(loaded["w1"], 16)

            def f0(b, units, want, more_x=True):
                if "res" in want:
                    sp.wait_ge(*seen.next("x1_ready"))
                    load(x1_d[b - 1], x1n[:], "x1_stored")
                    if not (isinstance(b, int) and b >= NB):
                        load(xr[:], x_v[b], "xr_loaded")
                if "pre" in want:
                    sp.wait_ge(*seen.next("xn0_ready"))
                    if more_x:
                        load(xs[:], x_v[b + 2], "x_loaded")
                if "res" in want:
                    sp.wait_ge(*seen.next("xn1T_ready"))
                    load(xn1T_d[b - 1], xn1Tn[:], "xn1T_stored")
                if units and "res" in want:
                    clear(rows, (b - 1) * MORE_PAGES + FIRST_PAGES, MORE_PAGES, "zeros")
                    clear(y_d, (b - 1) * (NJ // (NB - 1)), NJ // (NB - 1), "rest_zeros")

            f0(-1, False, {"pre"})
            f0(0, True, {"pre"})
            f0(1, True, {"res", "pre"})
            f0(2, True, {"res", "pre"})
            with sp.Fori(3, NB - 2) as g:
                seen.loop(g, 3)
                f0(g, True, {"res", "pre"})
                seen.loop_end(NB - 5)
            f0(NB - 2, True, {"res", "pre"}, more_x=False)
            f0(NB - 1, True, {"res"})
            f0(NB, False, {"res"})

            sp.wait_ge(once["tab_ready"], 1)
            sp.dma_start(tab_d.rearrange("f (k p) -> p f k", p=P), tabi[:], allow_slow_non_contiguous=True).then_inc(once["tab_out"], 16)
            sp.wait_ge(once["tab_out"], 16)
            for f in range(2):
                sp.dma_start(tabs[f], tab_d[f:f + 1, :]).then_inc(loaded["tab"], 16)
            sp.wait_ge(loaded["tab"], 32)
            sp.wait_ge(sem["scattered"], 16 * T * TOPK1 * NB)
            sp.wait_ge(loaded["zeros"], 16 * NB)
            sp.wait_ge(loaded["rest_zeros"], 16 * NB)
            sp.wait_ge(sem["x1_stored"], 16 * NB)
            sp.wait_ge(sem["xn1T_stored"], 16 * NB)

            rows_v = rows.rearrange("(g q p) d -> g p q d", q=Q, p=P)

            def load_rows(n, par):
                done(sp, "xt_ps", n - 2)
                load(xg[:, par, :, :], rows_v[n], f"rows{par}_loaded")

            y_v = y_d.rearrange("(g q p) d -> g p q d", q=Q, p=P)

            def store_y(n, par):
                done(sp, "y_ready", n)
                sp.dma_start(y_v[n], ys[:, par, :].rearrange("p (q d) -> p q d", q=Q)).then_inc(once[f"yst{par}"], 16)

            LAGY = 5

            def s_load_rest(half, b):
                load(x1f, x1_d[ended(b, half)], "x1f_loaded")
                load(shf, sh_d[ended(b, half)], "shf_loaded")

            def s_load_s1(half, b):
                sp.wait_ge(sem["s1_stored"], (ended(b, half) + 1) * 16)
                load(s1f, s1_d[ended(b, half)], "s1f_loaded")

            def s_store_out(half, b):
                sp.wait_ge(*seen.next("out_ready"))
                load(out_v[ended(b, half)], outs, "out_stored")

            steps = {n[2:]: f for n, f in locals().items() if n.startswith("s_")}

            def ends(b, u, want):
                for name, i in beside(STEPS1, u, want):
                    if name in steps:
                        steps[name](i, b - 1 if (name, i) in LATE_END else b)

            def layer1(b, want):
                for u in range(GROUPS):
                    n = b * GROUPS + u
                    if u == 0:
                        settled(sp, seen, "xg_ready")
                        settled(sp, seen, "sg_ps")
                        load(xin[:], xn1T_d[b], "xin_loaded")
                    load_rows(n, u % 2)
                    if not (isinstance(b, int) and n < LAGY):
                        store_y(n - LAGY, (u - LAGY) % 2)
                    if u == 6:
                        sp.wait_ge(*seen.next("sh_ready"))
                        load(sh_d[b], shb[:], "sh_stored")
                    if u == 5 and "late" in want:
                        sp.wait_ge(*seen.next("s1_ready"))
                        load(s1_d[b - 1], s1b[:], "s1_stored")
                    ends(b, u, want)

            layer1_passes(seen, sp.Fori, layer1)
            for n in range(NG - LAGY, NG):
                store_y(n, n % 2)
            sp.wait_ge(*seen.next("s1_ready"))
            load(s1_d[NB - 1], s1b[:], "s1_stored")
            for u in range(GROUPS):
                ends(NB, u, {"late_end"})
            sp.wait_ge(sem["out_stored"], 16 * NB)
            sp.wait_ge(sem["sh_stored"], 16 * NB)
            for par in range(2):
                sp.wait_ge(once[f"yst{par}"], 16 * NG // 2)

        @block.tensor
        def _(pe):
            seen = Seen(sems)

            def reuse(bank):
                for s, v in seen.bank(bank):
                    pe.wait_ge(s, v)

            def transposes(bank, src, name):
                for t in range(T):
                    last = nc.tensor.transpose(ps[bank][:, t * P:(t + 1) * P], src(t), ident[:])
                last.then_inc(sem[name], 1)

            def s_xn0_T(t):
                pe.wait_ge(*seen.next("xn0_ready"))
                reuse("X0")
                transposes("X0", lambda t: xn0[:, t, :], "xn0T_ps")
                seen.readers["X0"] = ["xn0T_ready"]

            def s_router0(t):
                pe.wait_ge(*seen.next("xn0T_ready"))
                reuse("X1")
                for t in range(T):
                    last = nc.tensor.matmul(X1[:, t * E0:(t + 1) * E0], xn0Tn[:, t * P:(t + 1) * P], wr0[:], start=True, stop=True)
                last.then_inc(sem["lg0_ps"], 1)
                seen.readers["X1"] = ["e0_in"]

            def s_cw0_T(t):
                pe.wait_ge(*seen.next("cw0_ready"))
                reuse("V")
                xb = V[:, :].bitcast(BF16)
                for t in range(T):
                    last = nc.tensor.transpose(xb[0:3 * E0, t * P:(t + 1) * P],
                                               cwp0[:, t, :, :].rearrange("p a e -> p (a e)"), identb[:])
                last.then_inc(sem["cw0T_ps"], 1)
                seen.readers["V"] = ["cw0T_ready"]

            def s_qkv0(t):
                reuse("X0")
                nc.tensor.matmul(X0[:, 0:3 * D], xn0Tn[:, t * P:(t + 1) * P], wqkv0[:], start=True, stop=True)\
                    .then_inc(sem["qkv0_ps"], 1)
                seen.readers["X0"] = ["rope_ready", "v0_ready"]

            def s_qk_T(t):
                pe.wait_ge(*seen.next("qk0_ready"))
                reuse("X1")
                nc.tensor.transpose(X1[:, 0:P], qk[:, 0:D], ident[:])
                nc.tensor.transpose(X1[:, P:2 * P], qk[:, D:2 * D], ident[:]).then_inc(sem["qkT0_ps"], 1)
                seen.readers["X1"] = ["qkT0_ready", "qm_ready"]

            def score(g, bank):
                reuse(bank)
                nc.tensor.matmul(ps[bank][:, :], qkT[32 * g:32 * g + 32, P:2 * P], qm[32 * g:32 * g + 32, :, :],
                                 start=True, stop=True).then_inc(sem["sc_ps"], 1)
                seen.readers[bank] = ["at_ready"]

            def s_scores_a(t):
                pe.wait_ge(*seen.next("qkT0_ready"))
                pe.wait_ge(*seen.next("qm_ready"))
                if t:
                    pe.wait_ge(*seen.next("state_ready"))
                    reuse("V")
                    nc.tensor.matmul(V[:, 0:H * HA], qkT[:, 0:P], state[:], start=True, stop=False, skip_group_check=True)
                score(0, "X0")
                score(1, "X1")

            def s_scores_b(t):
                pe.wait_ge(*seen.next("at_ready"))
                score_now(2, "X0")
                pe.wait_ge(*seen.next("at_ready"))
                score_now(3, "X1")

            def score_now(g, bank):
                nc.tensor.matmul(ps[bank][:, :], qkT[32 * g:32 * g + 32, P:2 * P], qm[32 * g:32 * g + 32, :, :],
                                 start=True, stop=True).then_inc(sem["sc_ps"], 1)
                seen.readers[bank] = []

            def s_av(t):
                pe.wait_ge(*seen.next("at_ready", 2))
                reuse("V")
                if t < T - 1:
                    nc.tensor.matmul(X0[:, 0:H * HA], qk[:, D:2 * D], vaug[:].rearrange("p h m -> p (h m)"), start=True, stop=True)
                    seen.readers["X0"] = ["state_read"]
                for h in range(H):
                    last = nc.tensor.matmul(V[:, h * HA:(h + 1) * HA], att[:, h // 4, (h % 4) * P:(h % 4 + 1) * P], vaug[:, h, :],
                                            start=(t == 0 and h == 0), stop=(h == H - 1), skip_group_check=True)
                last.then_inc(sem["av_ps"], 1)
                seen.readers["V"] = ["o0_ready"]

            def s_o_T(t):
                pe.wait_ge(*seen.next("o0_ready"))
                reuse("X1")
                nc.tensor.transpose(X1[:, 0:P], o0[:].rearrange("p h m -> p (h m)"), ident[:]).then_inc(sem["oT_ps"], 1)
                seen.readers["X1"] = ["oT_ready"]

            def s_wo(t):
                pe.wait_ge(*seen.next("oT_ready"))
                reuse("X0")
                nc.tensor.matmul(X0[:, :], wo0[:], oT[:], start=True, stop=True).then_inc(sem["sT0_ps"], 1)
                seen.readers["X0"] = ["sT0_ready"]

            def s_res_T(t):
                pe.wait_ge(*seen.next("pT0_ready"))
                reuse("X0")
                transposes("X0", lambda t: pT[:, t * P:(t + 1) * P], "p0_ps")
                seen.readers["X0"] = ["x1_ready"]

            def s_xn1_T(t):
                pe.wait_ge(*seen.next("xn1_ready"))
                reuse("X1")
                transposes("X1", lambda t: xn1[:, t, :], "xn1T_ps")
                seen.readers["X1"] = ["xn1T_ready"]

            def s_router1(t):
                pe.wait_ge(*seen.next("xn1T_ready"))
                reuse("X0")
                reuse("V")
                for t in range(T):
                    bank = (X0, V)[t // 2]
                    last = nc.tensor.matmul(bank[:, (t % 2) * E1:(t % 2 + 1) * E1], xn1Tn[:, t * P:(t + 1) * P], wr1[:],
                                            start=True, stop=True)
                last.then_inc(sem["lg1_ps"], 1)
                seen.readers["X0"], seen.readers["V"] = ["lg1a_ready"], ["lg1b_ready"]

            def s_rank(t):
                pe.wait_ge(*seen.next("chosen_ready"))
                for bank in ("X0", "X1", "V"):
                    reuse(bank)
                for t in range(T):
                    o = (X0, X1)[t // 2][:, (t % 2) * E1:(t % 2 + 1) * E1]
                    nc.tensor.matmul(o, before[:], chosen[:, t, :], start=True, stop=(t == 0))
                    for s in range(t):
                        nc.tensor.matmul(o, onesb[:], chosen[:, s, :], start=False, stop=(s == t - 1))
                for t in range(T):
                    last = nc.tensor.matmul(V[:, 0:E1], onesb[:], chosen[:, t, :], start=(t == 0), stop=(t == T - 1))
                last.then_inc(sem["rank_ps"], 1)
                seen.readers["X0"], seen.readers["X1"], seen.readers["V"] = ["ranka_read"], ["rankb_read"], ["run_ready"]

            def s_qkv1(t):
                reuse("X0")
                nc.tensor.matmul(X0[:, 0:3 * D], xgT[:, t * P:(t + 1) * P], wqkv1[:], start=True, stop=True)\
                    .then_inc(sem["qkv1_ps"], 1)
                seen.readers["X0"] = ["mn1_ready", "mx1_ready", "v1_ready"]

            def s_a1_T(t):
                pe.wait_ge(*seen.next("a1_ready"))
                if t == 0:
                    reuse("X1")
                nc.tensor.transpose(X1[:, t * P:(t + 1) * P], a1b[:, t, :], ident[:]).then_inc(sem["a1T_ps"], 1)
                seen.readers["X1"] = ["a1T_ready"] if t == T - 1 else []

            def s_xg(t):
                pe.wait_ge(*seen.next("xg_ready"))

            def s_shared_up(t):
                reuse("U")
                nc.tensor.matmul(U[0:INTER, :], wgs[:], xin[:], start=True, stop=True).then_inc(sem["sg_ps"], 1)
                seen.readers["U"] = ["sg_ready"]

            def s_shared_down(t):
                pe.wait_ge(*seen.next("sg_ready"))
                reuse("X1")
                for t in range(T):
                    last = nc.tensor.matmul(X1[:, t * P:(t + 1) * P], sg[0:INTER, t * P:(t + 1) * P], wds[:], start=True, stop=True)
                last.then_inc(sem["sh_ps"], 1)
                seen.readers["X1"] = ["sh_ready"]

            def s_ffh1(t):
                pe.wait_ge(*seen.next("a1T_ready"))
                reuse("U")
                nc.tensor.matmul(U[:, :], wf1[:], a1T[:], start=True, stop=True).then_inc(sem["h1_ps"], 1)
                seen.readers["U"] = ["gl_ready"]

            def s_ffo1(t):
                pe.wait_ge(*seen.next("gl_ready"))
                reuse("X0")
                for t in range(T):
                    last = nc.tensor.matmul(X0[:, t * P:(t + 1) * P], gl[:, t * P:(t + 1) * P], wf2[:], start=True, stop=True)
                last.then_inc(sem["o1_ps"], 1)
                seen.readers["X0"] = ["s1_ready"]

            steps = {n[2:]: f for n, f in locals().items() if n.startswith("s_")}

            def others(table, u, want):
                for name, t in beside(table, u, want):
                    if name in steps:
                        steps[name](t)

            def f0(b, units, want):
                if isinstance(b, int) and b == 0:
                    pe.wait_ge(loaded["f0"], 48)
                if units:
                    pe.wait_ge(*seen.next("rot_ready"))
                for s in range(4 * (U0 + LAG)):
                    u, part = divmod(s, 4)
                    if units and u < U0 and part == 0:
                        free = seen.lag("g_ps", 2)
                        if free:
                            pe.wait_ge(sem["silu_ready"], free[1])
                        nc.tensor.matmul(G[u % 2][:, :], w1_0[:, u * P:(u + 1) * P], xn0T[:], start=True, stop=True).then_inc(sem["g_ps"], 1)
                        seen.next("g_ps")
                    if units and u < U0 and part == 1:
                        free = seen.lag("up_ps", 1)
                        if free:
                            pe.wait_ge(sem["hu_ready"], free[1])
                        nc.tensor.matmul(U[:, :], w3_0[:, u * P:(u + 1) * P], xn0T[:], start=True, stop=True).then_inc(sem["up_ps"], 1)
                        seen.next("up_ps")
                    if units and u < U0 and part == 2:
                        free = seen.lag("b_ps", 1)
                        if free:
                            pe.wait_ge(sem["hw_ready"], free[1])
                        nc.tensor.matmul(B[:, :], sel0[:, u * P:(u + 1) * P], cw0T[:], start=True, stop=True).then_inc(sem["b_ps"], 1)
                        seen.next("b_ps")
                    if units and u >= LAG and part == 3:
                        v = u - LAG
                        if v == 0:
                            reuse("ACC")
                        pe.wait_ge(*seen.next("hw_ready"))
                        nc.tensor.matmul(ACC[:, :], w2_0[:, v, :], hw[:, v % RH, :], start=(v == 0), stop=(v == U0 - 1))\
                            .then_inc(sem["acc_done" if v == U0 - 1 else "down_done"], 1)
                    others(STEPS, s, want)
                if units:
                    seen.readers["ACC"] = ["gT0_ready"]

            pe.wait_ge(loaded["small"], 16 * len(small))
            pe.wait_ge(once["const_ready"], 1)
            layer0(seen, pe.Fori, f0)

            pe.wait_ge(once["half_in"], 1)
            for bank in ("X0", "X1", "V"):
                reuse(bank)
            for k in range(JB):
                last = nc.tensor.matmul(X0[:, k * P:(k + 1) * P], parj[:, k:k + 1].broadcast_to([P, P]), ident[:], start=True, stop=True)
            last.then_inc(once["half_ps"], 1)
            pe.wait_ge(once["half_ready"], 1)
            pe.wait_ge(loaded["w1"], 64)
            pe.wait_ge(loaded["tab"], 32)
            pe.wait_ge(once["phase2"], 1)

            def columns(field, n, high):
                _, at = nc.values_load_multi_w_load_instructions(
                    tabs[field][:, bass.ds(n * Q, Q)], engines=[mybir.EngineType.PE], min_val=0, max_val=high,
                    skip_runtime_bounds_check_because="the table's experts are held below E1")
                return at

            def group(n, b, u, stages):
                def has(k):
                    return k in stages and not (isinstance(b, int) and b == 0 and u < k)
                if has(0):
                    pe.wait_ge(sem[f"rows{u % 2}_loaded"], (b * (GROUPS // 2) + u // 2 + 1) * 16)
                    done(pe, "xt_ready", n - 1)
                    for q in range(Q):
                        last = nc.tensor.transpose(G[0][:, q * P:(q + 1) * P], xg[:, u % 2, q, :], ident[:])
                    last.then_inc(sem["xt_ps"], 1)
                if has(1):
                    done(pe, "xt_ready", n - 1)
                    done(pe, "gt_ready", n - 2)
                    at = columns(0, n - 1, (E1 - 1) * INTER)
                    for q in range(Q):
                        last = nc.tensor.matmul(B[:, q * INTER:(q + 1) * INTER], xgTt[:, q * P:(q + 1) * P],
                                                wg_1[:, bass.ds(at[q], INTER)], start=True, stop=True)
                    last.then_inc(sem["gt_ps"], 1)
                if has(2):
                    done(pe, "gt_ready", n - 2)
                    done(pe, "ht_ready", n - 3)
                    for q in range(Q):
                        last = nc.tensor.transpose(V[:, q * P:(q + 1) * P], h1d[:, q, :, :].rearrange("p a i -> p (a i)"), ident[:])
                    last.then_inc(sem["ht_ps"], 1)
                if has(3):
                    done(pe, "ht_ready", n - 3)
                    done(pe, "y_ready", n - 4)
                    at = columns(1, n - 3, (E1 // 2 - 1) * D)
                    for q in range(Q):
                        last = nc.tensor.matmul(ACC[:, q * P:(q + 1) * P], hT[:, q * P:(q + 1) * P],
                                                wd_1[:, bass.ds(at[q], D)], start=True, stop=True)
                    last.then_inc(sem["y_ps"], 1)

            def layer1(b, want):
                for u in range(GROUPS):
                    group(b * GROUPS + u, b, u, {0, 1, 2, 3})
                    others(STEPS1, u, want)

            layer1_passes(seen, pe.Fori, layer1)
            for k in range(1, 4):
                group(NG - 1 + k, NB, 10 ** 6, set(range(k, 4)))
            for last in ({"late"}, {"late_end"}):
                for u in range(GROUPS):
                    others(STEPS1, u, last)

        @block.scalar
        def _(act):
            seen = Seen(sems)

            def copy(dst, src, after, name):
                if after:
                    act.wait_ge(*seen.next(after))
                nc.scalar.activation(dst, src, ACT.Copy).then_inc(sem[name], 1)

            def s_xn0T_copy(t):
                settled(act, seen, "rot_ready")
                copy(xn0Tn[:], X0[:, :], "xn0T_ps", "xn0T_ready")

            def s_exp0(t):
                act.wait_ge(*seen.next("e0_in"))
                nc.scalar.activation(e0[:], l0[:], ACT.Exp).then_inc(sem["e0_ready"], 1)

            def s_cw0T_copy(t):
                copy(cw0Tn[:], V[:, :].bitcast(BF16)[0:3 * E0, 0:L], "cw0T_ps", "cw0T_ready")

            def s_rope(t):
                act.wait_ge(*seen.next("rope_ready"))
                nc.scalar.activation(qk[:], rr[:], ACT.Relu).then_inc(sem["qk0_ready"], 1)
                copy(vaug[:, :, 0:HD], X0[:, 2 * D:3 * D].rearrange("p (h m) -> p h m", h=H), None, "v0_ready")

            def s_qkT_copy(t):
                copy(qkT[:], X1[:, 0:2 * P], "qkT0_ps", "qkT0_ready")

            def s_oT_copy(t):
                copy(oT[:, t * P:(t + 1) * P], X1[:, 0:P], "oT_ps", "oT_ready")

            def s_s0(t):
                settled(act, seen, "s_rot_ready")
                copy(sT0n[:], X0[:, :], "sT0_ps", "sT0_ready")

            def s_res_silu(t):
                act.wait_ge(*seen.next("acc_done"))
                nc.scalar.activation(gT[:], ACC[:, :], ACT.Silu).then_inc(sem["gT0_ready"], 1)

            def s_xn1T_copy(t):
                settled(act, seen, "xn1T_stored", 16)
                copy(xn1Tn[:], X1[:, :], "xn1T_ps", "xn1T_ready")

            def s_probs1(t):
                act.wait_ge(*seen.next("lg1a_ready"))
                act.wait_ge(*seen.next("lg1b_ready"))
                nc.scalar.activation(pr, place, ACT.Sigmoid).then_inc(sem["probs_ready"], 1)

            def s_exp1(t):
                act.wait_ge(*seen.next("mx1_ready"))
                nc.scalar.activation(v1, X0[:, 2 * D:3 * D], ACT.Copy, scale=r1c[:, t:t + 1]).then_inc(sem["v1_ready"], 1)
                act.wait_ge(*seen.next("mn1_ready"))
                nc.scalar.activation(ex1[:], mn1[:], ACT.Exp).then_inc(sem["ex1_ready"], 1)

            def s_shared_up(t):
                act.wait_ge(*seen.next("sg_ps"))
                nc.scalar.activation(sg[0:INTER, :], U[0:INTER, :], ACT.Silu).then_inc(sem["sg_ready"], 1)

            def s_shared_down(t):
                act.wait_ge(*seen.next("sh_ps"))
                settled(act, seen, "sh_stored", 16)
                nc.scalar.activation(shb[:], X1[:, :].rearrange("p (t d) -> p t d", t=T), ACT.Copy).then_inc(sem["sh_ready"], 1)

            def s_a1T_copy(t):
                act.wait_ge(*seen.next("a1T_ps", T))
                nc.scalar.activation(a1T[:], X1[:, :], ACT.Copy).then_inc(sem["a1T_ready"], 1)

            def s_end_silu(half):
                act.wait_ge(*seen.next("sum_ready"))
                nc.scalar.activation(g1, acc.rearrange("p t d -> p (t d)"), ACT.Silu).then_inc(sem["g1_ready"], 1)

            def s_gelu1(t):
                act.wait_ge(*seen.next("h1_ps"))
                nc.scalar.activation(gl[:], U[:, :], ACT.Gelu).then_inc(sem["gl_ready"], 1)

            steps = {n[2:]: f for n, f in locals().items() if n.startswith("s_")}

            def others(table, u, want):
                for name, t in beside(table, u, want):
                    if name in steps:
                        steps[name](t)

            def f0(b, units, want):
                for s in range(4 * U0):
                    u, part = divmod(s, 4)
                    if units and part == 1:
                        act.wait_ge(*seen.next("g_ps"))
                        if u >= 2:
                            act.wait_ge(*seen.next("hw_ready"))
                        nc.scalar.activation(hs[:, u % 2, :], G[u % 2][:, :], ACT.Silu).then_inc(sem["silu_ready"], 1)
                    others(STEPS, s, want)
                if units:
                    seen.next("hw_ready", 2)

            act.wait_ge(once["coef_in"], 2)
            nc.scalar.activation(lw[:, 2:4], lw[:, 0:2], ACT.Exp).then_inc(once["coef_exp"], 1)
            layer0(seen, act.Fori, f0)

            def group(n, b, u, stages):
                def has(k):
                    return k in stages and not (isinstance(b, int) and b == 0 and u < k)
                if has(0):
                    done(act, "xt_ps", n)
                    done(act, "gt_ps", n - 1)
                    nc.scalar.activation(xgTt[:], G[0][:, :], ACT.Copy).then_inc(sem["xt_ready"], 1)
                if has(1):
                    done(act, "gt_ps", n - 1)
                    done(act, "ht_ps", n - 2)
                    nc.scalar.activation(h1d[:], B[:, 0:Q * INTER].rearrange("p (q i) -> p q i", q=Q).unsqueeze(2)
                                         .broadcast_to([P, Q, 2, INTER]), ACT.Silu).then_inc(sem["gt_ready"], 1)
                if has(3):
                    done(act, "y_ps", n - 3)
                    par = (u - 3) % 2 if u < 10 ** 6 else (n - 3) % 2
                    if not (isinstance(b, int) and b == 0 and u < 5):
                        k = (b * (GROUPS // 2) + (u - 3) // 2) if u < 10 ** 6 else (n - 3) // 2
                        act.wait_ge(once[f"yst{par}"], k * 16)
                    nc.scalar.activation(ys[:, par, :], ACC[:, :], ACT.Copy).then_inc(sem["y_ready"], 1)

            def layer1(b, want):
                for u in range(GROUPS):
                    group(b * GROUPS + u, b, u, {0, 1, 3})
                    others(STEPS1, u, want)

            act.wait_ge(once["phase2"], 1)
            layer1_passes(seen, act.Fori, layer1)
            for k in range(1, 4):
                group(NG - 1 + k, NB, 10 ** 6, {1, 3} if k == 1 else {3})
            for last in ({"late"}, {"late_end"}):
                for u in range(GROUPS):
                    others(STEPS1, u, last)

        @block.gpsimd
        def _(pool):
            seen = Seen(sems)

            def rsqrt(v, name="rsq"):
                pool.wait_ge(*seen.next(name + "_in"))
                nc.gpsimd.tensor_tensor(v, v, neg_half[:, 0:v.shape[1]], ALU.pow).then_inc(sem[name + "_ready"], 1)

            def waited(name):
                if seen.count[name]:
                    pool.wait_ge(sem[name], seen.value(name, seen.count[name]))
                seen.next(name)
                nc.gpsimd.tensor_tensor(ppause[:], neg_half[:, 0:1], neg_half[:, 0:1], ALU.mult).then_inc(sem[name], 1)

            def s_norm0a(t):
                rsqrt(rs[:])

            def s_res_add(t):
                rsqrt(rs[:])

            def s_res_norm(t):
                rsqrt(r1[:])

            def s_scatter(t):
                pool.wait_ge(*seen.next("idx_ready"))
                waited("pool_link")
                for t in range(T):
                    for k in range(TOPK1):
                        pool.indirect_dma_start(rows, bass.IndirectOffsetOnAxis(ap=idx[:, t * 8 + k:t * 8 + k + 1], axis=0), xn1[:, t, :], None)\
                            .then_inc(sem["scattered"], 16)

            step_of = [0]

            def s_gather(i):
                if i == 0:
                    pool.wait_ge(*seen.next("idxc_ready"))
                if i % T == 0:
                    groups = FIRST_PAGES // Q + ended(step_of[0], i // T) * (MORE_PAGES // Q)
                    for par in range(2):
                        pool.wait_ge(once[f"yst{par}"], groups * 8)
                c = seen.count["gathered_used"] - 1
                if c > 0 or seen.reg is not None:
                    pool.wait_ge(sem["gathered_used"], seen.value("gathered_used", c))
                seen.next("gathered_used")
                waited("pool_link3")
                t = i % T
                for k in range(TOPK1):
                    pool.indirect_dma_start(y8[:, i % 2, k, :], None, y_d, bass.IndirectOffsetOnAxis(
                        ap=idxc[:, i // T, t * 8 + k:t * 8 + k + 1], axis=0)).then_inc(sem[f"gath{i % 2}"], 16)

            def s_mix1a(t):
                rsqrt(ss1[:], "rsq1")

            def s_mix1b(t):
                rsqrt(rd1[:], "rsq1")

            steps = {n[2:]: f for n, f in locals().items() if n.startswith("s_")}

            def others(n, table, want, b=0):
                step_of[0] = b
                for u in range(n):
                    for name, t in beside(table, u, want):
                        if name in steps:
                            steps[name](t)

            nc.gpsimd.memset(zero[:], 0.0).then_inc(once["zero_ready"], 1)
            nc.gpsimd.memset(neg_half[:], -0.5).then_inc(once["neg_ready"], 1)
            pool.wait_ge(once["neg_ready"], 1)

            def f0(b, units, want):
                if "res" in want:
                    pool.wait_ge(loaded["zeros"], b * 16)
                others(4 * U0, STEPS, want)

            layer0(seen, pool.Fori, f0)
            pool.wait_ge(once["phase2"], 1)
            layer1_passes(seen, pool.Fori, lambda b, want: others(GROUPS, STEPS1, want, b))

        @block.vector
        def _(dve):
            seen = Seen(sems)
            LK = ["dve_link"]

            def link(ins):
                seen.next(LK[0])
                ins.then_inc(sem[LK[0]], 1)
                return ins

            def join():
                if seen.count[LK[0]]:
                    dve.wait_ge(sem[LK[0]], seen.value(LK[0], seen.count[LK[0]]))

            def join_alone():
                join()
                nc.vector.memset(pause[:], 0.0)

            def ask(ins, name="rsq"):
                ins.then_inc(sem[name + "_in"], 1)
                seen.next(name + "_in")

            def take(name="rsq"):
                dve.wait_ge(*seen.next(name + "_ready"))

            def norm_ask(src):
                for t in range(T):
                    link(nc.vector.bn_stats(st[:, t, :], src[:, t, :]))
                join_alone()
                for t in range(T):
                    link(nc.vector.bn_aggr(mv[:, t, :], st[:, t, :]))
                join()
                ask(nc.vector.tensor_scalar(rs[:], mv[:, :, 1], LN_EPS, None, ALU.add))

            def norm_take(src, dst, name):
                take()
                for t in range(T):
                    last = nc.vector.tensor_scalar(dst[:, t, :], src[:, t, :], mv[:, t, 0:1], rs[:, t:t + 1], ALU.subtract, ALU.mult)
                last.then_inc(sem[name], 1)

            def parts(cw, rest, out_p, name):
                link(nc.vector.tensor_copy(out_p(0), cw))
                join()
                link(nc.vector.tensor_tensor(rest, cw, out_p(0), ALU.subtract))
                join()
                link(nc.vector.tensor_copy(out_p(1), rest))
                join()
                nc.vector.tensor_tensor(out_p(2), rest, out_p(1), ALU.subtract).then_inc(sem[name], 1)

            def s_norm0a(t):
                dve.wait_ge(*seen.next("x_loaded", 16))
                norm_ask(xs)

            def s_norm0b(t):
                norm_take(xs, xn0, "xn0_ready")

            def s_exp0(t):
                dve.wait_ge(*seen.next("lg0_ps"))
                lgt = X1[:, 0:T * E0].rearrange("p (t e) -> p t e", t=T)
                link(nc.vector.tensor_reduce(mx0[:], lgt, AX.X, ALU.max))
                join()
                nc.vector.tensor_tensor(l0[:], lgt, mx0[:].unsqueeze(2).broadcast_to([P, T, E0]), ALU.subtract).then_inc(sem["e0_in"], 1)

            def s_topk0a(t):
                dve.wait_ge(*seen.next("e0_ready"))
                link(nc.vector.tensor_reduce(sm0[:], e0[:], AX.X, ALU.add))
                join()
                link(nc.vector.reciprocal(sm0[:], sm0[:]))
                join()
                link(nc.vector.tensor_tensor(sc0[:, :, 0:E0], e0[:], sm0[:].unsqueeze(2).broadcast_to([P, T, E0]), ALU.mult))
                join_alone()
                for t in range(T):
                    link(nc.vector.max(m80[:, t, :], sc0[:, t, 0:E0]))

            def s_topk0b(t):
                join()
                link(nc.vector.memset(m80[:, :, 2:8], -1.0))
                link(nc.vector.tensor_tensor(sm0[:], m80[:, :, 0], m80[:, :, 1], ALU.add))
                join_alone()
                for t in range(T):
                    link(nc.vector.match_replace(sr0[:, t, :], m80[:, t, :], sc0[:, t, :], 0.0))
                link(nc.vector.tensor_scalar(sm0[:], sm0[:], 1e-20, None, ALU.add))
                join()
                link(nc.vector.reciprocal(sm0[:], sm0[:]))
                link(nc.vector.tensor_tensor(cwf0[:], sc0[:, :, 0:E0], sr0[:, :, 0:E0], ALU.subtract))
                join()
                link(nc.vector.tensor_tensor(cwf0[:], cwf0[:], sm0[:].unsqueeze(2).broadcast_to([P, T, E0]), ALU.mult))
                join()
                parts(cwf0[:], cwr0[:], lambda i: cwp0[:, :, i, :], "cw0_ready")

            def s_rope(t):
                dve.wait_ge(*seen.next("qkv0_ps"))
                x = X0[:, 0:2 * D].rearrange("p (h m) -> p h m", m=HD)
                c = cosr[:, t, :].unsqueeze(1).broadcast_to([P, 2 * H, HD])
                link(nc.vector.tensor_tensor(rA[:].rearrange("p (h m) -> p h m", m=HD), x, c, ALU.mult))
                xp = X0[:, 0:2 * D].rearrange("p (h i two) -> p h i two", i=HD // 2, two=2)
                op = rB[:].rearrange("p (h i two) -> p h i two", i=HD // 2, two=2)
                s = sinr[:, t, :].rearrange("p (i two) -> p i two", two=2)
                for j in range(2):
                    link(nc.vector.tensor_tensor(op[:, :, :, j], xp[:, :, :, 1 - j],
                                                 s[:, :, j].unsqueeze(1).broadcast_to([P, 2 * H, HD // 2]), ALU.mult))
                join()
                nc.vector.tensor_tensor(rr[:], rA[:], rB[:], ALU.add).then_inc(sem["rope_ready"], 1)

            def s_qkT_copy(t):
                dve.wait_ge(*seen.next("qkT0_ready"))
                nc.vector.tensor_tensor(qm[:], qkT[:, 0:P].unsqueeze(1).broadcast_to([P, 4, P]),
                                        headm[:].unsqueeze(2).broadcast_to([P, 4, P]), ALU.mult).then_inc(sem["qm_ready"], 1)

            def mask(g):
                dve.wait_ge(*seen.next("sc_ps"))
                nc.vector.tensor_tensor(att[:, g, :].rearrange("p (r i) -> p r i", r=4),
                                        (X0, X1)[g % 2][:, :].rearrange("p (r i) -> p r i", r=4),
                                        causal[:].unsqueeze(1).broadcast_to([P, 4, P]), ALU.mult).then_inc(sem["at_ready"], 1)

            def s_mask_a(t):
                mask(0)
                mask(1)

            def s_mask_b(t):
                mask(2)
                mask(3)

            def s_o_norm(t):
                dve.wait_ge(*seen.next("av_ps"))
                u = V[:, 0:H * HA].rearrange("p (h m) -> p h m", m=HA)
                link(nc.vector.tensor_scalar(dn[:], u[:, :, HD], ATT_EPS, None, ALU.add))
                if t == 0:
                    link(nc.vector.memset(state[:], 0.0))
                if t < T - 1:
                    nc.vector.tensor_tensor(stmp[:], X0[:, 0:H * HA], blockd[:], ALU.mult).then_inc(sem["state_read"], 1)
                join()
                link(nc.vector.reciprocal(rc[:], dn[:]))
                if t < T - 1:
                    dve.wait_ge(*seen.next("state_read"))
                    nc.vector.tensor_tensor(state[:], state[:], stmp[:], ALU.add).then_inc(sem["state_ready"], 1)
                join()
                nc.vector.tensor_tensor(o0[:], u[:, :, 0:HD], rc[:].unsqueeze(2).broadcast_to([P, H, HD]), ALU.mult)\
                    .then_inc(sem["o0_ready"], 1)

            batch = [0]

            def s_res_gate(t):
                dve.wait_ge(*seen.next("gT0_ready"))
                dve.wait_ge(*seen.next("s_rot_ready"))
                nc.vector.tensor_tensor(pT[:], sT0[:], gT[:], ALU.mult).then_inc(sem["pT0_ready"], 1)

            def s_res_add(t):
                dve.wait_ge(*seen.next("p0_ps"))
                dve.wait_ge(*seen.next("xr_loaded", 16))
                settled(dve, seen, "x1_stored", 16)
                nc.vector.tensor_tensor(x1n[:], xr[:], X0[:, :].rearrange("p (t d) -> p t d", t=T), ALU.add).then_inc(sem["x1_ready"], 1)
                dve.wait_ge(*seen.next("x1_ready"))
                norm_ask(x1n)

            def s_res_norm(t):
                settled(dve, seen, "scattered", 16 * T * TOPK1)
                norm_take(x1n, xn1, "xn1_ready")
                link(nc.vector.tensor_tensor(ms1[:], rs[:], rs[:], ALU.mult))
                join()
                link(nc.vector.tensor_tensor(ms1[:], ms1[:], mv[:, :, 1], ALU.mult))
                join()
                ask(nc.vector.tensor_scalar(r1[:], ms1[:], RMS_EPS, None, ALU.add))

            def s_res_r1(t):
                take()
                link(nc.vector.tensor_copy(r1all[:, batch[0], :], r1[:]))

            def s_probs1(t):
                dve.wait_ge(*seen.next("lg1_ps"))
                for i, (bank, done_) in enumerate(((X0, "lg1a_ready"), (V, "lg1b_ready"))):
                    nc.vector.tensor_tensor(place[:, 2 * i:2 * i + 2, :], bank[:, 0:2 * E1].rearrange("p (t e) -> p t e", t=2),
                                            bias1[:].unsqueeze(1).broadcast_to([P, 2, E1]), ALU.add).then_inc(sem[done_], 1)

            def s_topk1a(t):
                dve.wait_ge(*seen.next("probs_ready"))
                nc.vector.memset(pause[:], 0.0)
                for t in range(T):
                    link(nc.vector.max(m8[:, t, :], pr[:, t, :]))

            def s_topk1b(t):
                join_alone()
                for t in range(T):
                    link(nc.vector.match_replace(pr2[:, t, :], m8[:, t, :], pr[:, t, :], -1.0))
                link(nc.vector.tensor_reduce(s8[:], m8[:], AX.X, ALU.add))
                join()
                nc.vector.tensor_tensor(chosen, pr2, pr, ALU.not_equal).then_inc(sem["chosen_ready"], 1)
                link(nc.vector.tensor_scalar(s8[:], s8[:], 1e-9, None, ALU.add))
                join()
                link(nc.vector.reciprocal(s8[:], s8[:]))
                join()
                link(nc.vector.tensor_scalar(s8[:], s8[:], 2.5, None, ALU.mult))

            def s_place_a(t):
                dve.wait_ge(*seen.next("rank_ps"))
                nc.vector.tensor_tensor(runn[:], run[:], V[:, 0:E1], ALU.add).then_inc(sem["run_ready"], 1)
                dve.wait_ge(*seen.next("run_ready"))
                link(nc.vector.tensor_scalar(pagesi[:], runn[:], float(P - 2), None, ALU.add))
                link(nc.vector.scalar_tensor_tensor(limit[:], pages[:], float(P), run[:], ALU.mult, ALU.subtract))
                join()
                link(nc.vector.tensor_scalar(pagesi[:], pagesi[:], 7, None, ALU.arith_shift_right))
                join()
                link(nc.vector.tensor_copy(pagesn[:], pagesi[:]))
                join()
                link(nc.vector.tensor_tensor(new[:], pagesn[:], pages[:], ALU.subtract))
                link(nc.vector.tensor_copy(hj[:, 0:1], given[:, E1 - 1:E1]))
                join()
                link(nc.vector.tensor_tensor_scan(given[:], ones1[:], new[:], 0.0, ALU.mult, ALU.add))
                join()
                link(nc.vector.tensor_scalar(given[:], given[:], hj[:, 0:1], None, ALU.add))
                join()
                link(nc.vector.tensor_tensor(shiftn[:], given[:], pagesn[:], ALU.subtract))
                join()
                link(nc.vector.tensor_tensor(dshift[:], shift[:], shiftn[:], ALU.subtract))
                link(nc.vector.scalar_tensor_tensor(base[:], shiftn[:], float(P), run[:], ALU.mult, ALU.add))
                join()

            def s_place_b(t):
                link(nc.vector.scalar_tensor_tensor(shift[:], new[:], 0.0, dshift[:], ALU.is_equal, ALU.mult))
                link(nc.vector.tensor_scalar(scr[:], dshift[:], float(P), None, ALU.mult))
                for i, bank in enumerate((X0, X1)):
                    link(nc.vector.tensor_tensor(pr2[:, 2 * i:2 * i + 2, :], bank[:, 0:2 * E1].rearrange("p (t e) -> p t e", t=2),
                                                 limit[:].unsqueeze(1).broadcast_to([P, 2, E1]), ALU.is_le))
                join()
                link(nc.vector.tensor_tensor(shift[:], shift[:], shiftn[:], ALU.add))
                link(nc.vector.tensor_tensor(pr2, pr2, scr[:].unsqueeze(1).broadcast_to([P, T, E1]), ALU.mult))
                for i, (bank, done_) in enumerate(((X0, "ranka_read"), (X1, "rankb_read"))):
                    nc.vector.tensor_tensor(place[:, 2 * i:2 * i + 2, :], bank[:, 0:2 * E1].rearrange("p (t e) -> p t e", t=2),
                                            base[:].unsqueeze(1).broadcast_to([P, 2, E1]), ALU.add).then_inc(sem[done_], 1)
                dve.wait_ge(*seen.next("ranka_read"))
                dve.wait_ge(*seen.next("rankb_read"))
                join()
                link(nc.vector.tensor_copy(run[:], runn[:]))
                link(nc.vector.tensor_copy(pages[:], pagesn[:]))
                link(nc.vector.tensor_tensor(place, place, pr2, ALU.add))
                join()
                dve.wait_ge(*seen.next("chosen_ready"))
                nc.vector.tensor_tensor(place, place, chosen, ALU.mult).then_inc(sem["places_ready"], 1)

            def s_place_c(t):
                dve.wait_ge(*seen.next("places_ready"))
                nc.vector.memset(pause[:], 0.0)
                for t in range(T):
                    link(nc.vector.max(p8[:, t, :], place[:, t, :]))
                join()
                p8f = p8[:].rearrange("p t k -> p (t k)")
                link(nc.vector.tensor_scalar(idxy[:, batch[0], :], p8f, -1.0, None, ALU.add))
                nc.vector.tensor_scalar(idx[:], p8f, -1.0, None, ALU.add).then_inc(sem["idx_ready"], 1)
                for k in range(JB):
                    link(nc.vector.tensor_scalar(scr[:], given[:], jcol[:, k:k + 1], 0.0, ALU.is_le, ALU.add, accum_out=cj[:, k:k + 1]))
                    join()
                link(nc.vector.scalar_tensor_tensor(cj[:], cj[:], E1 - 0.5, cj[:], ALU.is_lt, ALU.mult))
                join()
                link(nc.vector.tensor_tensor(ej[:], ej[:], cj[:], ALU.add))

            def s_weights(t):
                join()
                for k in range(TOPK1):
                    if k and k % TERMS == 0:
                        join()
                    link(nc.vector.scalar_tensor_tensor(terms[:, k % TERMS, :], place[:, t, :], p8[:, t, k:k + 1], pr[:, t, :],
                                                        ALU.is_equal, ALU.mult, accum_out=w8[:, t, k:k + 1]))
                if t == T - 1:
                    join()
                    link(nc.vector.tensor_tensor(w8all[:, batch[0], :].rearrange("p (t k) -> p t k", t=T), w8[:],
                                                 s8[:].unsqueeze(2).broadcast_to([P, T, TOPK1]), ALU.mult))

            def s_xg(t):
                dve.wait_ge(*seen.next("xin_loaded", 16))
                link(nc.vector.tensor_copy(r1c[:], r1all[:, batch[0], :]))
                nc.vector.tensor_scalar(xgT, xin[:], g1c[:, 0:1], None, ALU.mult).then_inc(sem["xg_ready"], 1)
                join()

            def s_elu1(t):
                dve.wait_ge(*seen.next("qkv1_ps"))
                nc.vector.tensor_scalar(mn1[:], X0[:, 0:2 * D], r1c[:, t:t + 1], 0.0, ALU.mult, ALU.min).then_inc(sem["mn1_ready"], 1)
                nc.vector.tensor_scalar(mxq1[:], X0[:, 0:2 * D], r1c[:, t:t + 1], 0.0, ALU.mult, ALU.max).then_inc(sem["mx1_ready"], 1)

            def s_mix1a(t):
                dve.wait_ge(*seen.next("mx1_ready"))
                dve.wait_ge(*seen.next("ex1_ready"))
                nc.vector.scalar_tensor_tensor(qk1[:], ex1[:], -1.0, mxq1[:], ALU.add, ALU.add).then_inc(sem["k1_ready"], 1)
                dve.wait_ge(*seen.next("k1_ready"))
                link(nc.vector.tensor_tensor(qc1.rearrange("p (h e) -> p h e", h=H), qk1[:, 0:D].rearrange("p (h e) -> p h e", h=H),
                                             coef[:].unsqueeze(1).broadcast_to([P, H, HD]), ALU.mult))
                dve.wait_ge(*seen.next("v1_ready"))
                k = qk1[:, D:2 * D].rearrange("p (h e) -> p e h", h=H).unsqueeze(2).broadcast_to([P, HD, HD, H])
                v = v1.rearrange("p (h d) -> p d h", h=H).unsqueeze(1).broadcast_to([P, HD, HD, H])
                nc.vector.tensor_tensor(prodA, k, v, ALU.mult).then_inc(sem["prod1_ready"], 1)
                dve.wait_ge(*seen.next("prod1_ready"))
                link(nc.vector.tensor_reduce(kv1, prodA, AX.X, ALU.add))
                join()
                q = qc1.rearrange("p (h e) -> p h e", h=H).unsqueeze(2).broadcast_to([P, H, HD, HD])
                kv = kv1.rearrange("p e d -> p d e").unsqueeze(1).broadcast_to([P, H, HD, HD])
                link(nc.vector.tensor_tensor(prodB, q, kv, ALU.mult))
                join()
                link(nc.vector.tensor_reduce(at1, prodB, AX.X, ALU.add))
                join()
                link(nc.vector.tensor_tensor(sq1, at1, at1, ALU.mult))
                join()
                link(nc.vector.tensor_reduce(ss1[:], sq1, AX.X, ALU.add))
                join()
                ask(nc.vector.tensor_scalar(ss1[:], ss1[:], 1.0 / HD, RMS_EPS, ALU.mult, ALU.add), "rsq1")

            def s_mix1b(t):
                take("rsq1")
                link(nc.vector.tensor_tensor(sq1, at1, ss1[:].unsqueeze(2).broadcast_to([P, H, HD]), ALU.mult))
                join()
                link(nc.vector.tensor_tensor(a1, sq1, g2r[:].unsqueeze(1).broadcast_to([P, H, HD]), ALU.mult))
                join()
                link(nc.vector.scalar_tensor_tensor(sq1, a1, 1.0, a1, ALU.mult, ALU.mult, accum_out=rd1[:]))
                join()
                ask(nc.vector.tensor_scalar(rd1[:], rd1[:], 1.0 / D, RMS_EPS, ALU.mult, ALU.add), "rsq1")

            def s_mix1c(t):
                take("rsq1")
                sqf = sq1.rearrange("p h d -> p (h d)")
                link(nc.vector.tensor_scalar(sqf, g3r[:], rd1[:, 0:1], 1.0, ALU.mult, ALU.add))
                join()
                nc.vector.tensor_tensor(a1b[:, t, :], a1.rearrange("p h d -> p (h d)"), sqf, ALU.mult).then_inc(sem["a1_ready"], 1)

            def s_idxc(t):
                link(nc.vector.tensor_copy(w8c[:], w8all[:, bass.ds(ended(batch[0], 0), 2), :]))
                nc.vector.tensor_copy(idxc[:], idxy[:, bass.ds(ended(batch[0], 0), 2), :]).then_inc(sem["idxc_ready"], 1)

            def s_weigh(i):
                t = i % T
                dve.wait_ge(*seen.next(f"gath{i % 2}", 16 * TOPK1))
                y = y8[:, i % 2, :, :]
                link(nc.vector.tensor_tensor(y, y, w8c[:, i // T, t * 8:(t + 1) * 8].unsqueeze(2).broadcast_to([P, 8, D]), ALU.mult))
                join()
                nc.vector.tensor_reduce(acc[:, t, :], y.rearrange("p k d -> p d k"), AX.X, ALU.add).then_inc(sem["gathered_used"], 1)

            def s_end_sum(half):
                settled_all("gathered_used")
                dve.wait_ge(*seen.next("shf_loaded", 16))
                nc.vector.tensor_tensor(acc, acc, shf, ALU.add).then_inc(sem["sum_ready"], 1)

            def s_end_out(half):
                dve.wait_ge(*seen.next("g1_ready"))
                dve.wait_ge(*seen.next("s1f_loaded", 16))
                link(nc.vector.tensor_tensor(s1f, s1f, g1.rearrange("p (t d) -> p t d", t=T), ALU.mult))
                join()
                dve.wait_ge(*seen.next("x1f_loaded", 16))
                settled(dve, seen, "out_stored", 16)
                nc.vector.tensor_tensor(outs, x1f, s1f, ALU.add).then_inc(sem["out_ready"], 1)

            def settled_all(name):
                dve.wait_ge(*seen.next(name, T))

            def s_s1(t):
                dve.wait_ge(*seen.next("o1_ps"))
                settled(dve, seen, "s1_stored", 16)
                nc.vector.tensor_tensor(s1b[:], a1b[:], X0[:, :].rearrange("p (t d) -> p t d", t=T), ALU.add).then_inc(sem["s1_ready"], 1)

            steps = {n[2:]: f for n, f in locals().items() if n.startswith("s_")}

            def others(table, u, want):
                for name, t in beside(table, u, want):
                    if name in steps:
                        steps[name](t)

            def f0(b, units, want):
                batch[0] = b - 1
                if units:
                    dve.wait_ge(*seen.next("xn0T_ready"))
                    dve.wait_ge(*seen.next("cw0T_ready"))
                    settled(dve, seen, "acc_done")
                    link(nc.vector.tensor_copy(cw0T[:], cw0Tn[:]))
                    nc.vector.tensor_copy(xn0T[:], xn0Tn[:]).then_inc(sem["rot_ready"], 1)
                for s in range(4 * U0):
                    u, part = divmod(s, 4)
                    if units and part == 2:
                        dve.wait_ge(*seen.next("silu_ready"))
                        dve.wait_ge(*seen.next("up_ps"))
                        nc.vector.tensor_tensor(hs[:, u % 2, :], hs[:, u % 2, :], U[:, :], ALU.mult).then_inc(sem["hu_ready"], 1)
                        dve.wait_ge(*seen.next("hu_ready"))
                        dve.wait_ge(*seen.next("b_ps"))
                        if u >= RH:
                            dve.wait_ge(*seen.next("down_done"))
                        nc.vector.tensor_tensor(hw[:, u % RH, :], hs[:, u % 2, :], B[:, :], ALU.mult).then_inc(sem["hw_ready"], 1)
                    if units and s == 4:
                        dve.wait_ge(*seen.next("sT0_ready"))
                        if "res" in want:
                            dve.wait_ge(sem["pT0_ready"], seen.value("pT0_ready", seen.count["pT0_ready"] + 1))
                        nc.vector.tensor_copy(sT0[:], sT0n[:]).then_inc(sem["s_rot_ready"], 1)
                    others(STEPS, s, want)
                if "res" in want:
                    seen.next("pT0_ready")
                if units:
                    seen.next("down_done", RH - 1)

            dve.wait_ge(loaded["small"], 16 * len(small))
            nc.vector.memset(sc0[:], -1.0)
            nc.vector.memset(idxy[:], 0)
            for v, x in ((run, 1.0), (ones1, 1.0), (pages, 0.0), (given, 0.0), (shift, 0.0), (ej, 0.0)):
                link(nc.vector.memset(v[:], x))
            nc.vector.memset(vaug[:], 1.0).then_inc(once["const_ready"], 1)
            lm = lam[:].rearrange("p (a b) -> p a b", b=2)
            nc.vector.tensor_tensor(lw[:, 0:2], lm[:, :, 0], lm[:, :, 1], ALU.mult).then_inc(once["coef_in"], 1)
            link(nc.vector.memset(coef[:], SCALE1))
            nc.vector.tensor_scalar(g2r[:], g2r[:], 1.0 - LAMBDA_INIT, None, ALU.mult).then_inc(once["coef_in"], 1)
            dve.wait_ge(once["coef_exp"], 1)
            link(nc.vector.tensor_tensor(lw[:, 0:1], lw[:, 2:3], lw[:, 3:4], ALU.subtract))
            join()
            link(nc.vector.tensor_scalar(lw[:, 1:2], lw[:, 0:1], LAMBDA_INIT, -1.0, ALU.add, ALU.mult))
            join()
            link(nc.vector.tensor_scalar(coef[:, HD // 2:HD], coef[:, HD // 2:HD], lw[:, 1:2], None, ALU.mult))
            join()
            layer0(seen, dve.Fori, f0)

            join()
            link(nc.vector.tensor_copy(hji[:], ej[:]))
            link(nc.vector.tensor_scalar(tabi[:, 0, :], ej[:], float(INTER), None, ALU.mult))
            join()
            link(nc.vector.tensor_scalar(hji[:], hji[:], 1, None, ALU.arith_shift_right))
            join()
            link(nc.vector.tensor_copy(hj[:], hji[:]))
            join()
            nc.vector.tensor_scalar(tabi[:, 1, :], hj[:], float(D), None, ALU.mult).then_inc(once["tab_ready"], 1)
            nc.vector.scalar_tensor_tensor(parj[:], hj[:], -2.0, ej[:], ALU.mult, ALU.add).then_inc(once["half_in"], 1)
            dve.wait_ge(once["half_ps"], 1)
            nc.vector.tensor_scalar(half_of, X0[:, :], hid[:, 0:1], None, ALU.is_equal).then_inc(once["half_ready"], 1)
            dve.wait_ge(once["half_ready"], 1)
            dve.wait_ge(sem["scattered"], 16 * T * TOPK1 * NB)
            dve.wait_ge(sem["x1_stored"], 16 * NB)
            dve.wait_ge(sem["xn1T_stored"], 16 * NB)
            nc.vector.memset(pause[:], 0.0).then_inc(once["phase2"], 1)
            LK[0] = "dve_link2"

            def group(n, b, u):
                if isinstance(b, int) and b == 0 and u < 2:
                    return
                done(dve, "ht_ps", n - 2)
                done(dve, "y_ps", n - 3)
                nc.vector.tensor_tensor(hT[:].rearrange("p (q r) -> p q r", q=Q), V[:, :].rearrange("p (q r) -> p q r", q=Q),
                                        half_of[:, bass.ds((n - 2) * Q, Q)].unsqueeze(2).broadcast_to([P, Q, P]), ALU.mult)\
                    .then_inc(sem["ht_ready"], 1)

            def layer1(b, want):
                if isinstance(b, int) and b == FIRST_END:
                    join()
                    LK[0] = "dve_link3"
                batch[0] = b
                for u in range(GROUPS):
                    group(b * GROUPS + u, b, u)
                    others(STEPS1, u, want)

            layer1_passes(seen, dve.Fori, layer1)
            for k in range(1, 3):
                group(NG - 1 + k, NB, 10 ** 6)
            for last in ({"late"}, {"late_end"}):
                for u in range(GROUPS):
                    others(STEPS1, u, last)


def kernel(**inputs):
    import numpy as _np
    import concourse.bacc as _bacc
    from concourse import mybir as _mybir
    from concourse.bass_utils import run_bass_kernel_spmd as _run

    i = {k: _np.asarray(v) for k, v in inputs.items()}
    f4 = _np.float32
    import ml_dtypes
    bf = ml_dtypes.bfloat16

    def tiles(w, n):
        return w.reshape(n, P, D).transpose(1, 0, 2)

    def rows(v):
        return _np.broadcast_to(v.reshape(1, -1), (P, v.size))

    inv_freq = (f4(1.0) / _np.power(f4(10000.0), _np.arange(0, HD, 2, dtype=f4) / f4(HD), dtype=f4)).astype(f4)
    freqs = (_np.arange(L, dtype=f4)[:, None] * inv_freq[None, :]).astype(f4)
    cos, sin = _np.cos(freqs.astype(_np.float64)), _np.sin(freqs.astype(_np.float64))
    cosr = _np.repeat(cos, 2, axis=1)
    sinr = _np.stack([-sin, sin], axis=-1).reshape(L, HD)
    pos = _np.arange(P)
    sel0 = _np.tile((_np.arange(U0 * P)[None, :] // HID0 == _np.arange(E0)[:, None]), (3, 1))
    given = {
        "x": i["L0_attn_x"].reshape(NB * L, D),
        "wqkv0": _np.concatenate([i["L0_attn_wq"], i["L0_attn_wk"], i["L0_attn_wv"]], axis=1),
        "wo0": i["L0_attn_wo"],
        "wr0": i["L0_ffn_Wg"].T,
        "w1_0": i["L0_ffn_W1"].reshape(-1, D).T,
        "w3_0": i["L0_ffn_W3"].reshape(-1, D).T,
        "w2_0": tiles(i["L0_ffn_W2"].transpose(0, 2, 1).reshape(-1, D), U0),
        "wqkv1": _np.concatenate([i["L1_attn_Wq"], i["L1_attn_Wk"], i["L1_attn_Wv"]], axis=0).T,
        "wf1": i["L1_attn_W1"].T,
        "wf2": i["L1_attn_W2"].T,
        "wr1": i["L1_ffn_router_w"].T,
        "bias1": rows(i["L1_ffn_expert_bias"]),
        "g1c": i["L1_attn_g1"].reshape(P, 1),
        "g2r": rows(i["L1_attn_g2"]),
        "g3r": rows(i["L1_attn_g3"]),
        "lam": rows(i["L1_attn_lambda_params"]),
        "wg_1": i["L1_ffn_w_gate"].reshape(-1, D).T,
        "wd_1": tiles(i["L1_ffn_w_down"].transpose(0, 2, 1).reshape(-1, D), E1 // 2).reshape(P, -1),
        "wgs": i["L1_ffn_w_gate_shared"].T,
        "wds": i["L1_ffn_w_down_shared"].T,
        "ident": _np.eye(P, dtype=f4),
        "identb": _np.eye(P, dtype=bf),
        "cosr": cosr.astype(f4).reshape(T, P, HD).transpose(1, 0, 2),
        "sinr": sinr.astype(f4).reshape(T, P, HD).transpose(1, 0, 2),
        "causal": (pos[:, None] <= pos[None, :]).astype(f4),
        "headm": ((pos[:, None] // HD) % 4 == _np.arange(4)[None, :]).astype(f4),
        "blockd": (pos[:, None] // HD == _np.arange(H * HA)[None, :] // HA).astype(f4),
        "sel0": sel0.astype(bf),
        "before": (pos[:, None] < pos[None, :]).astype(bf),
        "onesb": _np.ones((P, P), dtype=bf),
        "jcol": (_np.arange(JB)[None, :] * P + pos[:, None]).astype(f4),
        "hid": (pos[:, None] // INTER).astype(f4),
    }
    nc = _bacc.Bacc("TRN2", target_bir_lowering=False, num_devices=1)
    arrays, aps = {}, {}
    for name, v in given.items():
        v = _np.ascontiguousarray(v)
        arrays[f"in_{name}"] = v
        aps[name] = nc.dram_tensor(f"in_{name}", v.shape, _mybir.dt.from_np(v.dtype), kind="ExternalInput").ap()
    out = nc.dram_tensor("out_dram", (NB * L, D), F32, kind="ExternalOutput").ap()
    build(nc, aps, out)
    r = _run(nc, [arrays], core_ids=[0])
    return r.results[0]["out_dram"].reshape(NB, L, D)
```
